# Optimizing a Trainium2 kernel written in Bass

```python
import numpy as np
import jax
import jax.numpy as jnp

def _softmax(x, axis=-1):
    return jax.nn.softmax(x, axis=axis)

def _gelu(x):
    return jax.nn.gelu(x, approximate=True)

def _silu(x):
    return jax.nn.silu(x)

def _sigmoid(x):
    return jax.nn.sigmoid(x)

def _layernorm(x, axis=-1, eps=1e-05):
    m = jnp.mean(x, axis=axis, keepdims=True)
    v = jnp.var(x, axis=axis, keepdims=True)
    return (x - m) / jnp.sqrt(v + eps)

def _scatter_add(tgt, idx, src, axis=0):
    return tgt.at[idx].add(src)

def _segment_sum(src, seg, n):
    return jax.ops.segment_sum(src, seg, n)
kernel_name = 'mk_adj_preln_d4_adj_r2_ec197b'

def setup_inputs(seed: int=0):
    np.random.seed(seed)
    _w = jnp.asarray

    def _rec_inputs():
        import jax
        import jax.numpy as jnp
        _gk = jax.random.key(seed)
        x = -0.0002928 + 1 * jax.random.normal(jax.random.fold_in(_gk, 1), (16, 512, 128), jnp.float32)
        _w = (1.0 + jnp.arange(512, dtype=jnp.float32)) ** (-0.5)
        _w = _w / _w.mean()
        _pij = jnp.clip(0.0078125 * _w[:, None] * _w[None, :], 0.0, 1.0)
        _a = jax.random.uniform(jax.random.fold_in(_gk, 2), (16, 512, 512)) < _pij
        _a = jnp.logical_or(_a, jnp.swapaxes(_a, -1, -2))
        _a = jnp.logical_or(_a, jnp.eye(512, dtype=bool))
        _af = _a.astype(jnp.float32)
        _af = _af * jax.random.uniform(jax.random.fold_in(_gk, 3), (16, 512, 512), jnp.float32, 0.05, 0.999994)
        adj = _af
        _nm = jnp.ones((16, 512), dtype=bool)
        nodemask = jnp.where(_nm, 1.0, 0.0).astype(jnp.float32)
        return (x, adj, nodemask)
    x, adj, nodemask = _rec_inputs()

    def _L0_gnn_setup():
        import jax, jax.numpy as jnp
        import numpy as np
        EPS = 1e-08
        key = jax.random.key(seed)
        kH, kA, kW = jax.random.split(key, 3)
        B, N, IN, OUT = (32, 256, 128, 128)
        H = jax.random.normal(kH, (B, N, IN), dtype=jnp.float32)
        A = jax.random.uniform(kA, (B, N, N), dtype=jnp.float32)
        mask = jnp.ones((B, N), dtype=jnp.float32)
        W = jax.random.normal(kW, (OUT, IN), dtype=jnp.float32) * (1.0 / np.sqrt(IN))
        b = jnp.zeros((OUT,), dtype=jnp.float32)
        return {'H': H, 'A': A, 'mask': mask, 'W': W, 'b': b}
    _L0_gnn_all = _L0_gnn_setup()
    _L0_gnn_in = {k: v for k, v in _L0_gnn_all.items() if k in ('W', 'b')}
    del _L0_gnn_all

    def _L1_gnn_setup():
        import jax, jax.numpy as jnp
        import numpy as np
        MIN_VALUE = 1e-10
        key = jax.random.key(seed)
        k1, k2, k3, k4, k5 = jax.random.split(key, 5)
        B, N, F, P = (32, 512, 128, 128)
        x = jax.random.normal(k1, (B, N, F), dtype=jnp.float32)
        adjacency_matrix = jax.random.uniform(k2, (B, N, N), dtype=jnp.float32)
        bound = 1.0 / np.sqrt(F)
        W = jax.random.uniform(k3, (P, F), minval=-bound, maxval=bound, dtype=jnp.float32)
        b = jax.random.uniform(k4, (P,), minval=-bound, maxval=bound, dtype=jnp.float32)
        alpha = jax.random.uniform(k5, (1,), dtype=jnp.float32)
        return {'x': x, 'adjacency_matrix': adjacency_matrix, 'W': W, 'b': b, 'alpha': alpha}
    _L1_gnn_all = _L1_gnn_setup()
    _L1_gnn_in = {k: v for k, v in _L1_gnn_all.items() if k in ('W', 'b', 'alpha')}
    del _L1_gnn_all

    def _L2_gnn_setup():
        import jax, jax.numpy as jnp
        import numpy as np
        from jax import lax
        DIM = 128
        EPS = 1e-05

        def _bn(h, g, b, m, v):
            scale = g / jnp.sqrt(v + EPS)
            return h * scale[None, :, None] + (b - m * scale)[None, :, None]

        def _conv1d(h, w, pad):
            return lax.conv_general_dilated(h, w, window_strides=(1,), padding=[(pad, pad)], dimension_numbers=('NCH', 'OIH', 'NCH'))
        key = jax.random.key(seed)
        ks = jax.random.split(key, 16)
        bs, n, d = (16, 1024, DIM)
        s = 0.05
        return {'x': jax.random.normal(ks[0], (bs, n, d), jnp.float32), 'mask': jnp.ones((bs, n, n), jnp.float32), 'w_se': jax.random.normal(ks[1], (3, d), jnp.float32) * s, 'b_se': jnp.zeros((3,), jnp.float32), 'conv1_w': jax.random.normal(ks[2], (d, d, 1), jnp.float32) * s, 'bn1_g': jnp.ones((d,), jnp.float32), 'bn1_b': jnp.zeros((d,), jnp.float32), 'bn1_m': jnp.zeros((d,), jnp.float32), 'bn1_v': jnp.ones((d,), jnp.float32), 'conv2_w': jax.random.normal(ks[3], (d, d, 17), jnp.float32) * s, 'bn2_g': jnp.ones((d,), jnp.float32), 'bn2_b': jnp.zeros((d,), jnp.float32), 'bn2_m': jnp.zeros((d,), jnp.float32), 'bn2_v': jnp.ones((d,), jnp.float32), 'w_msg': jax.random.normal(ks[4], (d, d), jnp.float32) * s, 'b_msg': jnp.zeros((d,), jnp.float32), 'w_ih': jax.random.normal(ks[5], (3 * d, 2 * d), jnp.float32) * s, 'b_ih': jnp.zeros((3 * d,), jnp.float32), 'w_hh': jax.random.normal(ks[6], (3 * d, d), jnp.float32) * s, 'b_hh': jnp.zeros((3 * d,), jnp.float32)}
    _L2_gnn_all = _L2_gnn_setup()
    _L2_gnn_in = {k: v for k, v in _L2_gnn_all.items() if k in ('w_se', 'b_se', 'conv1_w', 'bn1_g', 'bn1_b', 'bn1_m', 'bn1_v', 'conv2_w', 'bn2_g', 'bn2_b', 'bn2_m', 'bn2_v', 'w_msg', 'b_msg', 'w_ih', 'b_ih', 'w_hh', 'b_hh')}
    del _L2_gnn_all

    def _L3_gnn_setup():
        import jax, jax.numpy as jnp
        import numpy as np
        B, N, IN_DIM, OUT_DIM, H = (8, 512, 128, 128, 4)
        D = OUT_DIM // H
        NEG_INF = -9000000000000000.0
        LRELU_SLOPE = 0.2
        key = jax.random.key(seed)
        k1, k2, k3, k4 = jax.random.split(key, 4)
        x = jax.random.normal(k1, (B, N, IN_DIM), dtype=jnp.float32)
        adj = jax.random.randint(k2, (B, N, N), 0, 2).astype(jnp.float32)
        W = jax.random.normal(k3, (IN_DIM, H * D), dtype=jnp.float32) * jnp.sqrt(2.0 / (IN_DIM + H * D))
        a = jax.random.normal(k4, (H, 2 * D), dtype=jnp.float32) * jnp.sqrt(2.0 / (H + 2 * D))
        return {'x': x, 'adj': adj, 'W': W, 'a': a}
    _L3_gnn_all = _L3_gnn_setup()
    _L3_gnn_in = {k: v for k, v in _L3_gnn_all.items() if k in ('W', 'a')}
    del _L3_gnn_all
    return {'x': x, 'adj': adj, 'nodemask': nodemask, 'L0_gnn_W': _L0_gnn_in['W'], 'L0_gnn_b': _L0_gnn_in['b'], 'L1_gnn_W': _L1_gnn_in['W'], 'L1_gnn_b': _L1_gnn_in['b'], 'L1_gnn_alpha': _L1_gnn_in['alpha'], 'L2_gnn_w_se': _L2_gnn_in['w_se'], 'L2_gnn_b_se': _L2_gnn_in['b_se'], 'L2_gnn_conv1_w': _L2_gnn_in['conv1_w'], 'L2_gnn_bn1_g': _L2_gnn_in['bn1_g'], 'L2_gnn_bn1_b': _L2_gnn_in['bn1_b'], 'L2_gnn_bn1_m': _L2_gnn_in['bn1_m'], 'L2_gnn_bn1_v': _L2_gnn_in['bn1_v'], 'L2_gnn_conv2_w': _L2_gnn_in['conv2_w'], 'L2_gnn_bn2_g': _L2_gnn_in['bn2_g'], 'L2_gnn_bn2_b': _L2_gnn_in['bn2_b'], 'L2_gnn_bn2_m': _L2_gnn_in['bn2_m'], 'L2_gnn_bn2_v': _L2_gnn_in['bn2_v'], 'L2_gnn_w_msg': _L2_gnn_in['w_msg'], 'L2_gnn_b_msg': _L2_gnn_in['b_msg'], 'L2_gnn_w_ih': _L2_gnn_in['w_ih'], 'L2_gnn_b_ih': _L2_gnn_in['b_ih'], 'L2_gnn_w_hh': _L2_gnn_in['w_hh'], 'L2_gnn_b_hh': _L2_gnn_in['b_hh'], 'L3_gnn_W': _L3_gnn_in['W'], 'L3_gnn_a': _L3_gnn_in['a']}

def reference(x, adj, nodemask, L0_gnn_W, L0_gnn_b, L1_gnn_W, L1_gnn_b, L1_gnn_alpha, L2_gnn_w_se, L2_gnn_b_se, L2_gnn_conv1_w, L2_gnn_bn1_g, L2_gnn_bn1_b, L2_gnn_bn1_m, L2_gnn_bn1_v, L2_gnn_conv2_w, L2_gnn_bn2_g, L2_gnn_bn2_b, L2_gnn_bn2_m, L2_gnn_bn2_v, L2_gnn_w_msg, L2_gnn_b_msg, L2_gnn_w_ih, L2_gnn_b_ih, L2_gnn_w_hh, L2_gnn_b_hh, L3_gnn_W, L3_gnn_a):
    import jax
    import jax.numpy as jnp

    def _L0_gnn_ref(H, A, mask, W, b):
        import jax, jax.numpy as jnp
        import numpy as np
        EPS = 1e-08
        N = A.shape[-1]
        A_hat = A + jnp.eye(N, dtype=A.dtype)
        deg = A_hat.sum(axis=-1)
        dis = (deg + EPS) ** (-0.5)
        A_norm = dis[:, :, None] * A_hat * dis[:, None, :]
        H_lin = jnp.einsum('bni,oi->bno', H, W) + b
        out = jnp.einsum('bnm,bmo->bno', A_norm, H_lin)
        out = out * mask[:, :, None]
        return jax.nn.relu(out)

    def _L1_gnn_ref(x, adjacency_matrix, W, b, alpha):
        import jax, jax.numpy as jnp
        import numpy as np
        MIN_VALUE = 1e-10
        deg = adjacency_matrix.sum(axis=-1)
        deg = jnp.where(deg != 0, deg, 1.0)
        d_inv_sqrt = deg ** (-0.5)
        norm_adj = d_inv_sqrt[:, :, None] * adjacency_matrix * d_inv_sqrt[:, None, :]
        alpha_eff = jnp.maximum(alpha[0], MIN_VALUE)
        N = adjacency_matrix.shape[1]
        a_plus = norm_adj + alpha_eff * jnp.eye(N, dtype=adjacency_matrix.dtype)
        h = jnp.einsum('bnm,bmf->bnf', a_plus, x)
        return jnp.einsum('bnf,pf->bnp', h, W) + b

    def _L2_gnn_ref(x, mask, w_se, b_se, conv1_w, bn1_g, bn1_b, bn1_m, bn1_v, conv2_w, bn2_g, bn2_b, bn2_m, bn2_v, w_msg, b_msg, w_ih, b_ih, w_hh, b_hh):
        import jax, jax.numpy as jnp
        import numpy as np
        from jax import lax
        DIM = 128
        EPS = 1e-05

        def _bn(h, g, b, m, v):
            scale = g / jnp.sqrt(v + EPS)
            return h * scale[None, :, None] + (b - m * scale)[None, :, None]

        def _conv1d(h, w, pad):
            return lax.conv_general_dilated(h, w, window_strides=(1,), padding=[(pad, pad)], dimension_numbers=('NCH', 'OIH', 'NCH'))
        d = x.shape[-1]
        xc = jnp.transpose(x, (0, 2, 1))
        h = _bn(_conv1d(xc, conv1_w, 0), bn1_g, bn1_b, bn1_m, bn1_v)
        h = jax.nn.relu(h)
        h = _bn(_conv1d(h, conv2_w, 8), bn2_g, bn2_b, bn2_m, bn2_v)
        x_conv = jnp.transpose(jax.nn.relu(h + xc), (0, 2, 1))
        s = x @ w_se.T + b_se
        sq = jnp.sum(s * s, axis=-1)
        dist = sq[:, :, None] + sq[:, None, :] - 2.0 * jnp.einsum('bnd,bmd->bnm', s, s)
        A = jnp.exp(-dist) * mask
        msg = jax.nn.relu(x @ w_msg.T + b_msg)
        x_nmp = jnp.einsum('bnm,bmd->bnd', A, msg)
        x_in = jnp.concatenate([x_conv, x_nmp], axis=-1)
        gi = x_in @ w_ih.T + b_ih
        gh = x @ w_hh.T + b_hh
        gi_r, gi_z, gi_n = (gi[..., :d], gi[..., d:2 * d], gi[..., 2 * d:])
        gh_r, gh_z, gh_n = (gh[..., :d], gh[..., d:2 * d], gh[..., 2 * d:])
        r = jax.nn.sigmoid(gi_r + gh_r)
        z = jax.nn.sigmoid(gi_z + gh_z)
        nn_ = jnp.tanh(gi_n + r * gh_n)
        return (1.0 - z) * nn_ + z * x

    def _L3_gnn_ref(x, adj, W, a):
        import jax, jax.numpy as jnp
        import numpy as np
        B, N, IN_DIM, OUT_DIM, H = (8, 512, 128, 128, 4)
        D = OUT_DIM // H
        NEG_INF = -9000000000000000.0
        LRELU_SLOPE = 0.2
        h = jnp.einsum('bni,io->bno', x, W).reshape(x.shape[0], x.shape[1], H, D)
        h = h.transpose(0, 2, 1, 3)
        a1, a2 = (a[:, :D], a[:, D:])
        e_i = jnp.einsum('bhnd,hd->bhn', h, a1)
        e_j = jnp.einsum('bhmd,hd->bhm', h, a2)
        e = e_i[:, :, :, None] + e_j[:, :, None, :]
        e = jnp.where(e > 0, e, LRELU_SLOPE * e)
        e = jnp.where(adj[:, None, :, :] > 0, e, NEG_INF)
        attn = jax.nn.softmax(e, axis=-1)
        out = jnp.einsum('bhnm,bhmd->bhnd', attn, h)
        out = out.transpose(0, 2, 1, 3).reshape(x.shape[0], x.shape[1], H * D)
        return out
    h = jnp.maximum(_layernorm(x, axis=-1), 0.0)
    x = x + _L0_gnn_ref(h, adj, nodemask, L0_gnn_W, L0_gnn_b)
    h = jnp.maximum(_layernorm(x, axis=-1), 0.0)
    x = x + _L1_gnn_ref(h, adj, L1_gnn_W, L1_gnn_b, L1_gnn_alpha)
    h = jnp.maximum(_layernorm(x, axis=-1), 0.0)
    x = x + _L2_gnn_ref(h, adj, L2_gnn_w_se, L2_gnn_b_se, L2_gnn_conv1_w, L2_gnn_bn1_g, L2_gnn_bn1_b, L2_gnn_bn1_m, L2_gnn_bn1_v, L2_gnn_conv2_w, L2_gnn_bn2_g, L2_gnn_bn2_b, L2_gnn_bn2_m, L2_gnn_bn2_v, L2_gnn_w_msg, L2_gnn_b_msg, L2_gnn_w_ih, L2_gnn_b_ih, L2_gnn_w_hh, L2_gnn_b_hh)
    h = jnp.maximum(_layernorm(x, axis=-1), 0.0)
    x = x + _L3_gnn_ref(h, adj, L3_gnn_W, L3_gnn_a)
    return x

_drawn_inputs = setup_inputs


def setup_inputs(seed=0):
    import zlib

    import numpy as np

    out = dict(_drawn_inputs(seed))
    spreads = {'L0_gnn_b': (0.0, 0.1),
     'L2_gnn_b_se': (0.0, 2.0),
     'L2_gnn_bn1_g': (1.0, 0.6),
     'L2_gnn_bn1_b': (0.0, 0.391),
     'L2_gnn_bn1_m': (0.0, 0.343),
     'L2_gnn_bn1_v': (1.0, 0.6),
     'L2_gnn_bn2_g': (1.0, 0.6),
     'L2_gnn_bn2_b': (0.0, 0.656),
     'L2_gnn_bn2_m': (0.0, 0.616),
     'L2_gnn_bn2_v': (1.0, 0.6),
     'L2_gnn_b_msg': (0.0, 0.68),
     'L2_gnn_b_ih': (0.0, 0.1),
     'L2_gnn_b_hh': (0.0, 0.448)}
    factors = {'L2_gnn_w_se': 8.516}
    for name, (base, spread) in spreads.items():
        noise = np.random.default_rng([zlib.crc32(name.encode()), seed]).standard_normal(out[name].shape)
        drawn = base * np.exp(spread * noise) if base else spread * noise
        out[name] = jnp.asarray(drawn.astype(out[name].dtype))
    for name, factor in factors.items():
        out[name] = (out[name] * factor).astype(out[name].dtype)
    return out
```

```python
from contextlib import ExitStack

import concourse.bass as bass
from concourse import mybir

P = 128
F32 = mybir.dt.float32
F32R = mybir.dt.float32r
BF16 = mybir.dt.bfloat16
ALU = mybir.AluOpType
ACT = mybir.ActivationFunctionType
AX = mybir.AxisListType
RMAX = bass.bass_isa.ReduceOp.max


def build_gnn(nc: bass.Bass, x, adj, nodemask, w0, b0, w1, b1, alpha, w_se, b_se, conv1_w, bn1_g, bn1_b,
              bn1_m, bn1_v, conv2_w, bn2_g, bn2_b, bn2_m, bn2_v, w_msg, b_msg, w_ih, b_ih, w_hh, b_hh,
              w3, a3, out):
    GRAPHS, N, D = x.shape
    T = N // P
    TAPS = conv2_w.shape[2]
    PAD = TAPS // 2
    HEADS = a3.shape[0]
    HD = D // HEADS
    SE = w_se.shape[0]
    C = HD + 1
    assert D == P and N == 4 * P and GRAPHS % 2 == 0 and SE == 3
    LN_EPS = 1e-5
    BN_EPS = 1e-5

    ctx = ExitStack()
    with ctx:
        def sb(name, shape, dt=F32):
            return ctx.enter_context(nc.sbuf_tensor(name, shape, dt))

        def sem(name):
            return ctx.enter_context(nc.semaphore(name))

        psum = ctx.enter_context(nc.psum_tensor("psum", [P, 8, N], F32))
        LIGHT, HEAVY, LAST = 0, 2, 5

        def bank(i):
            return psum[:, i, :]

        def tiles(ap, c=P):
            return ap.rearrange("p (t c) -> p t c", c=c)

        ident = sb("ident", [P, P])
        half_pow = sb("half_pow", [P, 8])
        se_nat = sb("se_nat", [SE, P])
        mask_nat = sb("mask_nat", [GRAPHS * T, P])
        mask_sb = sb("mask_sb", [P, GRAPHS * T])
        wT = sb("wT", [P, 3, P])
        NSPLIT = 10 + TAPS
        w_hi = sb("w_hi", [P, NSPLIT, P], F32R)
        w_lo = sb("w_lo", [P, NSPLIT, P], F32R)
        w_se_pad = sb("w_se_pad", [P, P])
        neg_sq = sb("neg_sq", [P, P])
        hot = sb("hot", [P, 3])
        bse = sb("bse", [P, 1])
        left_sc = sb("left_sc", [P, 2])
        right_sc = sb("right_sc", [P, 2])
        bn = sb("bn", [P, 2, 4])
        bn_ve = sb("bn_ve", [P, 2])
        bn_rs = sb("bn_rs", [P, 2])
        bn_sc = sb("bn_sc", [P, 2])
        bn_ms = sb("bn_ms", [P, 2])
        bn_sh = sb("bn_sh", [P, 2])
        b0B = sb("b0B", [P, P])
        b1B = sb("b1B", [P, P])
        bmB = sb("bmB", [P, P])
        alphaB = sb("alphaB", [P, 1])
        alpha_eff = sb("alpha_eff", [P, 1])
        aB = sb("aB", [P, HEADS, 2, HD])
        wx = sb("wx", [P, D + 2 * HEADS])
        w_ei = sb("w_ei", [P, P])
        sel_col = sb("sel_col", [P, HEADS])
        sel = sb("sel", [P, HEADS, P], F32R)
        br = sb("br", [P, N], BF16)
        ones3 = sb("ones3", [P, P], BF16)
        ones = sb("ones", [P, P])

        a_nat = sb("a_nat", [P, T, N])
        x_in = [sb(f"x_in{i}", [P, T, D]) for i in range(2)]
        aT = [sb(f"aT{i}", [P, T, N]) for i in range(2)]
        rowsum = sb("rowsum", [P, T])
        degs = sb("degs", [P, 2, T])
        dis = sb("dis", [P, 2, T])
        dmask = sb("dmask", [P, T])
        t0 = sb("t0", [P, T, D])
        g0 = sb("g0", [P, T, D])
        y0 = sb("y0", [P, T, D])
        x1 = sb("x1", [P, T, D])
        r0 = sb("r0", [P, T, D])
        g1 = sb("g1", [P, T, D])
        y1 = t0
        x2 = [sb(f"x2_{i}", [P, T, D]) for i in range(2)]
        h_light, hT_light = sb("h_light", [P, T, D]), sb("hT_light", [P, N])
        h = [h_light, h_light, sb("h2", [P, T, D]), sb("h3", [P, T, D])]
        hT = [hT_light, hT_light, sb("hT2", [P, N]), sb("hT3", [P, N])]
        ln_st = [sb(f"ln_st{i}", [P, T, 6]) for i in range(4)]
        ln_mv = [sb(f"ln_mv{i}", [P, T, 2]) for i in range(4)]
        ln_ve = [sb(f"ln_ve{i}", [P, T]) for i in range(4)]
        ln_rs = [sb(f"ln_rs{i}", [P, T]) for i in range(4)]
        ln_nm = [sb(f"ln_nm{i}", [P, T]) for i in range(4)]

        h2_hi = sb("h2_hi", [P, N], F32R)
        h2_lo = sb("h2_lo", [P, N], F32R)
        c1 = sb("c1", [P, N])
        c1_hi = sb("c1_hi", [P, N + 2 * PAD], F32R)
        c1_lo = sb("c1_lo", [P, N + 2 * PAD], F32R)
        left_f = sb("left_f", [P, N])
        right_f = sb("right_f", [P, N])
        s_sq = right_f
        left = sb("left", [P, N], F32R)
        right = sb("right", [P, N], F32R)
        msg_b = left_f[:, :].rearrange("p (t d) -> p t d", d=D)
        msg = sb("msg", [P, T, D])
        ker_kadj = sb("ker_kadj", [P, T + 2, N])
        ker, kadj = ker_kadj[:, T:T + 2, :], ker_kadj[:, 0:T, :]
        adj_on = [sb(f"adj_on{i}", [P, T, N], BF16) for i in range(2)]
        n_hi = sb("n_hi", [P, N], F32R)
        n_lo = sb("n_lo", [P, N], F32R)
        u = c1
        c_hi = sb("c_hi", [P, N], F32R)
        c_lo = sb("c_lo", [P, N], F32R)
        rz = sb("rz", [P, T, 2 * D])
        q2 = sb("q2", [P, T, D])
        nn = sb("nn", [P, T, D])
        zd = sb("zd", [P, T, D])
        xn = sb("xn", [P, T, D])
        x3 = [sb(f"x3_{i}", [P, T, D]) for i in range(2)]

        WX = D + 2 * HEADS
        hsum = sb("hsum", [P, 1])
        hsB = sb("hsB", [P, P])
        meanh = sb("meanh", [P, P])
        hx = sb("hx", [P, T, WX])
        eh = sb("eh", [P, N], F32R)
        nei = sb("nei", [P, HEADS, N])
        mxl = sb("mxl", [P, HEADS])
        cB = sb("cB", [P, HEADS])
        z = sb("z", [P, T, HEADS])
        ex = sb("ex", [P, 4, T, HEADS])
        ee = sb("ee", [P, 4, T, HEADS])
        gf = sb("gf", [P, T, HEADS, 2, C])
        gp = [sb(f"gp{i}", [P, T, HEADS, 2, C], BF16) for i in range(3)]
        S = [sb(f"S{i}", [P, T, N], BF16) for i in range(2)]
        bf = sb("bf", [P, T, HEADS, C])
        sf = sb("sf", [P, HEADS, T, 2, C])
        tot = sb("tot", [P, HEADS, T, C])
        ue = sb("ue", [P, HEADS, T, C])
        flag = sb("flag", [P, HEADS, T])
        den = sb("den", [P, HEADS, T])
        rec = sb("rec", [P, HEADS, T])
        fm = sb("fm", [P, T, D])
        o1 = ue[:, :, :, 0:HD]
        o_sb = sb("o_sb", [P, T, D])

        wnat = aT[1][:, :, :].rearrange("p t n -> p (t n)")[:, 0:13 * P].rearrange("p (w i) -> p w i", i=P)
        c2nat = ker_kadj[:, :, :].rearrange("p t n -> p (t n)")[:, 0:P * TAPS]
        br_a, br_b = nei[:, 0, :], nei[:, 1, :]
        wa = nei[:, 2, 0:2 * D].rearrange("p (s h d) -> p s h d", s=2, d=HD)
        br_p = S[0][:, 0:3, :]

        set_loaded = sem("set_loaded")
        set_pool = sem("set_pool")
        set_dve = sem("set_dve")
        set_pe = sem("set_pe")
        a_loaded = sem("a_loaded")
        x_loaded = [sem(f"x_loaded{i}") for i in range(2)]
        stored = sem("stored")
        ln_st_ok = [sem(f"ln_st_ok{i}") for i in range(4)]
        ln_mv_ok = [sem(f"ln_mv_ok{i}") for i in range(4)]
        ln_ve_ok = [sem(f"ln_ve_ok{i}") for i in range(4)]
        ln_rs_ok = [sem(f"ln_rs_ok{i}") for i in range(4)]
        ln_nm_ok = [sem(f"ln_nm_ok{i}") for i in range(4)]
        h_ok = [sem(f"h_ok{i}") for i in range(4)]
        turned = [sem(f"turned{i}") for i in range(4)]
        hT_ok = [sem(f"hT_ok{i}") for i in range(4)]
        a_turned = sem("a_turned")
        aT_act = sem("aT_act")
        aT_dve = sem("aT_dve")
        rowsum_ok = sem("rowsum_ok")
        degs_ok = sem("degs_ok")
        dis_ok = sem("dis_ok")
        dmask_ok = sem("dmask_ok")
        lin0 = sem("lin0")
        t0_ok = sem("t0_ok")
        g0_ok = sem("g0_ok")
        agg0 = sem("agg0")
        y0_ok = sem("y0_ok")
        y0m_ok = sem("y0m_ok")
        x1_ok = sem("x1_ok")
        lin1 = sem("lin1")
        r0_ok = sem("r0_ok")
        g1_ok = sem("g1_ok")
        r1_ok = sem("r1_ok")
        agg1 = sem("agg1")
        y1_ok = sem("y1_ok")
        x2_ok = sem("x2_ok")
        h2_hi_ok = sem("h2_hi_ok")
        h2_lo_ok = sem("h2_lo_ok")
        conv1 = sem("conv1")
        c1_ok = sem("c1_ok")
        c1_hi_ok = sem("c1_hi_ok")
        c1_lo_ok = sem("c1_lo_ok")
        s_lin = sem("s_lin")
        s_sq_ok = sem("s_sq_ok")
        s_all = sem("s_all")
        left_f_ok = sem("left_f_ok")
        right_f_ok = sem("right_f_ok")
        lr_hi_ok = sem("lr_hi_ok")
        lr_ok = sem("lr_ok")
        msg_lin = sem("msg_lin")
        msg_b_ok = sem("msg_b_ok")
        msg_ok = sem("msg_ok")
        dist = sem("dist")
        ker_ok = sem("ker_ok")
        kadj_dve = sem("kadj_dve")
        kadj_pool = sem("kadj_pool")
        adj_on_ok = sem("adj_on_ok")
        nmp = sem("nmp")
        n_hi_ok = sem("n_hi_ok")
        n_lo_ok = sem("n_lo_ok")
        conv2 = sem("conv2")
        u_ok = sem("u_ok")
        c_hi_ok = sem("c_hi_ok")
        c_lo_ok = sem("c_lo_ok")
        gru = sem("gru")
        rz_ok = sem("rz_ok")
        q1_ok = sem("q1_ok")
        q2_ok = sem("q2_ok")
        nn_ok = sem("nn_ok")
        hmn_ok = sem("hmn_ok")
        zd_ok = sem("zd_ok")
        xn_ok = sem("xn_ok")
        x3_ok = sem("x3_ok")
        hx_lin = sem("hx_lin")
        hx_ok = sem("hx_ok")
        hsB_ok = sem("hsB_ok")
        mean_lin = sem("mean_lin")
        meanh_ok = sem("meanh_ok")
        ei_lin = sem("ei_lin")
        eh_hi_ok = sem("eh_hi_ok")
        eh_ok = sem("eh_ok")
        ei_rows = sem("ei_rows")
        nei_ok = sem("nei_ok")
        mxl_ok = sem("mxl_ok")
        cB_ok = sem("cB_ok")
        z_ok = sem("z_ok")
        ex_ok = sem("ex_ok")
        ee_ok = sem("ee_ok")
        gf_dve = sem("gf_dve")
        gf_pool = sem("gf_pool")
        gp0_ok = sem("gp0_ok")
        gr_ok = sem("gr_ok")
        gp1_ok = sem("gp1_ok")
        gp2_ok = sem("gp2_ok")
        all_sum = sem("all_sum")
        bf_ok = sem("bf_ok")
        S_ok = sem("S_ok")
        head_sum = sem("head_sum")
        sf_ok = sem("sf_ok")
        v1_ok = sem("v1_ok")
        v2_ok = sem("v2_ok")
        ue_ok = sem("ue_ok")
        tot_ok = sem("tot_ok")
        flag_ok = sem("flag_ok")
        den_ok = sem("den_ok")
        rec_ok = sem("rec_ok")
        fm_ok = sem("fm_ok")
        xf_ok = sem("xf_ok")
        o1_ok = sem("o1_ok")
        o_ok = sem("o_ok")

        x_v = x.rearrange("g (t p) d -> g p t d", p=P)
        adj_v = adj.rearrange("g (t p) m -> g p t m", p=P)
        out_v = out.rearrange("g (t p) d -> g p t d", p=P)

        def wide(col):
            return col.unsqueeze(2).broadcast_to([P, T, D])

        def run(eng, turn, light):
            light(0, 0, 0)
            turn(0, 0, 0, True, True, False)
            turn(1, 1, 1, True, True, True)
            with eng.Fori(0, GRAPHS // 2 - 2, 1) as k:
                turn(2 * k + 2, 0, k + 1, True, True, True)
                turn(2 * k + 3, 1, k + 2, True, True, True)
            turn(GRAPHS - 2, 0, GRAPHS // 2 - 1, True, True, True)
            turn(GRAPHS - 1, 1, 0, False, True, True)
            turn(GRAPHS, 0, 0, False, False, True)

        block = ctx.enter_context(nc.Block())

        @block.sync
        def _(sp):
            def fetch(q, b):
                sp.dma_start(a_nat[:, :, :], adj_v[q]).then_inc(a_loaded, 16)
                sp.dma_start(x_in[b][:, :, :], x_v[q]).then_inc(x_loaded[b], 16)

            fetch(0, 0)


            def load(dst, src):
                sp.dma_start(dst, src).then_inc(set_loaded, 16)

            load(wnat[:, 0, :], w0)
            load(wnat[:, 1, :], w1)
            load(wnat[:, 2, :], w_msg)
            load(wnat[:, 3, :], conv1_w.rearrange("o i k -> o (i k)"))
            load(wnat[:, 4:10, :], w_ih.rearrange("(r o) (c i) -> o r c i", o=P, c=2))
            load(wnat[:, 10:13, :], w_hh.rearrange("(r o) i -> o r i", o=P))
            load(c2nat, conv2_w.rearrange("o i k -> o (i k)"))
            load(se_nat[:, :], w_se)
            load(mask_nat[:, :], nodemask.rearrange("g (t p) -> (g t) p", p=P))
            load(wx[:, 0:D], w3)
            for i, v in enumerate((bn1_g, bn1_b, bn1_m, bn1_v)):
                load(bn[:, 0, i:i + 1], v.unsqueeze(1))
            for i, v in enumerate((bn2_g, bn2_b, bn2_m, bn2_v)):
                load(bn[:, 1, i:i + 1], v.unsqueeze(1))
            load(b0B[:, :], b0.partition_broadcast(P))
            load(b1B[:, :], b1.partition_broadcast(P))
            load(bmB[:, :], b_msg.partition_broadcast(P))
            load(alphaB[:, :], alpha.partition_broadcast(P))
            load(aB[:, :, :, :], a3.rearrange("h (s d) -> h s d", s=2).partition_broadcast(P))
            sp.wait_ge(set_pool, 1)
            for q in range(3):
                load(bse[32 * q:32 * q + SE, :], b_se.unsqueeze(1))
                row = slice(32 * q, 32 * q + 1)
                load(br_a[row, 0:D], b_ih[2 * D:3 * D].unsqueeze(0))
                load(br_a[row, D:3 * D], b_ih[0:2 * D].unsqueeze(0))
                load(br_b[row, D:4 * D], b_hh.unsqueeze(0))
            def value(v):
                return v if isinstance(v, int) else sp.snap(v)

            def turn(g, b, light, last):
                if light:
                    turned4, read, before = value(4 * (g + 1)), value(g + 1), value(g)
                    sp.wait_ge(set_pool, 1)
                    sp.wait_ge(a_turned, turned4)
                    sp.wait_ge(rowsum_ok, read)
                    sp.wait_ge(x1_ok, before)
                    fetch(g + 1, 1 - b)
                if last:
                    sp.wait_ge(set_pool, 1)
                    sp.wait_ge(o_ok, g)
                    sp.dma_start(out_v[g - 1], o_sb[:, :, :]).then_inc(stored, 16)

            turn(0, 0, True, False)
            turn(1, 1, True, True)
            with sp.Fori(2, GRAPHS - 3, 2) as g:
                turn(g, 0, True, True)
                turn(g + 1, 1, True, True)
            turn(GRAPHS - 2, 0, True, True)
            for g in range(GRAPHS - 1, GRAPHS + 1):
                turn(g, 0, False, True)
            sp.wait_ge(stored, 16 * GRAPHS)

        LOADS = 10 + 8 + 5 + 12

        @block.gpsimd
        def _(pool):
            pool.memset(bse[:, :], 0.0)
            pool.memset(br_a, 0.0)
            pool.memset(br_b, 0.0).then_inc(set_pool, 1)
            pool.memset(ident[:, :], 0.0).then_inc(set_pool, 1)
            pool.wait_ge(set_pool, 2)
            pool.affine_select(out=ident[:, :], in_=ident[:, :], compare_op=ALU.not_equal, fill=1.0, base=0,
                               pattern=[[-1, P]], channel_multiplier=1).then_inc(set_pool, 1)
            pool.memset(half_pow[:, :], -0.5).then_inc(set_pool, 1)
            pool.memset(w_se_pad[:, :], 0.0)
            pool.memset(w_ei[:, :], 0.0)
            pool.memset(ones[:, :], 1.0)
            pool.memset(br[:, :], 0.0)
            pool.memset(ones3[:, :], 0.0)
            pool.memset(neg_sq[:, :], 0.0)
            for t in (c1_hi, c1_lo):
                pool.memset(t[:, 0:PAD].bitcast(F32), 0.0)
                ins = pool.memset(t[:, PAD + N:2 * PAD + N].bitcast(F32), 0.0)
            ins.then_inc(set_pool, 1)
            pool.wait_ge(set_pool, 5)
            for q in range(3):
                pool.memset(ones3[32 * q:32 * q + 1, :], 1.0)
                ins = pool.memset(neg_sq[0:SE, 32 * q + 3:32 * q + 5], -1.0)
            ins.then_inc(set_pool, 1)
            pool.wait_ge(set_dve, 1)
            pool.tensor_tensor(bn_rs[:, :], bn_ve[:, :], half_pow[:, 0:2], ALU.pow).then_inc(set_pool, 1)

            def norm(i, q):
                pool.wait_ge(ln_ve_ok[i], q + 1)
                pool.wait_ge(ln_nm_ok[i], q)
                pool.wait_ge(h_ok[i], q)
                pool.tensor_tensor(ln_rs[i][:, :], ln_ve[i][:, :], half_pow[:, 0:T], ALU.pow).then_inc(ln_rs_ok[i], 1)

            def dis_pow(q):
                pool.wait_ge(degs_ok, 2 * (q + 1))
                pool.wait_ge(dmask_ok, q)
                pool.wait_ge(y1_ok, q)
                pool.tensor_tensor(dis[:, :, :].rearrange("p a t -> p (a t)"),
                                   degs[:, :, :].rearrange("p a t -> p (a t)"), half_pow[:, :], ALU.pow
                                   ).then_inc(dis_ok, 1)

            def scale_g0(q):
                pool.wait_ge(t0_ok, q + 1)
                pool.wait_ge(dis_ok, q + 1)
                pool.wait_ge(agg0, q)
                pool.wait_ge(y0_ok, q)
                pool.tensor_tensor(g0[:, :, :], t0[:, :, :], wide(dis[:, 0, :]), ALU.mult).then_inc(g0_ok, 1)

            def scale_y0(q):
                pool.wait_ge(y0_ok, q + 1)
                pool.wait_ge(dmask_ok, q + 1)
                pool.wait_ge(x1_ok, q)
                pool.tensor_tensor(y0[:, :, :], y0[:, :, :], wide(dmask[:, :]), ALU.mult).then_inc(y0m_ok, 1)

            def residual1(q):
                pool.wait_ge(r0_ok, q + 1)
                pool.wait_ge(x1_ok, q + 1)
                pool.wait_ge(x2_ok, q)
                pool.tensor_tensor(r0[:, :, :], r0[:, :, :], x1[:, :, :], ALU.add).then_inc(r1_ok, 1)

            def kernel_adj(q, b, j):
                pool.wait_ge(ker_ok, 4 * q + j + 1)
                pool.wait_ge(aT_dve, 2 * (q + 1))
                pool.wait_ge(nmp, q)
                pool.tensor_tensor(kadj[:, j, :], ker[:, j % 2, :], aT[b][:, j, :], ALU.mult).then_inc(kadj_pool, 1)

            def residual2(q, b):
                pool.wait_ge(nn_ok, q + 1)
                pool.wait_ge(x2_ok, q + 1)
                pool.wait_ge(x3_ok, q)
                pool.tensor_tensor(xn[:, :, :], nn[:, :, :], x2[b][:, :, :], ALU.add).then_inc(xn_ok, 1)

            def mean_col(q):
                pool.wait_ge(set_pool, 1)
                pool.wait_ge(hT_ok[3], q + 1)
                pool.wait_ge(mean_lin, q)
                pool.tensor_scalar(hsB[:, :], ones[:, :], hsum[:, 0:1], 1.0 / N, ALU.mult, ALU.mult).then_inc(hsB_ok, 1)

            def guard(q):
                pool.wait_ge(set_pool, 1)
                pool.wait_ge(mxl_ok, q + 1)
                pool.wait_ge(ex_ok, q)
                pool.partition_all_reduce(cB[:, :], mxl[:, :], P, RMAX).then_inc(cB_ok, 1)

            def weigh_f(q):
                pool.wait_ge(ee_ok, q + 1)
                pool.wait_ge(gr_ok, q)
                pool.wait_ge(gp0_ok, q)
                pool.tensor_tensor(gf[:, :, :, 1, 0:HD], hx[:, :, 0:D].rearrange("p t (h d) -> p t h d", d=HD),
                                   ee[:, 1, :, :].unsqueeze(3).broadcast_to([P, T, HEADS, HD]), ALU.mult
                                   ).then_inc(gf_pool, 1)

            def third_part(q):
                pool.wait_ge(gp1_ok, q + 1)
                pool.wait_ge(head_sum, 4 * q)
                flat = "p t h s c -> p (t h s c)"
                pool.tensor_tensor(gp[2][:, :, :, :, :].rearrange(flat), gf[:, :, :, :, :].rearrange(flat),
                                   gp[1][:, :, :, :, :].rearrange(flat), ALU.subtract).then_inc(gp2_ok, 1)

            def fallback(q, b):
                pool.wait_ge(flag_ok, q + 1)
                pool.wait_ge(meanh_ok, q + 1)
                pool.wait_ge(xf_ok, q)
                pool.tensor_tensor(fm[:, :, :].rearrange("p t (h d) -> p h t d", d=HD),
                                   flag[:, :, :].unsqueeze(3).broadcast_to([P, HEADS, T, HD]),
                                   meanh[:, :].rearrange("p (h d) -> p h d", d=HD).unsqueeze(2).broadcast_to([P, HEADS, T, HD]),
                                   ALU.mult).then_inc(fm_ok, 1)
                pool.wait_ge(fm_ok, q + 1)
                pool.wait_ge(o_ok, q)
                pool.tensor_tensor(fm[:, :, :], fm[:, :, :], x3[b][:, :, :], ALU.add).then_inc(xf_ok, 1)

            def weigh_e(q):
                pool.wait_ge(sf_ok, 4 * (q + 1))
                pool.wait_ge(ee_ok, q + 1)
                pool.wait_ge(o_ok, q)
                pool.tensor_tensor(ue[:, :, :, :], sf[:, :, :, 0, :],
                                   ee[:, 2, :, :].rearrange("p t h -> p h t").unsqueeze(3).broadcast_to([P, HEADS, T, C]),
                                   ALU.mult).then_inc(ue_ok, 1)

            def light_a(q):
                dis_pow(q)
                norm(0, q)

            def light_only(q, b, k):
                light_a(q)
                scale_g0(q)
                scale_y0(q)
                norm(1, q)
                residual1(q)

            def turn(g, b, k, light, heavy, last):
                if heavy:
                    norm(2, g)
                if light:
                    light_a(g + 1)
                if last:
                    norm(3, g - 1)
                    mean_col(g - 1)
                    guard(g - 1)
                if heavy:
                    kernel_adj(g, b, 1)
                if last:
                    weigh_f(g - 1)
                if light:
                    scale_g0(g + 1)
                if heavy:
                    kernel_adj(g, b, 3)
                if last:
                    third_part(g - 1)
                if light:
                    scale_y0(g + 1)
                    norm(1, g + 1)
                    residual1(g + 1)
                if last:
                    weigh_e(g - 1)
                    fallback(g - 1, 1 - b)
                if heavy:
                    residual2(g, b)

            run(pool, turn, light_only)

        @block.scalar
        def _(act):
            def norm(i, q, src):
                act.wait_ge(ln_nm_ok[i], q + 1)
                act.wait_ge(ln_rs_ok[i], q + 1)
                act.wait_ge(turned[i], q)
                if i == 2:
                    act.wait_ge(hmn_ok, q)
                for t in range(T):
                    ins = act.activation(h[i][:, t, :], src[:, t, :], ACT.Relu, bias=ln_nm[i][:, t:t + 1],
                                         scale=ln_rs[i][:, t:t + 1])
                ins.then_inc(h_ok[i], 1)

            def take_aT(q, b, j, warm=True):
                act.wait_ge(a_turned, 4 * q + j + 1)
                if warm:
                    act.wait_ge(adj_on_ok, q - 1)
                    act.wait_ge(kadj_dve, 2 * (q - 1))
                    act.wait_ge(kadj_pool, 2 * (q - 1))
                act.activation(aT[b][:, j, :], bank(LIGHT + j % 2), ACT.Copy).then_inc(aT_act, 1)

            def take_hT(i, q, at, used):
                act.wait_ge(turned[i], q + 1)
                act.wait_ge(used, q)
                if i == 2:
                    act.wait_ge(u_ok, q)
                    act.wait_ge(h2_lo_ok, q)
                    act.wait_ge(s_lin, q)
                if i == 3:
                    act.wait_ge(hsB_ok, q)
                    act.activation(hT[i][:, :], bank(at), ACT.Copy, accum_out=hsum[:, 0:1]).then_inc(hT_ok[i], 1)
                else:
                    act.activation(hT[i][:, :], bank(at), ACT.Copy).then_inc(hT_ok[i], 1)

            def take_c1(q):
                act.wait_ge(conv1, q + 1)
                act.wait_ge(c_lo_ok, q)
                act.activation(c1[:, :], bank(HEAVY + 1), ACT.Relu, bias=bn_sh[:, 0:1]).then_inc(c1_ok, 1)

            def square_s(q):
                act.wait_ge(s_lin, q + 1)
                act.wait_ge(lr_ok, 2 * q)
                act.activation(s_sq[:, :], bank(HEAVY + 2), ACT.Square, bias=bse[:, 0:1]).then_inc(s_sq_ok, 1)

            def sides(q):
                act.wait_ge(s_all, q + 1)
                act.wait_ge(lr_ok, 2 * q)
                act.activation(left_f[:, :], bank(HEAVY + 2), ACT.Identity, bias=left_sc[:, 1:2],
                               scale=left_sc[:, 0:1]).then_inc(left_f_ok, 1)
                act.activation(right_f[:, :], bank(HEAVY + 2), ACT.Identity, bias=right_sc[:, 1:2],
                               scale=right_sc[:, 0:1]).then_inc(right_f_ok, 1)

            def relu_msg(q):
                act.wait_ge(msg_b_ok, q + 1)
                act.wait_ge(nmp, q)
                act.activation(msg[:, :, :], msg_b, ACT.Relu).then_inc(msg_ok, 1)

            def exps(q, js):
                for j in js:
                    act.wait_ge(dist, 4 * q + j + 1)
                    act.wait_ge(kadj_pool if j % 2 else kadj_dve, 2 * q + j // 2)
                    act.activation(ker[:, j % 2, :], bank(HEAVY + 2 * (1 - j % 2)), ACT.Exp).then_inc(ker_ok, 1)

            def take_n(q):
                act.wait_ge(nmp, q + 1)
                act.wait_ge(gru, 4 * q)
                act.activation(n_hi[:, :], bank(HEAVY + 2), ACT.Copy).then_inc(n_hi_ok, 1)

            def relu_conv(q):
                act.wait_ge(u_ok, q + 1)
                act.wait_ge(gru, 4 * q)
                act.activation(c_hi[:, :], u[:, :], ACT.Relu).then_inc(c_hi_ok, 1)

            def gates(q, t):
                act.wait_ge(gru, 4 * q + t + 1)
                act.wait_ge(zd_ok, q)
                act.activation(rz[:, t, :], bank(HEAVY + t % 3)[:, D:3 * D], ACT.Tanh, scale=0.5).then_inc(rz_ok, 1)

            def new_gate(q):
                act.wait_ge(q2_ok, 4 * (q + 1))
                act.wait_ge(xn_ok, q)
                act.activation(nn[:, :, :], q2[:, :, :], ACT.Tanh).then_inc(nn_ok, 1)

            def take_hx(q):
                for i in range(2):
                    act.wait_ge(hx_lin, 2 * q + i + 1)
                    act.wait_ge(S_ok, 4 * q)
                    act.wait_ge(gf_dve, q)
                    act.wait_ge(gf_pool, q)
                    act.activation(hx[:, 2 * i:2 * i + 2, :], tiles(bank(LAST + 1 + i)[:, 0:2 * WX], WX), ACT.Copy
                                   ).then_inc(hx_ok, 1)

            def take_mean(q):
                act.wait_ge(mean_lin, q + 1)
                act.wait_ge(fm_ok, q)
                act.activation(meanh[:, :], bank(LAST)[:, 0:P], ACT.Copy).then_inc(meanh_ok, 1)

            def take_ei(q):
                act.wait_ge(ei_lin, q + 1)
                act.wait_ge(ei_rows, 4 * q)
                act.activation(eh[:, :], bank(LAST), ACT.Copy).then_inc(eh_hi_ok, 1)

            def take_rows(q, hs):
                for i in hs:
                    act.wait_ge(ei_rows, 4 * q + i + 1)
                    act.wait_ge(S_ok, 4 * q)
                    act.activation(nei[:, i, :], bank(LAST + 1 + i % 2), ACT.Copy).then_inc(nei_ok, 1)

            def exp_e(q):
                act.wait_ge(ex_ok, q + 1)
                act.wait_ge(gf_dve, q)
                act.wait_ge(v2_ok, q)
                act.wait_ge(ue_ok, q)
                act.activation(ee[:, :, :, :].rearrange("p k t h -> p (k t h)"),
                               ex[:, :, :, :].rearrange("p k t h -> p (k t h)"), ACT.Exp).then_inc(ee_ok, 1)

            flat = "p t h s c -> p (t h s c)"

            def first_part(q):
                act.wait_ge(gf_dve, q + 1)
                act.wait_ge(gf_pool, q + 1)
                act.wait_ge(head_sum, 4 * q)
                act.activation(gp[0][:, :, :, :, :].rearrange(flat), gf[:, :, :, :, :].rearrange(flat), ACT.Copy
                               ).then_inc(gp0_ok, 1)

            def second_part(q):
                act.wait_ge(gr_ok, q + 1)
                act.activation(gp[1][:, :, :, :, :].rearrange(flat), gf[:, :, :, :, :].rearrange(flat), ACT.Copy
                               ).then_inc(gp1_ok, 1)

            def take_all(q):
                for i in range(2):
                    act.wait_ge(all_sum, 2 * q + i + 1)
                    act.wait_ge(v1_ok, q)
                    act.activation(bf[:, 2 * i:2 * i + 2, :, :].rearrange("p t h c -> p (t h c)"),
                                   bank(LAST + i)[:, 0:2 * HEADS * C], ACT.Copy).then_inc(bf_ok, 1)

            def take_head(q, i):
                act.wait_ge(head_sum, 4 * q + i + 1)
                act.wait_ge(v1_ok, q)
                act.wait_ge(ue_ok, q)
                act.activation(sf[:, i, :, :, :].rearrange("p t s c -> p (t s c)"),
                               bank(LAST + 2 - 2 * (i % 2))[:, 0:T * 2 * C], ACT.Copy).then_inc(sf_ok, 1)

            def light_only(q, b, k):
                take_aT(q, b, 0, False)
                take_aT(q, b, 2, False)
                norm(0, q, x_in[b])
                take_hT(0, q, LIGHT, lin0)
                norm(1, q, x1)
                take_hT(1, q, LIGHT + 1, lin1)

            act.wait_ge(set_dve, 9)

            def turn(g, b, k, light, heavy, last):
                a, z_ = g + 1, g - 1
                if heavy:
                    norm(2, g, x2[b])
                if light:
                    take_aT(a, 1 - b, 0)
                if heavy:
                    take_hT(2, g, HEAVY, msg_lin)
                if light:
                    norm(0, a, x_in[1 - b])
                if last:
                    norm(3, z_, x3[1 - b])
                if heavy:
                    take_c1(g)
                    square_s(g)
                if light:
                    take_aT(a, 1 - b, 2)
                if last:
                    take_hT(3, z_, LAST, ei_lin)
                if heavy:
                    sides(g)
                if last:
                    take_hx(z_)
                    take_mean(z_)
                    take_ei(z_)
                if heavy:
                    relu_msg(g)
                    exps(g, (0, 1))
                if light:
                    take_hT(0, a, LIGHT, lin0)
                if last:
                    exp_e(z_)
                    take_rows(z_, (0, 1))
                    first_part(z_)
                if heavy:
                    exps(g, (2, 3))
                if last:
                    take_rows(z_, (2, 3))
                    second_part(z_)
                    take_all(z_)
                    take_head(z_, 0)
                if light:
                    norm(1, a, x1)
                if last:
                    take_head(z_, 1)
                if light:
                    take_hT(1, a, LIGHT + 1, lin1)
                if last:
                    take_head(z_, 2)
                if heavy:
                    take_n(g)
                if last:
                    take_head(z_, 3)
                if heavy:
                    relu_conv(g)
                    for t in range(T):
                        gates(g, t)
                    new_gate(g)

            run(act, turn, light_only)

        @block.tensor
        def _(pe):
            pe.wait_ge(set_dve, 3)

            def turn_weight(i, src, n=P):
                return pe.transpose(bank(i // 4)[:, (i % 4) * P:(i % 4) * P + n], src, ident[0:n, 0:n])

            for i in range(3):
                turn_weight(i, wnat[:, i, :])
            turn_weight(3, se_nat[:, :], SE)
            turn_weight(4, mask_nat[:, :], GRAPHS * T)
            turn_weight(5, wnat[:, 3, :])
            for n, r in enumerate((2, 0, 1)):
                turn_weight(6 + n, wnat[:, 4 + 2 * r, :])
                turn_weight(9 + n, wnat[:, 5 + 2 * r, :])
            for r in range(3):
                turn_weight(12 + r, wnat[:, 10 + r, :])
            for k in range(TAPS):
                ins = turn_weight(15 + k, c2nat.rearrange("p (i k) -> p i k", k=TAPS)[:, :, k])
            ins.then_inc(set_pe, 1)
            pe.wait_ge(set_dve, 9)

            def split_mm(dst, wh, wl, mh, ml, start, stop):
                pe.matmul(dst, wh, mh, start=start, stop=False, skip_group_check=True)
                pe.matmul(dst, wh, ml, start=False, stop=False, skip_group_check=True)
                return pe.matmul(dst, wl, mh, start=False, stop=stop, skip_group_check=True)

            def turn_a(q, b, k, js):
                if 0 in js:
                    pe.wait_ge(a_loaded, 16 * (q + 1))
                    pe.wait_ge(g1_ok, q)
                    pe.wait_ge(y1_ok, q)
                for j in js:
                    if j == 2:
                        pe.wait_ge(aT_act, 2 * q + 1)
                    if j == 3:
                        pe.wait_ge(aT_dve, 2 * q + 1)
                    for t in range(T):
                        ins = pe.transpose(bank(LIGHT + j % 2)[:, t * P:(t + 1) * P], a_nat[:, t, j * P:(j + 1) * P],
                                           ident[:, :])
                    ins.then_inc(a_turned, 1)

            def turn_h(i, q, at):
                pe.wait_ge(h_ok[i], q + 1)
                for t in range(T):
                    ins = pe.transpose(bank(at)[:, t * P:(t + 1) * P], h[i][:, t, :], ident[:, :])
                ins.then_inc(turned[i], 1)

            def linear(at, i, w, done, q):
                pe.wait_ge(hT_ok[i], q + 1)
                for t in range(T):
                    ins = pe.matmul(bank(at)[:, t * P:(t + 1) * P], hT[i][:, t * P:(t + 1) * P], w, start=True,
                                    stop=True, skip_group_check=True)
                ins.then_inc(done, 1)

            def aggregate(at, b, g, done):
                for t in range(T):
                    for j in range(T):
                        ins = pe.matmul(bank(at)[:, t * P:(t + 1) * P], aT[b][:, j, t * P:(t + 1) * P], g[:, j, :],
                                        start=(j == 0), stop=(j == T - 1), skip_group_check=True)
                ins.then_inc(done, 1)

            def light1(q, b):
                pe.wait_ge(aT_act, 2 * (q + 1))
                turn_h(0, q, LIGHT)

            def light2(q, b):
                pe.wait_ge(aT_dve, 2 * (q + 1))
                linear(LIGHT + 1, 0, wT[:, 0, :], lin0, q)

            def light3(q, b):
                pe.wait_ge(g0_ok, q + 1)
                aggregate(LIGHT, b, g0, agg0)

            def light4(q, b):
                pe.wait_ge(t0_ok, q + 1)
                turn_h(1, q, LIGHT + 1)

            def light5(q, b):
                pe.wait_ge(y0_ok, q + 1)
                linear(LIGHT, 1, wT[:, 1, :], lin1, q)

            def light6(q, b):
                pe.wait_ge(g1_ok, q + 1)
                aggregate(LIGHT + 1, b, g1, agg1)

            B0, B1, B2 = HEAVY, HEAVY + 1, HEAVY + 2

            def do_conv1(q):
                pe.wait_ge(h2_lo_ok, q + 1)
                split_mm(bank(B1), w_hi[:, 0, :], w_lo[:, 0, :], h2_hi[:, :], h2_lo[:, :], True, True
                         ).then_inc(conv1, 1)

            def do_s(q):
                pe.wait_ge(hT_ok[2], q + 1)
                pe.matmul(bank(B2), w_se_pad[:, :], hT[2][:, :], start=True, stop=False, skip_group_check=True
                          ).then_inc(s_lin, 1)

            def do_sq(q):
                pe.wait_ge(s_sq_ok, q + 1)
                pe.matmul(bank(B2), neg_sq[:, :], s_sq[:, :], start=False, stop=True, skip_group_check=True
                          ).then_inc(s_all, 1)

            def do_dist(q, js):
                for j in js:
                    if j == 0:
                        pe.wait_ge(lr_ok, 2 * (q + 1))
                    if j == 1:
                        pe.wait_ge(msg_b_ok, q + 1)
                    if j >= 2:
                        pe.wait_ge(ker_ok, 4 * q + j - 1)
                    pe.matmul(bank(HEAVY + 2 * (1 - j % 2)), left[:, j * P:(j + 1) * P], right[:, :], start=True,
                              stop=True, skip_group_check=True).then_inc(dist, 1)

            def do_conv2(q, ks):
                if 0 in ks:
                    pe.wait_ge(c1_lo_ok, q + 1)
                for k in ks:
                    ins = split_mm(bank(B1), w_hi[:, 10 + k, :], w_lo[:, 10 + k, :], c1_hi[:, k:k + N],
                                   c1_lo[:, k:k + N], k == 0, k == TAPS - 1)
                    if k == TAPS - 1:
                        ins.then_inc(conv2, 1)

            def do_nmp(q):
                pe.wait_ge(msg_ok, q + 1)
                pe.wait_ge(kadj_dve, 2 * (q + 1))
                pe.wait_ge(kadj_pool, 2 * (q + 1))
                pe.wait_ge(ker_ok, 4 * (q + 1))
                for j in range(T):
                    ins = pe.matmul(bank(B2), msg[:, j, :], kadj[:, j, :], start=(j == 0), stop=(j == T - 1),
                                    skip_group_check=True)
                ins.then_inc(nmp, 1)

            def do_gru(q):
                for t in range(T):
                    dst = bank(HEAVY + t % 3)
                    c = slice(t * P, (t + 1) * P)
                    if t == 1:
                        pe.wait_ge(u_ok, q + 1)
                    if t == 2:
                        pe.wait_ge(n_lo_ok, q + 1)
                    if t == 3:
                        pe.wait_ge(q2_ok, 4 * q + 1)
                    pe.matmul(dst, ones3[:, :], br[:, :], start=True, stop=False, skip_group_check=True)

                    def part(cols, hi, lo, i, last):
                        wh = w_hi[:, i:i + 3, :].rearrange("p a o -> p (a o)")
                        wl = w_lo[:, i:i + 3, :].rearrange("p a o -> p (a o)")
                        pe.matmul(dst[:, cols], hi[:, c], wh, start=False, stop=False, skip_group_check=True)
                        pe.matmul(dst[:, cols], hi[:, c], wl, start=False, stop=False, skip_group_check=True)
                        return pe.matmul(dst[:, cols], lo[:, c], wh, start=False, stop=last, skip_group_check=True)

                    part(slice(D, 4 * D), h2_hi, h2_lo, 7, False)
                    pe.wait_ge(n_lo_ok, q + 1)
                    part(slice(0, 3 * D), n_hi, n_lo, 4, False)
                    pe.wait_ge(c_lo_ok, q + 1)
                    part(slice(0, 3 * D), c_hi, c_lo, 1, True).then_inc(gru, 1)

            C0, C1, C2 = LAST, LAST + 1, LAST + 2

            def do_hx(q):
                pe.wait_ge(hT_ok[3], q + 1)
                for i in range(2):
                    for t in range(2):
                        c = slice((2 * i + t) * P, (2 * i + t + 1) * P)
                        ins = pe.matmul(bank(C1 + i)[:, t * WX:(t + 1) * WX], hT[3][:, c], wx[:, :], start=True,
                                        stop=True, skip_group_check=True)
                    ins.then_inc(hx_lin, 1)

            def do_mean(q):
                pe.wait_ge(hsB_ok, q + 1)
                pe.matmul(bank(C0)[:, 0:P], hsB[:, :], wx[:, 0:D], start=True, stop=True, skip_group_check=True
                          ).then_inc(mean_lin, 1)

            def do_ei(q):
                pe.wait_ge(meanh_ok, q + 1)
                pe.matmul(bank(C0), w_ei[:, :], hT[3][:, :], start=True, stop=True, skip_group_check=True
                          ).then_inc(ei_lin, 1)

            def do_rows(q, hs):
                for i in hs:
                    if i == 0:
                        pe.wait_ge(eh_ok, q + 1)
                    if i < 2:
                        pe.wait_ge(hx_ok, 2 * q + i + 1)
                    else:
                        pe.wait_ge(nei_ok, 4 * q + i - 1)
                    pe.matmul(bank(C1 + i % 2), sel[:, i, :], eh[:, :], start=True, stop=True, skip_group_check=True
                              ).then_inc(ei_rows, 1)

            def do_all(q, b):
                pe.wait_ge(gp2_ok, q + 1)
                pe.wait_ge(adj_on_ok, q + 1)
                for i in range(2):
                    if i == 1:
                        pe.wait_ge(nei_ok, 4 * q + 3)
                    for t in range(2):
                        tn = 2 * i + t
                        dst = tiles(bank(C0 + i)[:, t * HEADS * C:(t + 1) * HEADS * C], C)
                        for j in range(T):
                            for p in range(3):
                                ins = pe.matmul(dst, adj_on[b][:, j, tn * P:(tn + 1) * P], gp[p][:, j, :, 1, :],
                                                start=(j == 0 and p == 0), stop=(j == T - 1 and p == 2),
                                                skip_group_check=True)
                    ins.then_inc(all_sum, 1)

            def do_head(q, i):
                if i == 0:
                    pe.wait_ge(nei_ok, 4 * (q + 1))
                if i == 1:
                    pe.wait_ge(bf_ok, 2 * q + 1)
                if i >= 2:
                    pe.wait_ge(sf_ok, 4 * q + i - 1)
                pe.wait_ge(S_ok, 4 * q + i + 1)
                for tn in range(T):
                    dst = bank(C2 - 2 * (i % 2))[:, tn * 2 * C:(tn + 1) * 2 * C]
                    for j in range(T):
                        for p in range(3):
                            ins = pe.matmul(dst, S[i % 2][:, j, tn * P:(tn + 1) * P],
                                            gp[p][:, j, i, :, :].rearrange("p s c -> p (s c)"),
                                            start=(j == 0 and p == 0), stop=(j == T - 1 and p == 2),
                                            skip_group_check=True)
                ins.then_inc(head_sum, 1)

            def light_only(q, b, k):
                turn_a(q, b, k, range(T))
                for f in (light1, light2, light3, light4, light5, light6):
                    f(q, b)

            def turn(g, b, k, light, heavy, last):
                a, al, z_ = g + 1, 1 - b, g - 1
                if heavy:
                    pe.wait_ge(q2_ok, 4 * g)
                    turn_h(2, g, B0)
                if light:
                    turn_a(a, al, k, (0, 1))
                if last:
                    pe.wait_ge(sf_ok, 4 * z_)
                    turn_h(3, z_, C0)
                if heavy:
                    do_conv1(g)
                    do_s(g)
                if light:
                    turn_a(a, al, k, (2, 3))
                if last:
                    do_hx(z_)
                    do_mean(z_)
                if heavy:
                    do_sq(g)
                    linear(B0, 2, wT[:, 2, :], msg_lin, g)
                if last:
                    do_ei(z_)
                if light:
                    light1(a, al)
                if heavy:
                    do_conv2_gate(g)
                    do_conv2(g, range(0, 2))
                    do_dist(g, (0, 1))
                if last:
                    do_rows(z_, (0, 1))
                if light:
                    light2(a, al)
                if heavy:
                    do_conv2(g, range(2, 4))
                    do_dist(g, (2, 3))
                if last:
                    do_rows(z_, (2, 3))
                if heavy:
                    do_conv2(g, range(4, 7))
                if light:
                    light3(a, al)
                if last:
                    do_all(z_, al)
                    do_head(z_, 0)
                if light:
                    light4(a, al)
                if heavy:
                    do_conv2(g, range(7, 10))
                if last:
                    do_head(z_, 1)
                if light:
                    light5(a, al)
                if heavy:
                    do_conv2(g, range(10, 13))
                if last:
                    do_head(z_, 2)
                if heavy:
                    do_nmp(g)
                if light:
                    light6(a, al)
                if heavy:
                    do_conv2(g, range(13, TAPS))
                if last:
                    do_head(z_, 3)
                if heavy:
                    do_gru(g)

            def do_conv2_gate(q):
                pe.wait_ge(c1_ok, q + 1)

            run(pe, turn, light_only)

        @block.vector
        def _(dve):
            dve.wait_ge(set_loaded, 16 * LOADS)
            dve.wait_ge(set_pool, 6)
            dve.tensor_scalar(bn_ve[:, :], bn[:, :, 3], BN_EPS, None, ALU.add).then_inc(set_dve, 1)
            dve.wait_ge(set_pool, 7)
            dve.tensor_tensor(bn_sc[:, :], bn_rs[:, :], bn[:, :, 0], ALU.mult).then_inc(set_dve, 1)
            dve.wait_ge(set_dve, 2)
            dve.tensor_tensor(bn_ms[:, :], bn_sc[:, :], bn[:, :, 2], ALU.mult)
            dve.tensor_scalar(wnat[:, 3, :], wnat[:, 3, :], bn_sc[:, 0:1], None, ALU.mult)
            dve.tensor_scalar(c2nat, c2nat, bn_sc[:, 1:2], None, ALU.mult).then_inc(set_dve, 1)
            dve.wait_ge(set_dve, 3)
            dve.tensor_tensor(bn_sh[:, :], bn[:, :, 1], bn_ms[:, :], ALU.subtract)
            dve.tensor_scalar(alpha_eff[:, :], alphaB[:, :], 1e-10, None, ALU.max)
            hots = ident[:, 0:96].rearrange("p (q c) -> p q c", c=32)
            dve.tensor_reduce(hot[:, 0:1], hots[:, :, 0:3], AX.XY, ALU.add)
            dve.tensor_reduce(hot[:, 1:2], hots[:, :, 3:4], AX.XY, ALU.add)
            dve.tensor_reduce(hot[:, 2:3], hots[:, :, 4:5], AX.XY, ALU.add)
            dve.tensor_tensor(sel_col[:, :], ident[:, 0:HEADS], ident[:, 32:32 + HEADS], ALU.add)
            w3h = wx[:, 0:D].rearrange("p (h d) -> p h d", d=HD)
            for s in range(2):
                dve.tensor_tensor(wa[:, s, :, :], w3h, aB[:, :, s, :], ALU.mult)
            dve.tensor_tensor(br_a, br_a, br_b, ALU.add).then_inc(set_dve, 1)
            dve.wait_ge(set_dve, 4)
            dve.tensor_copy(br_p[:, 0, :], br_a)
            dve.scalar_tensor_tensor(out=left_sc[:, 0:1], in0=hot[:, 0:1], scalar=2.0, in1=hot[:, 1:2], op0=ALU.mult,
                                     op1=ALU.add)
            dve.scalar_tensor_tensor(out=left_sc[:, 1:2], in0=bse[:, :], scalar=2.0, in1=hot[:, 2:3], op0=ALU.mult,
                                     op1=ALU.add)
            dve.tensor_tensor(right_sc[:, 0:1], hot[:, 0:1], hot[:, 2:3], ALU.add)
            dve.tensor_tensor(right_sc[:, 1:2], bse[:, :], hot[:, 1:2], ALU.add)
            dve.tensor_copy(sel[:, :, :], sel_col[:, :].unsqueeze(2).broadcast_to([P, HEADS, P]))
            dve.tensor_reduce(wx[:, D:D + HEADS], wa[:, 1, :, :], AX.X, ALU.add)
            dve.tensor_reduce(wx[:, D + HEADS:WX], wa[:, 0, :, :], AX.X, ALU.add).then_inc(set_dve, 1)
            dve.wait_ge(set_dve, 5)
            for q in range(2):
                dve.tensor_scalar(w_ei[:, 32 * q:32 * q + HEADS], wx[:, D + HEADS:WX], -1.0, None, ALU.mult)
            dve.tensor_tensor(br_b, br_a, br_p[:, 0, :], ALU.subtract).then_inc(set_dve, 1)
            dve.wait_ge(set_dve, 6)
            dve.tensor_copy(br_p[:, 1, :], br_b)
            dve.tensor_copy(br[0:1, :], br_p[0:1, 0, :])
            dve.wait_ge(set_pe, 1)
            dve.tensor_copy(wT[:, :, :], tiles(bank(0)[:, 0:3 * P]))
            for q in range(3):
                dve.tensor_copy(w_se_pad[:, 32 * q:32 * q + SE], bank(0)[:, 3 * P:3 * P + SE])
            dve.tensor_copy(mask_sb[:, :], bank(1)[:, 0:GRAPHS * T])
            split = psum[:, :, :].rearrange("p b n -> p (b n)")[:, 5 * P:(5 + NSPLIT) * P]
            dve.tensor_copy(w_hi[:, :, :].rearrange("p a o -> p (a o)"), split).then_inc(set_dve, 1)
            dve.wait_ge(set_dve, 7)
            dve.tensor_tensor(w_lo[:, :, :].rearrange("p a o -> p (a o)"), split,
                              w_hi[:, :, :].rearrange("p a o -> p (a o)").bitcast(F32), ALU.subtract)
            dve.tensor_tensor(br_p[:, 2, :], br_b, br_p[:, 1, :], ALU.subtract)
            dve.tensor_copy(br[32:33, :], br_p[32:33, 1, :]).then_inc(set_dve, 1)
            dve.wait_ge(set_dve, 8)
            dve.tensor_copy(br[64:65, :], br_p[64:65, 2, :]).then_inc(set_dve, 1)

            def norm(i, q, src):
                dve.wait_ge(ln_mv_ok[i], q)
                for t in range(T):
                    ins = dve.bn_stats(ln_st[i][:, t, :], src[:, t, :])
                ins.then_inc(ln_st_ok[i], 1)
                dve.wait_ge(set_pool, 1)
                dve.wait_ge(ln_st_ok[i], q + 1)
                dve.wait_ge(ln_nm_ok[i], q)
                dve.wait_ge(ln_ve_ok[i], q)
                for t in range(T):
                    ins = dve.bn_aggr(ln_mv[i][:, t, :], ln_st[i][:, t, :])
                ins.then_inc(ln_mv_ok[i], 1)
                dve.wait_ge(ln_mv_ok[i], q + 1)
                dve.wait_ge(ln_rs_ok[i], q)
                dve.tensor_scalar(ln_ve[i][:, :], ln_mv[i][:, :, 1], LN_EPS, None, ALU.add).then_inc(ln_ve_ok[i], 1)

            def shift(i, q):
                dve.wait_ge(ln_rs_ok[i], q + 1)
                dve.wait_ge(h_ok[i], q)
                dve.scalar_tensor_tensor(out=ln_nm[i][:, :], in0=ln_mv[i][:, :, 0], scalar=-1.0, in1=ln_rs[i][:, :],
                                         op0=ALU.mult, op1=ALU.mult).then_inc(ln_nm_ok[i], 1)

            def degrees(q, b, k):
                dve.wait_ge(a_loaded, 16 * (q + 1))
                dve.wait_ge(x_loaded[b], 16 * (k + 1))
                dve.wait_ge(degs_ok, 2 * q)
                dve.tensor_reduce(rowsum[:, :], a_nat[:, :, :], AX.X, ALU.add).then_inc(rowsum_ok, 1)
                dve.wait_ge(rowsum_ok, q + 1)
                dve.wait_ge(dis_ok, q)
                dve.tensor_scalar(degs[:, 0, :], rowsum[:, :], 1.0, 1e-8, ALU.add, ALU.add).then_inc(degs_ok, 1)
                dve.scalar_tensor_tensor(out=degs[:, 1, :], in0=rowsum[:, :], scalar=0.0, in1=rowsum[:, :],
                                         op0=ALU.is_equal, op1=ALU.add).then_inc(degs_ok, 1)

            def mask_dis(q):
                dve.wait_ge(dis_ok, q + 1)
                dve.wait_ge(y0m_ok, q)
                dve.tensor_tensor(dmask[:, :], dis[:, 0, :], mask_sb[:, bass.ds(q * T, T)], ALU.mult
                                  ).then_inc(dmask_ok, 1)

            def take_aT(q, b, j, warm=True):
                dve.wait_ge(a_turned, 4 * q + j + 1)
                if warm:
                    dve.wait_ge(adj_on_ok, q - 1)
                    dve.wait_ge(kadj_dve, 2 * (q - 1))
                    dve.wait_ge(kadj_pool, 2 * (q - 1))
                dve.tensor_copy(aT[b][:, j, :], bank(LIGHT + j % 2)).then_inc(aT_dve, 1)

            def bias0(q):
                dve.wait_ge(lin0, q + 1)
                dve.wait_ge(g0_ok, q)
                dve.tensor_tensor(t0[:, :, :], tiles(bank(LIGHT + 1)), b0B[:, :].unsqueeze(1).broadcast_to([P, T, D]),
                                  ALU.add).then_inc(t0_ok, 1)

            def self0(q):
                dve.wait_ge(agg0, q + 1)
                dve.wait_ge(g0_ok, q + 1)
                dve.wait_ge(y0m_ok, q)
                dve.tensor_tensor(y0[:, :, :], tiles(bank(LIGHT)), g0[:, :, :], ALU.add).then_inc(y0_ok, 1)

            def add0(q, b):
                dve.wait_ge(y0m_ok, q + 1)
                dve.wait_ge(h_ok[1], q)
                dve.wait_ge(r1_ok, q)
                dve.wait_ge(h_ok[0], q + 1)
                dve.scalar_tensor_tensor(out=x1[:, :, :], in0=y0[:, :, :], scalar=0.0, in1=x_in[b][:, :, :],
                                         op0=ALU.max, op1=ALU.add).then_inc(x1_ok, 1)
                dve.wait_ge(x1_ok, q + 1)

            def split1(q):
                dve.wait_ge(lin1, q + 1)
                dve.wait_ge(r1_ok, q)
                dve.wait_ge(agg1, q)
                dve.scalar_tensor_tensor(out=r0[:, :, :], in0=tiles(bank(LIGHT)), scalar=alpha_eff[:, 0:1],
                                         in1=b1B[:, :].unsqueeze(1).broadcast_to([P, T, D]), op0=ALU.mult, op1=ALU.add
                                         ).then_inc(r0_ok, 1)
                dve.tensor_tensor(g1[:, :, :], tiles(bank(LIGHT)), wide(dis[:, 1, :]), ALU.mult).then_inc(g1_ok, 1)

            def add1(q, b, warm=True):
                dve.wait_ge(agg1, q + 1)
                dve.wait_ge(x2_ok, q)
                dve.tensor_tensor(y1[:, :, :], tiles(bank(LIGHT + 1)), wide(dis[:, 1, :]), ALU.mult).then_inc(y1_ok, 1)
                dve.wait_ge(y1_ok, q + 1)
                dve.wait_ge(r1_ok, q + 1)
                if warm:
                    dve.wait_ge(xn_ok, q - 1)
                    dve.wait_ge(h_ok[2], q - 1)
                dve.tensor_tensor(x2[b][:, :, :], y1[:, :, :], r0[:, :, :], ALU.add).then_inc(x2_ok, 1)

            def split_h2(q):
                dve.wait_ge(hT_ok[2], q + 1)
                dve.wait_ge(gru, 4 * q)
                dve.tensor_copy(h2_hi[:, :], hT[2][:, :]).then_inc(h2_hi_ok, 1)
                dve.wait_ge(h2_hi_ok, q + 1)
                dve.tensor_tensor(h2_lo[:, :], hT[2][:, :], h2_hi[:, :].bitcast(F32), ALU.subtract).then_inc(h2_lo_ok, 1)

            def split_c1(q):
                dve.wait_ge(c1_ok, q + 1)
                dve.wait_ge(conv2, q)
                dve.tensor_copy(c1_hi[:, PAD:PAD + N], c1[:, :]).then_inc(c1_hi_ok, 1)
                dve.wait_ge(c1_hi_ok, q + 1)
                dve.tensor_tensor(c1_lo[:, PAD:PAD + N], c1[:, :], c1_hi[:, PAD:PAD + N].bitcast(F32), ALU.subtract
                                  ).then_inc(c1_lo_ok, 1)

            def split_lr(q):
                dve.wait_ge(dist, 4 * q)
                for n, (src, dst, ok) in enumerate(((left_f, left, left_f_ok), (right_f, right, right_f_ok))):
                    c = slice(32 * (n + 1), 32 * (n + 2))
                    dve.wait_ge(ok, q + 1)
                    dve.tensor_copy(dst[:, :], src[:, :]).then_inc(lr_hi_ok, 1)
                    dve.wait_ge(lr_hi_ok, 2 * q + n + 1)
                    dve.tensor_tensor(dst[c, :], src[c, :], dst[c, :].bitcast(F32), ALU.subtract).then_inc(lr_ok, 1)

            def bias_msg(q):
                dve.wait_ge(msg_lin, q + 1)
                dve.wait_ge(msg_ok, q)
                dve.tensor_tensor(msg_b, tiles(bank(HEAVY)), bmB[:, :].unsqueeze(1).broadcast_to([P, T, D]),
                                  ALU.add).then_inc(msg_b_ok, 1)

            def kernel_adj(q, b, j):
                dve.wait_ge(ker_ok, 4 * q + j + 1)
                dve.wait_ge(nmp, q)
                dve.tensor_tensor(kadj[:, j, :], ker[:, j % 2, :], aT[b][:, j, :], ALU.mult).then_inc(kadj_dve, 1)

            def adjacent(q, b, warm=True):
                if warm:
                    dve.wait_ge(head_sum, 4 * (q - 1))
                    dve.wait_ge(S_ok, 4 * (q - 1))
                dve.wait_ge(aT_act, 2 * (q + 1))
                dve.tensor_scalar(adj_on[b][:, :, :], aT[b][:, :, :], 0.0, None, ALU.is_gt).then_inc(adj_on_ok, 1)

            def split_n(q):
                dve.wait_ge(n_hi_ok, q + 1)
                dve.tensor_tensor(n_lo[:, :], bank(HEAVY + 2), n_hi[:, :].bitcast(F32), ALU.subtract
                                  ).then_inc(n_lo_ok, 1)

            def add_conv(q):
                dve.wait_ge(conv2, q + 1)
                dve.wait_ge(c_lo_ok, q)
                dve.scalar_tensor_tensor(out=u[:, :], in0=bank(HEAVY + 1), scalar=bn_sh[:, 1:2], in1=hT[2][:, :],
                                         op0=ALU.add, op1=ALU.add).then_inc(u_ok, 1)

            def split_conv(q):
                dve.wait_ge(c_hi_ok, q + 1)
                dve.scalar_tensor_tensor(out=c_lo[:, :], in0=u[:, :], scalar=0.0, in1=c_hi[:, :].bitcast(F32),
                                         op0=ALU.max, op1=ALU.subtract).then_inc(c_lo_ok, 1)

            def gates(q, t):
                dst = bank(HEAVY + t % 3)
                dve.wait_ge(rz_ok, 4 * q + t + 1)
                dve.wait_ge(nn_ok, q)
                dve.scalar_tensor_tensor(out=q2[:, t, :], in0=rz[:, t, 0:D], scalar=1.0, in1=dst[:, 3 * D:4 * D],
                                         op0=ALU.add, op1=ALU.mult).then_inc(q1_ok, 1)
                dve.wait_ge(q1_ok, 4 * q + t + 1)
                dve.scalar_tensor_tensor(out=q2[:, t, :], in0=q2[:, t, :], scalar=0.5, in1=dst[:, 0:D],
                                         op0=ALU.mult, op1=ALU.add).then_inc(q2_ok, 1)

            def mix(q):
                dve.wait_ge(nn_ok, q + 1)
                dve.wait_ge(zd_ok, q)
                dve.tensor_tensor(zd[:, :, :], h[2][:, :, :], nn[:, :, :], ALU.subtract).then_inc(hmn_ok, 1)
                dve.wait_ge(hmn_ok, q + 1)
                dve.wait_ge(x3_ok, q)
                dve.scalar_tensor_tensor(out=zd[:, :, :], in0=rz[:, :, D:2 * D], scalar=1.0, in1=zd[:, :, :],
                                         op0=ALU.add, op1=ALU.mult).then_inc(zd_ok, 1)

            def add2(q, b, warm=True):
                dve.wait_ge(zd_ok, q + 1)
                dve.wait_ge(xn_ok, q + 1)
                if warm:
                    dve.wait_ge(xf_ok, q - 1)
                    dve.wait_ge(h_ok[3], q - 1)
                dve.scalar_tensor_tensor(out=x3[b][:, :, :], in0=zd[:, :, :], scalar=0.5, in1=xn[:, :, :],
                                         op0=ALU.mult, op1=ALU.add).then_inc(x3_ok, 1)
                dve.wait_ge(x3_ok, q + 1)

            def split_ei(q):
                dve.wait_ge(eh_hi_ok, q + 1)
                dve.tensor_tensor(eh[32:64, :], bank(LAST)[32:64, :], eh[32:64, :].bitcast(F32), ALU.subtract
                                  ).then_inc(eh_ok, 1)

            def local_max(q):
                dve.wait_ge(hx_ok, 2 * (q + 1))
                dve.wait_ge(cB_ok, q)
                dve.tensor_reduce(mxl[:, :], hx[:, :, D:D + HEADS].rearrange("p t h -> p h t"), AX.X, ALU.max
                                  ).then_inc(mxl_ok, 1)

            def exponents(q):
                c = cB[:, :].unsqueeze(1).broadcast_to([P, T, HEADS])
                dve.wait_ge(cB_ok, q + 1)
                dve.wait_ge(ee_ok, q)
                dve.tensor_tensor(z[:, :, :], hx[:, :, D + HEADS:WX], c, ALU.add)
                dve.tensor_tensor(ex[:, 0, :, :], hx[:, :, D:D + HEADS], c, ALU.subtract).then_inc(z_ok, 1)
                dve.wait_ge(z_ok, q + 1)
                dve.tensor_scalar(ex[:, 1, :, :], ex[:, 0, :, :], 0.2, None, ALU.mult)
                dve.tensor_scalar(ex[:, 2, :, :], z[:, :, :], 0.8, 0.0, ALU.mult, ALU.min)
                dve.tensor_scalar(ex[:, 3, :, :], z[:, :, :], -0.8, 0.0, ALU.mult, ALU.min).then_inc(ex_ok, 1)

            def weigh_e(q):
                dve.wait_ge(ee_ok, q + 1)
                dve.wait_ge(gr_ok, q)
                dve.wait_ge(gp0_ok, q)
                dve.tensor_tensor(gf[:, :, :, 0, 0:HD], hx[:, :, 0:D].rearrange("p t (h d) -> p t h d", d=HD),
                                  ee[:, 0, :, :].unsqueeze(3).broadcast_to([P, T, HEADS, HD]), ALU.mult)
                for s in range(2):
                    ins = dve.tensor_copy(gf[:, :, :, s, HD], ee[:, s, :, :])
                ins.then_inc(gf_dve, 1)

            def rest(q):
                dve.wait_ge(gp0_ok, q + 1)
                dve.wait_ge(gp2_ok, q)
                flat = "p t h s c -> p (t h s c)"
                dve.tensor_tensor(gf[:, :, :, :, :].rearrange(flat), gf[:, :, :, :, :].rearrange(flat),
                                  gp[0][:, :, :, :, :].rearrange(flat), ALU.subtract).then_inc(gr_ok, 1)

            def masks(q, b, i):
                dve.wait_ge(nei_ok, 4 * q + i + 1)
                dve.wait_ge(adj_on_ok, q + 1)
                if i >= 2:
                    dve.wait_ge(head_sum, 4 * q + i - 1)
                else:
                    dve.wait_ge(head_sum, 4 * q)
                for j in range(T):
                    ins = dve.scalar_tensor_tensor(out=S[i % 2][:, j, :], in0=nei[:, i, :],
                                                   scalar=hx[:, j, D + i:D + i + 1], in1=adj_on[b][:, j, :],
                                                   op0=ALU.is_lt, op1=ALU.mult)
                ins.then_inc(S_ok, 1)

            def combine(q):
                e3 = ee[:, 3, :, :].rearrange("p t h -> p h t").unsqueeze(3).broadcast_to([P, HEADS, T, C])
                dve.wait_ge(sf_ok, 4 * (q + 1))
                dve.wait_ge(bf_ok, 2 * (q + 1))
                dve.wait_ge(v2_ok, q)
                dve.tensor_tensor(tot[:, :, :, :], bf[:, :, :, :].rearrange("p t h c -> p h t c"), sf[:, :, :, 1, :],
                                  ALU.subtract).then_inc(v1_ok, 1)
                dve.wait_ge(v1_ok, q + 1)
                dve.wait_ge(tot_ok, q)
                dve.tensor_tensor(tot[:, :, :, :], tot[:, :, :, :], e3, ALU.mult).then_inc(v2_ok, 1)
                dve.wait_ge(v2_ok, q + 1)
                dve.wait_ge(ue_ok, q + 1)
                dve.wait_ge(o1_ok, q)
                dve.wait_ge(den_ok, q)
                dve.tensor_tensor(tot[:, :, :, :], tot[:, :, :, :], ue[:, :, :, :], ALU.add).then_inc(tot_ok, 1)
                dve.wait_ge(tot_ok, q + 1)
                dve.wait_ge(fm_ok, q)
                dve.tensor_scalar(flag[:, :, :], tot[:, :, :, HD], 0.0, None, ALU.is_equal).then_inc(flag_ok, 1)
                dve.wait_ge(flag_ok, q + 1)
                dve.wait_ge(rec_ok, q)
                dve.tensor_tensor(den[:, :, :], tot[:, :, :, HD], flag[:, :, :], ALU.add).then_inc(den_ok, 1)
                dve.wait_ge(den_ok, q + 1)
                dve.reciprocal(rec[:, :, :], den[:, :, :]).then_inc(rec_ok, 1)

            def finish(q):
                dve.wait_ge(rec_ok, q + 1)
                dve.wait_ge(o_ok, q)
                dve.tensor_tensor(o1, tot[:, :, :, 0:HD],
                                  rec[:, :, :].unsqueeze(3).broadcast_to([P, HEADS, T, HD]), ALU.mult
                                  ).then_inc(o1_ok, 1)
                dve.wait_ge(o1_ok, q + 1)
                dve.wait_ge(xf_ok, q + 1)
                dve.wait_ge(stored, 16 * q)
                dve.tensor_tensor(o_sb[:, :, :].rearrange("p t (h d) -> p h t d", d=HD), o1,
                                  fm[:, :, :].rearrange("p t (h d) -> p h t d", d=HD), ALU.add).then_inc(o_ok, 1)

            def light_only(q, b, k):
                degrees(q, b, k)
                take_aT(q, b, 1, False)
                take_aT(q, b, 3, False)
                norm(0, q, x_in[b])
                mask_dis(q)
                shift(0, q)
                bias0(q)
                self0(q)
                add0(q, b)
                norm(1, q, x1)
                shift(1, q)
                split1(q)
                add1(q, b, False)
                dve.wait_ge(x2_ok, q + 1)

            def turn(g, b, k, light, heavy, last):
                a, al, z_ = g + 1, 1 - b, g - 1
                if heavy:
                    dve.wait_ge(x2_ok, g + 1)
                    norm(2, g, x2[b])
                if light:
                    degrees(a, al, k)
                if heavy:
                    shift(2, g)
                if light:
                    norm(0, a, x_in[al])
                    mask_dis(a)
                    take_aT(a, al, 1)
                    shift(0, a)
                if last:
                    norm(3, z_, x3[al])
                if heavy:
                    split_h2(g)
                if last:
                    shift(3, z_)
                if heavy:
                    split_c1(g)
                if light:
                    take_aT(a, al, 3)
                if heavy:
                    split_lr(g)
                    bias_msg(g)
                if last:
                    local_max(z_)
                    split_ei(z_)
                if heavy:
                    kernel_adj(g, b, 0)
                if last:
                    exponents(z_)
                    weigh_e(z_)
                if light:
                    bias0(a)
                if heavy:
                    kernel_adj(g, b, 2)
                    adjacent(g, b, last)
                if last:
                    rest(z_)
                    masks(z_, al, 0)
                    masks(z_, al, 1)
                if light:
                    self0(a)
                    add0(a, al)
                    norm(1, a, x1)
                if last:
                    masks(z_, al, 2)
                if light:
                    shift(1, a)
                if last:
                    masks(z_, al, 3)
                if light:
                    split1(a)
                if heavy:
                    split_n(g)
                if light:
                    add1(a, al)
                if last:
                    combine(z_)
                if heavy:
                    add_conv(g)
                    split_conv(g)
                if last:
                    finish(z_)
                if heavy:
                    for t in range(T):
                        gates(g, t)
                    mix(g)
                    add2(g, b, last)

            run(dve, turn, light_only)


_INS = ['x', 'adj', 'nodemask', 'L0_gnn_W', 'L0_gnn_b', 'L1_gnn_W', 'L1_gnn_b', 'L1_gnn_alpha', 'L2_gnn_w_se',
        'L2_gnn_b_se', 'L2_gnn_conv1_w', 'L2_gnn_bn1_g', 'L2_gnn_bn1_b', 'L2_gnn_bn1_m', 'L2_gnn_bn1_v',
        'L2_gnn_conv2_w', 'L2_gnn_bn2_g', 'L2_gnn_bn2_b', 'L2_gnn_bn2_m', 'L2_gnn_bn2_v', 'L2_gnn_w_msg',
        'L2_gnn_b_msg', 'L2_gnn_w_ih', 'L2_gnn_b_ih', 'L2_gnn_w_hh', 'L2_gnn_b_hh', 'L3_gnn_W', 'L3_gnn_a']


def kernel(**inputs):
    import numpy as _np
    import concourse.bacc as _bacc
    from concourse import mybir as _mybir
    from concourse.bass_utils import run_bass_kernel_spmd as _run

    nc = _bacc.Bacc("TRN2", target_bir_lowering=False, num_devices=1)
    arrays, args = {}, []
    for name in _INS:
        a = _np.ascontiguousarray(inputs[name])
        arrays[f"in_{name}_dram"] = a
        args.append(nc.dram_tensor(f"in_{name}_dram", a.shape, _mybir.dt.from_np(a.dtype), kind="ExternalInput").ap())
    shape = inputs['x'].shape
    args.append(nc.dram_tensor("out_0_dram", shape, _mybir.dt.float32, kind="ExternalOutput").ap())
    build_gnn(nc, *args)
    r = _run(nc, [arrays], core_ids=[0])
    return r.results[0]["out_0_dram"]
```

```python
from contextlib import ExitStack

import concourse.bass as bass
from concourse import mybir

P = 128
F32 = mybir.dt.float32
F32R = mybir.dt.float32r
BF16 = mybir.dt.bfloat16
ALU = mybir.AluOpType
ACT = mybir.ActivationFunctionType
AX = mybir.AxisListType
RMAX = bass.bass_isa.ReduceOp.max


def build_gnn(nc: bass.Bass, x, adj, nodemask, w0, b0, w1, b1, alpha, w_se, b_se, conv1_w, bn1_g, bn1_b,
              bn1_m, bn1_v, conv2_w, bn2_g, bn2_b, bn2_m, bn2_v, w_msg, b_msg, w_ih, b_ih, w_hh, b_hh,
              w3, a3, out):
    GRAPHS, N, D = x.shape
    T = N // P
    TAPS = conv2_w.shape[2]
    PAD = TAPS // 2
    HEADS = a3.shape[0]
    HD = D // HEADS
    SE = w_se.shape[0]
    C = HD + 1
    assert D == P and N == 4 * P and GRAPHS % 2 == 0 and SE == 3
    LN_EPS = 1e-5
    BN_EPS = 1e-5

    ctx = ExitStack()
    with ctx:
        def sb(name, shape, dt=F32):
            return ctx.enter_context(nc.sbuf_tensor(name, shape, dt))

        def sem(name):
            return ctx.enter_context(nc.semaphore(name))

        psum = ctx.enter_context(nc.psum_tensor("psum", [P, 8, N], F32))
        LIGHT, HEAVY, LAST = 0, 2, 5
        GRU_BANK = (HEAVY + 2, HEAVY + 1, HEAVY, HEAVY + 2)
        HEAD_BANK = (LAST + 2, LAST + 1, LAST, LAST + 2)

        def bank(i):
            return psum[:, i, :]

        def tiles(ap, c=P):
            return ap.rearrange("p (t c) -> p t c", c=c)

        ident = sb("ident", [P, P])
        half_pow = sb("half_pow", [P, 8])
        se_nat = sb("se_nat", [SE, P])
        mask_nat = sb("mask_nat", [GRAPHS * T, P])
        mask_sb = sb("mask_sb", [P, GRAPHS * T])
        wT = sb("wT", [P, 3, P])
        NSPLIT = 10 + TAPS
        w_hi = sb("w_hi", [P, NSPLIT, P], F32R)
        w_lo = sb("w_lo", [P, NSPLIT, P], F32R)
        w_se_pad = sb("w_se_pad", [P, P])
        neg_sq = sb("neg_sq", [P, P])
        hot = sb("hot", [P, 3])
        bse = sb("bse", [P, 1])
        left_sc = sb("left_sc", [P, 2])
        right_sc = sb("right_sc", [P, 2])
        bn = sb("bn", [P, 2, 4])
        bn_ve = sb("bn_ve", [P, 2])
        bn_rs = sb("bn_rs", [P, 2])
        bn_sc = sb("bn_sc", [P, 2])
        bn_ms = sb("bn_ms", [P, 2])
        bn_sh = sb("bn_sh", [P, 2])
        b0B = sb("b0B", [P, P])
        b1B = sb("b1B", [P, P])
        bmB = sb("bmB", [P, P])
        alphaB = sb("alphaB", [P, 1])
        alpha_eff = sb("alpha_eff", [P, 1])
        aB = sb("aB", [P, HEADS, 2, HD])
        wx = sb("wx", [P, D + 2 * HEADS])
        w_ei = sb("w_ei", [P, P])
        sel_col = sb("sel_col", [P, HEADS])
        sel = sb("sel", [P, HEADS, P], F32R)
        br = sb("br", [P, N], BF16)
        ones3 = sb("ones3", [P, P], BF16)
        ones = sb("ones", [P, P])

        a_nat = sb("a_nat", [P, T, N])
        x_in = [sb(f"x_in{i}", [P, T, D]) for i in range(2)]
        aT = [sb(f"aT{i}", [P, T, N]) for i in range(2)]
        rowsum = sb("rowsum", [P, T])
        degs = sb("degs", [P, 2, T])
        dis = sb("dis", [P, 2, T])
        dmask = sb("dmask", [P, T])
        t0 = sb("t0", [P, T, D])
        g0 = sb("g0", [P, T, D])
        y0 = sb("y0", [P, T, D])
        x1 = sb("x1", [P, T, D])
        r0 = sb("r0", [P, T, D])
        g1 = sb("g1", [P, T, D])
        y1 = t0
        x2 = [sb(f"x2_{i}", [P, T, D]) for i in range(2)]
        h_light, hT_light = sb("h_light", [P, T, D]), sb("hT_light", [P, N])
        h = [h_light, h_light, sb("h2", [P, T, D]), sb("h3", [P, T, D])]
        hT = [hT_light, hT_light, sb("hT2", [P, N]), sb("hT3", [P, N])]
        ln_st = [sb(f"ln_st{i}", [P, T, 6]) for i in range(4)]
        ln_mv = [sb(f"ln_mv{i}", [P, T, 2]) for i in range(4)]
        ln_ve = [sb(f"ln_ve{i}", [P, T]) for i in range(4)]
        ln_rs = [sb(f"ln_rs{i}", [P, T]) for i in range(4)]
        ln_nm = [sb(f"ln_nm{i}", [P, T]) for i in range(4)]

        h2_hi = sb("h2_hi", [P, N], F32R)
        h2_lo = sb("h2_lo", [P, N], F32R)
        c1 = sb("c1", [P, N])
        c1_hi = sb("c1_hi", [P, N + 2 * PAD], F32R)
        c1_lo = sb("c1_lo", [P, N + 2 * PAD], F32R)
        left_f = sb("left_f", [P, N])
        right_f = sb("right_f", [P, N])
        s_sq = right_f
        left = sb("left", [P, N], F32R)
        right = sb("right", [P, N], F32R)
        msg_b = left_f[:, :].rearrange("p (t d) -> p t d", d=D)
        msg = sb("msg", [P, T, D])
        ker_kadj = sb("ker_kadj", [P, T + 2, N])
        ker, kadj = ker_kadj[:, T:T + 2, :], ker_kadj[:, 0:T, :]
        adj_on = [sb(f"adj_on{i}", [P, T, N], BF16) for i in range(2)]
        n_hi = sb("n_hi", [P, N], F32R)
        n_lo = sb("n_lo", [P, N], F32R)
        u = c1
        c_hi = sb("c_hi", [P, N], F32R)
        c_lo = sb("c_lo", [P, N], F32R)
        rz = sb("rz", [P, T, 2 * D])
        q2 = sb("q2", [P, T, D])
        nn = sb("nn", [P, T, D])
        zd = sb("zd", [P, T, D])
        xn = sb("xn", [P, T, D])
        x3 = [sb(f"x3_{i}", [P, T, D]) for i in range(2)]

        WX = D + 2 * HEADS
        hsum = sb("hsum", [P, 1])
        hsB = sb("hsB", [P, P])
        meanh = sb("meanh", [P, P])
        hx = sb("hx", [P, T, WX])
        eh = sb("eh", [P, N], F32R)
        nei = sb("nei", [P, HEADS, N])
        mxl = sb("mxl", [P, HEADS])
        cB = sb("cB", [P, HEADS])
        z = sb("z", [P, T, HEADS])
        ex = sb("ex", [P, 4, T, HEADS])
        ee = sb("ee", [P, 4, T, HEADS])
        gf = sb("gf", [P, T, HEADS, 2, C])
        gp = [sb(f"gp{i}", [P, T, HEADS, 2, C], BF16) for i in range(3)]
        S = [sb(f"S{i}", [P, T, N], BF16) for i in range(2)]
        bf = sb("bf", [P, T, HEADS, C])
        sf = sb("sf", [P, HEADS, T, 2, C])
        tot = sb("tot", [P, HEADS, T, C])
        ue = sb("ue", [P, HEADS, T, C])
        flag = sb("flag", [P, HEADS, T])
        den = sb("den", [P, HEADS, T])
        rec = sb("rec", [P, HEADS, T])
        fm = sb("fm", [P, T, D])
        o1 = ue[:, :, :, 0:HD]
        o_sb = sb("o_sb", [P, T, D])

        wnat = aT[1][:, :, :].rearrange("p t n -> p (t n)")[:, 0:13 * P].rearrange("p (w i) -> p w i", i=P)
        c2nat = ker_kadj[:, :, :].rearrange("p t n -> p (t n)")[:, 0:P * TAPS]
        br_a, br_b = nei[:, 0, :], nei[:, 1, :]
        wa = nei[:, 2, 0:2 * D].rearrange("p (s h d) -> p s h d", s=2, d=HD)
        br_p = S[0][:, 0:3, :]

        set_loaded = sem("set_loaded")
        set_pool = sem("set_pool")
        set_dve = sem("set_dve")
        set_pe = sem("set_pe")
        a_loaded = sem("a_loaded")
        x_loaded = [sem(f"x_loaded{i}") for i in range(2)]
        stored = sem("stored")
        ln_st_ok = [sem(f"ln_st_ok{i}") for i in range(4)]
        ln_mv_ok = [sem(f"ln_mv_ok{i}") for i in range(4)]
        ln_ve_ok = [sem(f"ln_ve_ok{i}") for i in range(4)]
        ln_rs_ok = [sem(f"ln_rs_ok{i}") for i in range(4)]
        ln_nm_ok = [sem(f"ln_nm_ok{i}") for i in range(4)]
        h_ok = [sem(f"h_ok{i}") for i in range(4)]
        turned = [sem(f"turned{i}") for i in range(4)]
        hT_ok = [sem(f"hT_ok{i}") for i in range(4)]
        a_turned = sem("a_turned")
        aT_act = sem("aT_act")
        aT_dve = sem("aT_dve")
        rowsum_ok = sem("rowsum_ok")
        degs_ok = sem("degs_ok")
        dis_ok = sem("dis_ok")
        dmask_ok = sem("dmask_ok")
        lin0 = sem("lin0")
        t0_ok = sem("t0_ok")
        g0_ok = sem("g0_ok")
        agg0 = sem("agg0")
        y0_ok = sem("y0_ok")
        y0m_ok = sem("y0m_ok")
        x1_ok = sem("x1_ok")
        lin1 = sem("lin1")
        r0_ok = sem("r0_ok")
        g1_ok = sem("g1_ok")
        r1_ok = sem("r1_ok")
        agg1 = sem("agg1")
        y1_ok = sem("y1_ok")
        x2_ok = sem("x2_ok")
        h2_hi_ok = sem("h2_hi_ok")
        h2_lo_ok = sem("h2_lo_ok")
        conv1 = sem("conv1")
        c1_ok = sem("c1_ok")
        c1_hi_ok = sem("c1_hi_ok")
        c1_lo_ok = sem("c1_lo_ok")
        s_lin = sem("s_lin")
        s_sq_ok = sem("s_sq_ok")
        s_all = sem("s_all")
        left_f_ok = sem("left_f_ok")
        right_f_ok = sem("right_f_ok")
        lr_hi_ok = sem("lr_hi_ok")
        lr_ok = sem("lr_ok")
        msg_lin = sem("msg_lin")
        msg_b_ok = sem("msg_b_ok")
        msg_ok = sem("msg_ok")
        dist = sem("dist")
        ker_ok = sem("ker_ok")
        kadj_dve = sem("kadj_dve")
        kadj_pool = sem("kadj_pool")
        adj_on_ok = sem("adj_on_ok")
        nmp = sem("nmp")
        n_hi_ok = sem("n_hi_ok")
        n_lo_ok = sem("n_lo_ok")
        conv2 = sem("conv2")
        u_ok = sem("u_ok")
        c_hi_ok = sem("c_hi_ok")
        c_lo_ok = sem("c_lo_ok")
        gru = sem("gru")
        rz_ok = sem("rz_ok")
        q1_ok = sem("q1_ok")
        q2_ok = sem("q2_ok")
        nn_ok = sem("nn_ok")
        hmn_ok = sem("hmn_ok")
        zd_ok = sem("zd_ok")
        xn_ok = sem("xn_ok")
        x3_ok = sem("x3_ok")
        hx_lin = sem("hx_lin")
        hx_ok = sem("hx_ok")
        hsB_ok = sem("hsB_ok")
        mean_lin = sem("mean_lin")
        meanh_ok = sem("meanh_ok")
        ei_lin = sem("ei_lin")
        eh_hi_ok = sem("eh_hi_ok")
        eh_ok = sem("eh_ok")
        ei_rows = sem("ei_rows")
        nei_ok = sem("nei_ok")
        mxl_ok = sem("mxl_ok")
        cB_ok = sem("cB_ok")
        z_ok = sem("z_ok")
        ex_ok = sem("ex_ok")
        ee_ok = sem("ee_ok")
        gf_dve = sem("gf_dve")
        gf_pool = sem("gf_pool")
        gp0_ok = sem("gp0_ok")
        gr_ok = sem("gr_ok")
        gp1_ok = sem("gp1_ok")
        gp2_ok = sem("gp2_ok")
        all_sum = sem("all_sum")
        bf_ok = sem("bf_ok")
        S_ok = sem("S_ok")
        head_sum = sem("head_sum")
        sf_ok = sem("sf_ok")
        v1_ok = sem("v1_ok")
        v2_ok = sem("v2_ok")
        ue_ok = sem("ue_ok")
        tot_ok = sem("tot_ok")
        flag_ok = sem("flag_ok")
        den_ok = sem("den_ok")
        rec_ok = sem("rec_ok")
        fm_ok = sem("fm_ok")
        xf_ok = sem("xf_ok")
        o1_ok = sem("o1_ok")
        o_ok = sem("o_ok")

        FIRST, LOOP, LOOP_END, END = -2, 4, GRAPHS - 2, GRAPHS + 2

        x_v = x.rearrange("g (t p) d -> g p t d", p=P)
        adj_v = adj.rearrange("g (t p) m -> g p t m", p=P)
        out_v = out.rearrange("g (t p) d -> g p t d", p=P)

        def wide(col):
            return col.unsqueeze(2).broadcast_to([P, T, D])

        def past(q):
            return not isinstance(q, int) or q >= 1

        def there(q):
            return not isinstance(q, int) or 0 <= q < GRAPHS

        def run(eng, turn):
            for g in range(FIRST, LOOP):
                turn(g, g // 2, g % 2)
            with eng.Fori(0, (LOOP_END - LOOP) // 2, 1) as k:
                turn(2 * k + LOOP, k + LOOP // 2, 0)
                turn(2 * k + LOOP + 1, k + LOOP // 2, 1)
            for g in range(LOOP_END, END):
                turn(g, g // 2, g % 2)

        block = ctx.enter_context(nc.Block())

        @block.sync
        def _(sp):
            def fetch(q, b):
                sp.dma_start(a_nat[:, :, :], adj_v[q]).then_inc(a_loaded, 16)
                sp.dma_start(x_in[b][:, :, :], x_v[q]).then_inc(x_loaded[b], 16)

            fetch(0, 0)


            def load(dst, src):
                sp.dma_start(dst, src).then_inc(set_loaded, 16)

            load(wnat[:, 0, :], w0)
            load(wnat[:, 1, :], w1)
            load(wnat[:, 2, :], w_msg)
            load(wnat[:, 3, :], conv1_w.rearrange("o i k -> o (i k)"))
            load(wnat[:, 4:10, :], w_ih.rearrange("(r o) (c i) -> o r c i", o=P, c=2))
            load(wnat[:, 10:13, :], w_hh.rearrange("(r o) i -> o r i", o=P))
            load(c2nat, conv2_w.rearrange("o i k -> o (i k)"))
            load(se_nat[:, :], w_se)
            load(mask_nat[:, :], nodemask.rearrange("g (t p) -> (g t) p", p=P))
            load(wx[:, 0:D], w3)
            for i, v in enumerate((bn1_g, bn1_b, bn1_m, bn1_v)):
                load(bn[:, 0, i:i + 1], v.unsqueeze(1))
            for i, v in enumerate((bn2_g, bn2_b, bn2_m, bn2_v)):
                load(bn[:, 1, i:i + 1], v.unsqueeze(1))
            load(b0B[:, :], b0.partition_broadcast(P))
            load(b1B[:, :], b1.partition_broadcast(P))
            load(bmB[:, :], b_msg.partition_broadcast(P))
            load(alphaB[:, :], alpha.partition_broadcast(P))
            load(aB[:, :, :, :], a3.rearrange("h (s d) -> h s d", s=2).partition_broadcast(P))
            sp.wait_ge(set_pool, 1)
            for q in range(3):
                load(bse[32 * q:32 * q + SE, :], b_se.unsqueeze(1))
                row = slice(32 * q, 32 * q + 1)
                load(br_a[row, 0:D], b_ih[2 * D:3 * D].unsqueeze(0))
                load(br_a[row, D:3 * D], b_ih[0:2 * D].unsqueeze(0))
                load(br_b[row, D:4 * D], b_hh.unsqueeze(0))
            def value(v):
                return v if isinstance(v, int) else sp.snap(v)

            def next_graph(q, b):
                turned4, read = value(4 * q), value(q)
                sp.wait_ge(set_pool, 1)
                sp.wait_ge(a_turned, turned4)
                sp.wait_ge(rowsum_ok, read)
                fetch(q, b)

            def store(q):
                done = value(q + 1)
                sp.wait_ge(set_pool, 1)
                sp.wait_ge(o_ok, done)
                sp.dma_start(out_v[q], o_sb[:, :, :]).then_inc(stored, 16)

            def turn(g, b):
                if there(g - 2):
                    store(g - 2)
                if there(g + 2) and past(g + 2):
                    next_graph(g + 2, b)

            for g in range(FIRST, LOOP):
                turn(g, g % 2)
            with sp.Fori(LOOP, LOOP_END - 1, 2) as g:
                turn(g, 0)
                turn(g + 1, 1)
            for g in range(LOOP_END, END):
                turn(g, g % 2)
            sp.wait_ge(stored, 16 * GRAPHS)

        LOADS = 10 + 8 + 5 + 12

        @block.gpsimd
        def _(pool):
            pool.memset(bse[:, :], 0.0)
            pool.memset(br_a, 0.0)
            pool.memset(br_b, 0.0).then_inc(set_pool, 1)
            pool.memset(ident[:, :], 0.0).then_inc(set_pool, 1)
            pool.wait_ge(set_pool, 2)
            pool.affine_select(out=ident[:, :], in_=ident[:, :], compare_op=ALU.not_equal, fill=1.0, base=0,
                               pattern=[[-1, P]], channel_multiplier=1).then_inc(set_pool, 1)
            pool.memset(half_pow[:, :], -0.5).then_inc(set_pool, 1)
            pool.memset(w_se_pad[:, :], 0.0)
            pool.memset(w_ei[:, :], 0.0)
            pool.memset(ones[:, :], 1.0)
            pool.memset(br[:, :], 0.0)
            pool.memset(ones3[:, :], 0.0)
            pool.memset(neg_sq[:, :], 0.0)
            for t in (c1_hi, c1_lo):
                pool.memset(t[:, 0:PAD].bitcast(F32), 0.0)
                ins = pool.memset(t[:, PAD + N:2 * PAD + N].bitcast(F32), 0.0)
            ins.then_inc(set_pool, 1)
            pool.wait_ge(set_pool, 5)
            for q in range(3):
                pool.memset(ones3[32 * q:32 * q + 1, :], 1.0)
                ins = pool.memset(neg_sq[0:SE, 32 * q + 3:32 * q + 5], -1.0)
            ins.then_inc(set_pool, 1)
            pool.wait_ge(set_dve, 1)
            pool.tensor_tensor(bn_rs[:, :], bn_ve[:, :], half_pow[:, 0:2], ALU.pow).then_inc(set_pool, 1)

            def norm(i, q):
                pool.wait_ge(ln_ve_ok[i], q + 1)
                pool.wait_ge(ln_nm_ok[i], q)
                pool.wait_ge(h_ok[i], q)
                pool.tensor_tensor(ln_rs[i][:, :], ln_ve[i][:, :], half_pow[:, 0:T], ALU.pow).then_inc(ln_rs_ok[i], 1)

            def dis_pow(q):
                pool.wait_ge(degs_ok, 2 * (q + 1))
                pool.wait_ge(dmask_ok, q)
                pool.wait_ge(y1_ok, q)
                pool.tensor_tensor(dis[:, :, :].rearrange("p a t -> p (a t)"),
                                   degs[:, :, :].rearrange("p a t -> p (a t)"), half_pow[:, :], ALU.pow
                                   ).then_inc(dis_ok, 1)

            def scale_g0(q):
                pool.wait_ge(t0_ok, q + 1)
                pool.wait_ge(dis_ok, q + 1)
                pool.wait_ge(agg0, q)
                pool.wait_ge(y0_ok, q)
                pool.tensor_tensor(g0[:, :, :], t0[:, :, :], wide(dis[:, 0, :]), ALU.mult).then_inc(g0_ok, 1)

            def scale_y0(q):
                pool.wait_ge(y0_ok, q + 1)
                pool.wait_ge(dmask_ok, q + 1)
                pool.wait_ge(x1_ok, q)
                pool.tensor_tensor(y0[:, :, :], y0[:, :, :], wide(dmask[:, :]), ALU.mult).then_inc(y0m_ok, 1)

            def residual1(q):
                pool.wait_ge(r0_ok, q + 1)
                pool.wait_ge(x1_ok, q + 1)
                pool.wait_ge(x2_ok, q)
                pool.tensor_tensor(r0[:, :, :], r0[:, :, :], x1[:, :, :], ALU.add).then_inc(r1_ok, 1)

            def kernel_adj(q, b, j):
                pool.wait_ge(ker_ok, 4 * q + j + 1)
                pool.wait_ge(aT_dve, 2 * (q + 1))
                pool.wait_ge(nmp, q)
                pool.tensor_tensor(kadj[:, j, :], ker[:, j % 2, :], aT[b][:, j, :], ALU.mult).then_inc(kadj_pool, 1)

            def residual2(q, b):
                pool.wait_ge(nn_ok, q + 1)
                pool.wait_ge(x2_ok, q + 1)
                pool.wait_ge(x3_ok, q)
                pool.tensor_tensor(xn[:, :, :], nn[:, :, :], x2[b][:, :, :], ALU.add).then_inc(xn_ok, 1)

            def mean_col(q):
                pool.wait_ge(set_pool, 1)
                pool.wait_ge(hT_ok[3], q + 1)
                pool.wait_ge(mean_lin, q)
                pool.tensor_scalar(hsB[:, :], ones[:, :], hsum[:, 0:1], 1.0 / N, ALU.mult, ALU.mult).then_inc(hsB_ok, 1)

            def guard(q):
                pool.wait_ge(set_pool, 1)
                pool.wait_ge(mxl_ok, q + 1)
                pool.wait_ge(ex_ok, q)
                pool.partition_all_reduce(cB[:, :], mxl[:, :], P, RMAX).then_inc(cB_ok, 1)

            def weigh_f(q):
                pool.wait_ge(ee_ok, q + 1)
                pool.wait_ge(gr_ok, q)
                pool.wait_ge(gp0_ok, q)
                pool.tensor_tensor(gf[:, :, :, 1, 0:HD], hx[:, :, 0:D].rearrange("p t (h d) -> p t h d", d=HD),
                                   ee[:, 1, :, :].unsqueeze(3).broadcast_to([P, T, HEADS, HD]), ALU.mult
                                   ).then_inc(gf_pool, 1)

            def third_part(q):
                pool.wait_ge(gp1_ok, q + 1)
                pool.wait_ge(head_sum, 4 * q)
                flat = "p t h s c -> p (t h s c)"
                pool.tensor_tensor(gp[2][:, :, :, :, :].rearrange(flat), gf[:, :, :, :, :].rearrange(flat),
                                   gp[1][:, :, :, :, :].rearrange(flat), ALU.subtract).then_inc(gp2_ok, 1)

            def fallback(q, b):
                pool.wait_ge(flag_ok, q + 1)
                pool.wait_ge(meanh_ok, q + 1)
                pool.wait_ge(xf_ok, q)
                pool.tensor_tensor(fm[:, :, :].rearrange("p t (h d) -> p h t d", d=HD),
                                   flag[:, :, :].unsqueeze(3).broadcast_to([P, HEADS, T, HD]),
                                   meanh[:, :].rearrange("p (h d) -> p h d", d=HD).unsqueeze(2).broadcast_to([P, HEADS, T, HD]),
                                   ALU.mult).then_inc(fm_ok, 1)
                pool.wait_ge(fm_ok, q + 1)
                pool.wait_ge(o_ok, q)
                pool.tensor_tensor(fm[:, :, :], fm[:, :, :], x3[b][:, :, :], ALU.add).then_inc(xf_ok, 1)

            def weigh_e(q):
                pool.wait_ge(sf_ok, 4 * (q + 1))
                pool.wait_ge(ee_ok, q + 1)
                pool.wait_ge(o_ok, q)
                pool.tensor_tensor(ue[:, :, :, :], sf[:, :, :, 0, :],
                                   ee[:, 2, :, :].rearrange("p t h -> p h t").unsqueeze(3).broadcast_to([P, HEADS, T, C]),
                                   ALU.mult).then_inc(ue_ok, 1)

            def light_a(q):
                dis_pow(q)
                norm(0, q)

            def turn(g, half, b):
                if there(g):
                    norm(2, g)
                if there(g - 1):
                    residual2(g - 1, 1 - b)
                if there(g + 1):
                    dis_pow(g + 1)
                if there(g - 1):
                    norm(3, g - 1)
                if there(g - 2):
                    weigh_e(g - 2)
                if there(g - 1):
                    mean_col(g - 1)
                if there(g + 1):
                    scale_g0(g + 1)
                if there(g - 2):
                    fallback(g - 2, b)
                if there(g - 1):
                    guard(g - 1)
                    weigh_f(g - 1)
                if there(g + 1):
                    scale_y0(g + 1)
                    norm(1, g + 1)
                if there(g - 1):
                    third_part(g - 1)
                if there(g):
                    kernel_adj(g, b, 1)
                    kernel_adj(g, b, 3)
                if there(g + 1):
                    residual1(g + 1)
                if there(g + 2):
                    norm(0, g + 2)

            run(pool, turn)

        @block.scalar
        def _(act):
            def norm(i, q, src):
                act.wait_ge(ln_nm_ok[i], q + 1)
                act.wait_ge(ln_rs_ok[i], q + 1)
                act.wait_ge(turned[i], q)
                if i == 2:
                    act.wait_ge(hmn_ok, q)
                for t in range(T):
                    ins = act.activation(h[i][:, t, :], src[:, t, :], ACT.Relu, bias=ln_nm[i][:, t:t + 1],
                                         scale=ln_rs[i][:, t:t + 1])
                ins.then_inc(h_ok[i], 1)

            def take_aT(q, b, j):
                act.wait_ge(a_turned, 4 * q + j + 1)
                if past(q - 1):
                    act.wait_ge(adj_on_ok, q - 1)
                    act.wait_ge(kadj_dve, 2 * (q - 1))
                    act.wait_ge(kadj_pool, 2 * (q - 1))
                act.activation(aT[b][:, j, :], bank(LIGHT + j % 2), ACT.Copy).then_inc(aT_act, 1)

            def take_hT(i, q, at, used):
                act.wait_ge(turned[i], q + 1)
                act.wait_ge(used, q)
                if i == 2:
                    act.wait_ge(u_ok, q)
                    act.wait_ge(h2_lo_ok, q)
                    act.wait_ge(s_lin, q)
                if i == 3:
                    act.wait_ge(hsB_ok, q)
                    act.activation(hT[i][:, :], bank(at), ACT.Copy, accum_out=hsum[:, 0:1]).then_inc(hT_ok[i], 1)
                else:
                    act.activation(hT[i][:, :], bank(at), ACT.Copy).then_inc(hT_ok[i], 1)

            def take_c1(q):
                act.wait_ge(conv1, q + 1)
                act.wait_ge(c_lo_ok, q)
                act.activation(c1[:, :], bank(HEAVY + 2), ACT.Relu, bias=bn_sh[:, 0:1]).then_inc(c1_ok, 1)

            def square_s(q):
                act.wait_ge(s_lin, q + 1)
                act.wait_ge(lr_ok, 2 * q)
                act.activation(s_sq[:, :], bank(HEAVY), ACT.Square, bias=bse[:, 0:1]).then_inc(s_sq_ok, 1)

            def sides(q):
                act.wait_ge(s_all, q + 1)
                act.wait_ge(lr_ok, 2 * q)
                act.wait_ge(msg_ok, q)
                act.activation(left_f[:, :], bank(HEAVY), ACT.Identity, bias=left_sc[:, 1:2],
                               scale=left_sc[:, 0:1]).then_inc(left_f_ok, 1)
                act.activation(right_f[:, :], bank(HEAVY), ACT.Identity, bias=right_sc[:, 1:2],
                               scale=right_sc[:, 0:1]).then_inc(right_f_ok, 1)

            def relu_msg(q):
                act.wait_ge(msg_b_ok, q + 1)
                act.wait_ge(nmp, q)
                act.activation(msg[:, :, :], msg_b, ACT.Relu).then_inc(msg_ok, 1)

            def exps(q, j):
                act.wait_ge(dist, 4 * q + j + 1)
                act.wait_ge(kadj_pool if j % 2 else kadj_dve, 2 * q + j // 2)
                act.activation(ker[:, j % 2, :], bank(HEAVY + 2 * (j % 2)), ACT.Exp).then_inc(ker_ok, 1)

            def take_n(q):
                act.wait_ge(nmp, q + 1)
                act.wait_ge(gru, 4 * q)
                act.activation(n_hi[:, :], bank(HEAVY), ACT.Copy).then_inc(n_hi_ok, 1)

            def relu_conv(q):
                act.wait_ge(u_ok, q + 1)
                act.wait_ge(gru, 4 * q)
                act.activation(c_hi[:, :], u[:, :], ACT.Relu).then_inc(c_hi_ok, 1)

            def gates(q, t):
                act.wait_ge(gru, 4 * q + t + 1)
                act.wait_ge(zd_ok, q)
                act.activation(rz[:, t, :], bank(GRU_BANK[t])[:, D:3 * D], ACT.Tanh, scale=0.5).then_inc(rz_ok, 1)

            def new_gate(q):
                act.wait_ge(q2_ok, 4 * (q + 1))
                act.wait_ge(xn_ok, q)
                act.activation(nn[:, :, :], q2[:, :, :], ACT.Tanh).then_inc(nn_ok, 1)

            def take_hx(q, i):
                act.wait_ge(hx_lin, 2 * q + i + 1)
                act.wait_ge(S_ok, 4 * q)
                act.wait_ge(gf_dve, q)
                act.wait_ge(gf_pool, q)
                act.activation(hx[:, 2 * i:2 * i + 2, :], tiles(bank(LAST + 1 + i)[:, 0:2 * WX], WX), ACT.Copy
                               ).then_inc(hx_ok, 1)

            def take_mean(q):
                act.wait_ge(mean_lin, q + 1)
                act.wait_ge(fm_ok, q)
                act.activation(meanh[:, :], bank(LAST)[:, 0:P], ACT.Copy).then_inc(meanh_ok, 1)

            def take_ei(q):
                act.wait_ge(ei_lin, q + 1)
                act.wait_ge(ei_rows, 4 * q)
                act.activation(eh[:, :], bank(LAST + 1), ACT.Copy).then_inc(eh_hi_ok, 1)

            def take_rows(q, i):
                act.wait_ge(ei_rows, 4 * q + i + 1)
                act.wait_ge(S_ok, 4 * q)
                act.activation(nei[:, i, :], bank(LAST + 2 - 2 * (i % 2)), ACT.Copy).then_inc(nei_ok, 1)

            def exp_e(q):
                act.wait_ge(ex_ok, q + 1)
                act.wait_ge(gf_dve, q)
                act.wait_ge(v2_ok, q)
                act.wait_ge(ue_ok, q)
                act.activation(ee[:, :, :, :].rearrange("p k t h -> p (k t h)"),
                               ex[:, :, :, :].rearrange("p k t h -> p (k t h)"), ACT.Exp).then_inc(ee_ok, 1)

            flat = "p t h s c -> p (t h s c)"

            def first_part(q):
                act.wait_ge(gf_dve, q + 1)
                act.wait_ge(gf_pool, q + 1)
                act.wait_ge(head_sum, 4 * q)
                act.activation(gp[0][:, :, :, :, :].rearrange(flat), gf[:, :, :, :, :].rearrange(flat), ACT.Copy
                               ).then_inc(gp0_ok, 1)

            def second_part(q):
                act.wait_ge(gr_ok, q + 1)
                act.activation(gp[1][:, :, :, :, :].rearrange(flat), gf[:, :, :, :, :].rearrange(flat), ACT.Copy
                               ).then_inc(gp1_ok, 1)

            def take_all(q, i):
                act.wait_ge(all_sum, 2 * q + i + 1)
                act.wait_ge(v1_ok, q)
                act.activation(bf[:, 2 * i:2 * i + 2, :, :].rearrange("p t h c -> p (t h c)"),
                               bank(LAST + 1 - i)[:, 0:2 * HEADS * C], ACT.Copy).then_inc(bf_ok, 1)

            def take_head(q, i):
                act.wait_ge(head_sum, 4 * q + i + 1)
                act.wait_ge(v1_ok, q)
                act.wait_ge(ue_ok, q)
                act.activation(sf[:, i, :, :, :].rearrange("p t s c -> p (t s c)"),
                               bank(HEAD_BANK[i])[:, 0:T * 2 * C], ACT.Copy).then_inc(sf_ok, 1)

            act.wait_ge(set_dve, 9)

            def turn(g, half, b):
                if there(g):
                    square_s(g)
                    take_c1(g)
                if there(g - 1):
                    take_hT(3, g - 1, LAST, ei_lin)
                if there(g):
                    sides(g)
                if there(g - 1):
                    take_hx(g - 1, 0)
                    take_hx(g - 1, 1)
                    take_ei(g - 1)
                    exp_e(g - 1)
                if there(g):
                    exps(g, 0)
                if there(g - 1):
                    take_mean(g - 1)
                if there(g):
                    exps(g, 1)
                if there(g - 1):
                    first_part(g - 1)
                    second_part(g - 1)
                if there(g):
                    exps(g, 2)
                if there(g - 1):
                    take_rows(g - 1, 0)
                if there(g):
                    relu_msg(g)
                if there(g - 1):
                    take_rows(g - 1, 1)
                    take_rows(g - 1, 2)
                if there(g + 1):
                    norm(1, g + 1, x1)
                if there(g):
                    exps(g, 3)
                if there(g - 1):
                    take_rows(g - 1, 3)
                    take_all(g - 1, 0)
                if there(g + 1):
                    take_hT(1, g + 1, LIGHT + 1, lin1)
                if there(g):
                    take_n(g)
                    relu_conv(g)
                    gates(g, 0)
                    gates(g, 1)
                    gates(g, 2)
                    gates(g, 3)
                if there(g - 1):
                    take_head(g - 1, 0)
                if there(g + 2):
                    take_aT(g + 2, b, 0)
                if there(g - 1):
                    take_all(g - 1, 1)
                if there(g):
                    new_gate(g)
                if there(g + 2):
                    take_aT(g + 2, b, 2)
                if there(g + 1):
                    norm(2, g + 1, x2[1 - b])
                if there(g + 2):
                    norm(0, g + 2, x_in[b])
                if there(g + 1):
                    take_hT(2, g + 1, HEAVY + 1, msg_lin)
                if there(g - 1):
                    take_head(g - 1, 1)
                    take_head(g - 1, 2)
                    take_head(g - 1, 3)
                if there(g + 2):
                    take_hT(0, g + 2, LIGHT, lin0)
                if there(g):
                    norm(3, g, x3[b])

            run(act, turn)

        @block.tensor
        def _(pe):
            pe.wait_ge(set_dve, 3)

            def turn_weight(i, src, n=P):
                return pe.transpose(bank(i // 4)[:, (i % 4) * P:(i % 4) * P + n], src, ident[0:n, 0:n])

            for i in range(3):
                turn_weight(i, wnat[:, i, :])
            turn_weight(3, se_nat[:, :], SE)
            turn_weight(4, mask_nat[:, :], GRAPHS * T)
            turn_weight(5, wnat[:, 3, :])
            for n, r in enumerate((2, 0, 1)):
                turn_weight(6 + n, wnat[:, 4 + 2 * r, :])
                turn_weight(9 + n, wnat[:, 5 + 2 * r, :])
            for r in range(3):
                turn_weight(12 + r, wnat[:, 10 + r, :])
            for k in range(TAPS):
                ins = turn_weight(15 + k, c2nat.rearrange("p (i k) -> p i k", k=TAPS)[:, :, k])
            ins.then_inc(set_pe, 1)
            pe.wait_ge(set_dve, 9)

            def split_mm(dst, wh, wl, mh, ml, start, stop):
                pe.matmul(dst, wh, mh, start=start, stop=False, skip_group_check=True)
                pe.matmul(dst, wh, ml, start=False, stop=False, skip_group_check=True)
                return pe.matmul(dst, wl, mh, start=False, stop=stop, skip_group_check=True)

            def turn_a(q, j):
                if j == 0:
                    pe.wait_ge(a_loaded, 16 * (q + 1))
                    pe.wait_ge(g1_ok, q)
                if j == 1:
                    pe.wait_ge(y1_ok, q)
                if j == 2:
                    pe.wait_ge(aT_act, 2 * q + 1)
                if j == 3:
                    pe.wait_ge(aT_dve, 2 * q + 1)
                for t in range(T):
                    ins = pe.transpose(bank(LIGHT + j % 2)[:, t * P:(t + 1) * P], a_nat[:, t, j * P:(j + 1) * P],
                                       ident[:, :])
                ins.then_inc(a_turned, 1)

            def turn_h(i, q, at):
                if i == 2 and past(q):
                    pe.wait_ge(q2_ok, 4 * q - 2)
                if i == 3 and past(q):
                    pe.wait_ge(sf_ok, 4 * q - 1)
                pe.wait_ge(h_ok[i], q + 1)
                for t in range(T):
                    ins = pe.transpose(bank(at)[:, t * P:(t + 1) * P], h[i][:, t, :], ident[:, :])
                ins.then_inc(turned[i], 1)

            def linear(at, i, w, done, q):
                if i == 2:
                    pe.wait_ge(c1_ok, q + 1)
                pe.wait_ge(hT_ok[i], q + 1)
                for t in range(T):
                    ins = pe.matmul(bank(at)[:, t * P:(t + 1) * P], hT[i][:, t * P:(t + 1) * P], w, start=True,
                                    stop=True, skip_group_check=True)
                ins.then_inc(done, 1)

            def aggregate(at, b, g, done):
                for t in range(T):
                    for j in range(T):
                        ins = pe.matmul(bank(at)[:, t * P:(t + 1) * P], aT[b][:, j, t * P:(t + 1) * P], g[:, j, :],
                                        start=(j == 0), stop=(j == T - 1), skip_group_check=True)
                ins.then_inc(done, 1)

            def light1(q, b):
                pe.wait_ge(aT_act, 2 * (q + 1))
                turn_h(0, q, LIGHT)

            def light2(q, b):
                pe.wait_ge(aT_dve, 2 * (q + 1))
                linear(LIGHT + 1, 0, wT[:, 0, :], lin0, q)

            def light3(q, b):
                pe.wait_ge(g0_ok, q + 1)
                aggregate(LIGHT, b, g0, agg0)

            def light4(q, b):
                pe.wait_ge(t0_ok, q + 1)
                turn_h(1, q, LIGHT + 1)

            def light5(q, b):
                pe.wait_ge(y0_ok, q + 1)
                linear(LIGHT, 1, wT[:, 1, :], lin1, q)

            def light6(q, b):
                pe.wait_ge(g1_ok, q + 1)
                aggregate(LIGHT + 1, b, g1, agg1)

            B0, B1, B2 = HEAVY, HEAVY + 1, HEAVY + 2

            def do_conv1(q):
                pe.wait_ge(q2_ok, 4 * q)
                pe.wait_ge(h2_lo_ok, q + 1)
                split_mm(bank(B2), w_hi[:, 0, :], w_lo[:, 0, :], h2_hi[:, :], h2_lo[:, :], True, True
                         ).then_inc(conv1, 1)

            def do_s(q):
                if past(q):
                    pe.wait_ge(q2_ok, 4 * q - 1)
                pe.wait_ge(hT_ok[2], q + 1)
                pe.matmul(bank(B0), w_se_pad[:, :], hT[2][:, :], start=True, stop=False, skip_group_check=True
                          ).then_inc(s_lin, 1)

            def do_sq(q):
                pe.wait_ge(s_sq_ok, q + 1)
                pe.matmul(bank(B0), neg_sq[:, :], s_sq[:, :], start=False, stop=True, skip_group_check=True
                          ).then_inc(s_all, 1)

            def do_dist(q, j):
                if j == 0:
                    pe.wait_ge(lr_ok, 2 * (q + 1))
                if j == 1:
                    pe.wait_ge(msg_b_ok, q + 1)
                if j >= 2:
                    pe.wait_ge(ker_ok, 4 * q + j - 1)
                pe.matmul(bank(HEAVY + 2 * (j % 2)), left[:, j * P:(j + 1) * P], right[:, :], start=True,
                              stop=True, skip_group_check=True).then_inc(dist, 1)

            def do_conv2(q, ks):
                if 0 in ks:
                    pe.wait_ge(hT_ok[2], q + 1)
                    pe.wait_ge(c1_lo_ok, q + 1)
                for k in ks:
                    ins = split_mm(bank(B1), w_hi[:, 10 + k, :], w_lo[:, 10 + k, :], c1_hi[:, k:k + N],
                                   c1_lo[:, k:k + N], k == 0, k == TAPS - 1)
                    if k == TAPS - 1:
                        ins.then_inc(conv2, 1)

            def do_nmp(q):
                pe.wait_ge(msg_ok, q + 1)
                pe.wait_ge(kadj_dve, 2 * (q + 1))
                pe.wait_ge(kadj_pool, 2 * (q + 1))
                pe.wait_ge(ker_ok, 4 * (q + 1))
                for j in range(T):
                    ins = pe.matmul(bank(B0), msg[:, j, :], kadj[:, j, :], start=(j == 0), stop=(j == T - 1),
                                    skip_group_check=True)
                ins.then_inc(nmp, 1)

            def gru_part(q, t, at, hi, lo, i, last=False):
                dst = bank(GRU_BANK[t])[:, at:at + 3 * D]
                c = slice(t * P, (t + 1) * P)
                wh = w_hi[:, i:i + 3, :].rearrange("p a o -> p (a o)")
                wl = w_lo[:, i:i + 3, :].rearrange("p a o -> p (a o)")
                pe.matmul(dst, hi[:, c], wh, start=False, stop=False, skip_group_check=True)
                pe.matmul(dst, hi[:, c], wl, start=False, stop=False, skip_group_check=True)
                return pe.matmul(dst, lo[:, c], wh, start=False, stop=last, skip_group_check=True)

            def do_gru_h(q, t):
                if t == 0:
                    pe.wait_ge(ker_ok, 4 * (q + 1))
                if t == 1:
                    pe.wait_ge(u_ok, q + 1)
                if t == 2:
                    pe.wait_ge(n_lo_ok, q + 1)
                if t == 3:
                    pe.wait_ge(q2_ok, 4 * q + 1)
                pe.matmul(bank(GRU_BANK[t]), ones3[:, :], br[:, :], start=True, stop=False, skip_group_check=True)
                gru_part(q, t, D, h2_hi, h2_lo, 7)

            def do_gru_n(q, t):
                pe.wait_ge(n_lo_ok, q + 1)
                gru_part(q, t, 0, n_hi, n_lo, 4)

            def do_gru_c(q, t):
                pe.wait_ge(c_lo_ok, q + 1)
                gru_part(q, t, 0, c_hi, c_lo, 1, True).then_inc(gru, 1)

            C0, C1, C2 = LAST, LAST + 1, LAST + 2

            def do_hx(q, i):
                pe.wait_ge(hT_ok[3], q + 1)
                if i == 1:
                    pe.wait_ge(sf_ok, 4 * q)
                for t in range(2):
                    c = slice((2 * i + t) * P, (2 * i + t + 1) * P)
                    ins = pe.matmul(bank(C1 + i)[:, t * WX:(t + 1) * WX], hT[3][:, c], wx[:, :], start=True,
                                    stop=True, skip_group_check=True)
                ins.then_inc(hx_lin, 1)

            def do_mean(q):
                pe.wait_ge(hsB_ok, q + 1)
                pe.matmul(bank(C0)[:, 0:P], hsB[:, :], wx[:, 0:D], start=True, stop=True, skip_group_check=True
                          ).then_inc(mean_lin, 1)

            def do_ei(q):
                pe.wait_ge(hx_ok, 2 * q + 1)
                pe.matmul(bank(C1), w_ei[:, :], hT[3][:, :], start=True, stop=True, skip_group_check=True
                          ).then_inc(ei_lin, 1)

            def do_rows(q, i):
                if i == 0:
                    pe.wait_ge(eh_ok, q + 1)
                    pe.wait_ge(hx_ok, 2 * q + 2)
                if i == 1:
                    pe.wait_ge(meanh_ok, q + 1)
                if i >= 2:
                    pe.wait_ge(nei_ok, 4 * q + i - 1)
                pe.matmul(bank(C2 - 2 * (i % 2)), sel[:, i, :], eh[:, :], start=True, stop=True, skip_group_check=True
                              ).then_inc(ei_rows, 1)

            def do_all(q, b, i):
                pe.wait_ge(gp2_ok, q + 1)
                pe.wait_ge(adj_on_ok, q + 1)
                if i == 0:
                    pe.wait_ge(eh_ok, q + 1)
                else:
                    pe.wait_ge(nei_ok, 4 * (q + 1))
                for t in range(2):
                    tn = 2 * i + t
                    dst = tiles(bank(C1 - i)[:, t * HEADS * C:(t + 1) * HEADS * C], C)
                    for j in range(T):
                        for p in range(3):
                            ins = pe.matmul(dst, adj_on[b][:, j, tn * P:(tn + 1) * P], gp[p][:, j, :, 1, :],
                                            start=(j == 0 and p == 0), stop=(j == T - 1 and p == 2),
                                            skip_group_check=True)
                ins.then_inc(all_sum, 1)

            def do_head(q, i):
                if i == 0:
                    pe.wait_ge(gp2_ok, q + 1)
                    pe.wait_ge(nei_ok, 4 * q + 3)
                if i == 1:
                    pe.wait_ge(bf_ok, 2 * q + 1)
                if i == 2:
                    pe.wait_ge(bf_ok, 2 * q + 2)
                if i == 3:
                    pe.wait_ge(sf_ok, 4 * q + 1)
                pe.wait_ge(S_ok, 4 * q + i + 1)
                for tn in range(T):
                    dst = bank(HEAD_BANK[i])[:, tn * 2 * C:(tn + 1) * 2 * C]
                    for j in range(T):
                        for p in range(3):
                            ins = pe.matmul(dst, S[i % 2][:, j, tn * P:(tn + 1) * P],
                                            gp[p][:, j, i, :, :].rearrange("p s c -> p (s c)"),
                                            start=(j == 0 and p == 0), stop=(j == T - 1 and p == 2),
                                            skip_group_check=True)
                ins.then_inc(head_sum, 1)

            def turn(g, half, b):
                if there(g):
                    do_gru_c(g, 3)
                if there(g + 2):
                    turn_a(g + 2, 0)
                    turn_a(g + 2, 1)
                    turn_a(g + 2, 2)
                if there(g - 1):
                    do_head(g - 1, 2)
                    do_head(g - 1, 3)
                if there(g + 1):
                    turn_h(2, g + 1, B1)
                if there(g + 2):
                    turn_a(g + 2, 3)
                    light1(g + 2, b)
                if there(g + 1):
                    do_s(g + 1)
                    do_conv1(g + 1)
                if there(g + 2):
                    light2(g + 2, b)
                if there(g):
                    turn_h(3, g, C0)
                if there(g + 1):
                    do_sq(g + 1)
                    linear(B2, 2, wT[:, 2, :], msg_lin, g + 1)
                    do_conv2(g + 1, range(0, 2))
                if there(g):
                    do_hx(g, 0)
                    do_hx(g, 1)
                if there(g + 1):
                    do_conv2(g + 1, range(2, 3))
                if there(g):
                    do_ei(g)
                    do_mean(g)
                if there(g + 2):
                    light3(g + 2, b)
                if there(g + 1):
                    do_conv2(g + 1, range(3, 4))
                    do_dist(g + 1, 0)
                    do_conv2(g + 1, range(4, 6))
                    do_dist(g + 1, 1)
                    do_conv2(g + 1, range(6, 7))
                if there(g):
                    do_rows(g, 0)
                if there(g + 1):
                    do_dist(g + 1, 2)
                    do_conv2(g + 1, range(7, 9))
                if there(g):
                    do_rows(g, 1)
                if there(g + 1):
                    do_conv2(g + 1, range(9, 16))
                    do_dist(g + 1, 3)
                if there(g):
                    do_rows(g, 2)
                    do_rows(g, 3)
                    do_all(g, b, 0)
                if there(g + 2):
                    light4(g + 2, b)
                if there(g + 1):
                    do_conv2(g + 1, range(16, TAPS))
                    do_gru_h(g + 1, 0)
                if there(g + 2):
                    light5(g + 2, b)
                if there(g + 1):
                    do_nmp(g + 1)
                if there(g):
                    do_head(g, 0)
                if there(g + 2):
                    light6(g + 2, b)
                if there(g):
                    do_all(g, b, 1)
                    do_head(g, 1)
                if there(g + 1):
                    do_gru_n(g + 1, 0)
                    do_gru_c(g + 1, 0)
                    do_gru_h(g + 1, 1)
                    do_gru_n(g + 1, 1)
                    do_gru_c(g + 1, 1)
                    do_gru_h(g + 1, 2)
                    do_gru_n(g + 1, 2)
                    do_gru_c(g + 1, 2)
                    do_gru_h(g + 1, 3)
                    do_gru_n(g + 1, 3)

            run(pe, turn)

        @block.vector
        def _(dve):
            dve.wait_ge(set_loaded, 16 * LOADS)
            dve.wait_ge(set_pool, 6)
            dve.tensor_scalar(bn_ve[:, :], bn[:, :, 3], BN_EPS, None, ALU.add).then_inc(set_dve, 1)
            dve.wait_ge(set_pool, 7)
            dve.tensor_tensor(bn_sc[:, :], bn_rs[:, :], bn[:, :, 0], ALU.mult).then_inc(set_dve, 1)
            dve.wait_ge(set_dve, 2)
            dve.tensor_tensor(bn_ms[:, :], bn_sc[:, :], bn[:, :, 2], ALU.mult)
            dve.tensor_scalar(wnat[:, 3, :], wnat[:, 3, :], bn_sc[:, 0:1], None, ALU.mult)
            dve.tensor_scalar(c2nat, c2nat, bn_sc[:, 1:2], None, ALU.mult).then_inc(set_dve, 1)
            dve.wait_ge(set_dve, 3)
            dve.tensor_tensor(bn_sh[:, :], bn[:, :, 1], bn_ms[:, :], ALU.subtract)
            dve.tensor_scalar(alpha_eff[:, :], alphaB[:, :], 1e-10, None, ALU.max)
            hots = ident[:, 0:96].rearrange("p (q c) -> p q c", c=32)
            dve.tensor_reduce(hot[:, 0:1], hots[:, :, 0:3], AX.XY, ALU.add)
            dve.tensor_reduce(hot[:, 1:2], hots[:, :, 3:4], AX.XY, ALU.add)
            dve.tensor_reduce(hot[:, 2:3], hots[:, :, 4:5], AX.XY, ALU.add)
            dve.tensor_tensor(sel_col[:, :], ident[:, 0:HEADS], ident[:, 32:32 + HEADS], ALU.add)
            w3h = wx[:, 0:D].rearrange("p (h d) -> p h d", d=HD)
            for s in range(2):
                dve.tensor_tensor(wa[:, s, :, :], w3h, aB[:, :, s, :], ALU.mult)
            dve.tensor_tensor(br_a, br_a, br_b, ALU.add).then_inc(set_dve, 1)
            dve.wait_ge(set_dve, 4)
            dve.tensor_copy(br_p[:, 0, :], br_a)
            dve.scalar_tensor_tensor(out=left_sc[:, 0:1], in0=hot[:, 0:1], scalar=2.0, in1=hot[:, 1:2], op0=ALU.mult,
                                     op1=ALU.add)
            dve.scalar_tensor_tensor(out=left_sc[:, 1:2], in0=bse[:, :], scalar=2.0, in1=hot[:, 2:3], op0=ALU.mult,
                                     op1=ALU.add)
            dve.tensor_tensor(right_sc[:, 0:1], hot[:, 0:1], hot[:, 2:3], ALU.add)
            dve.tensor_tensor(right_sc[:, 1:2], bse[:, :], hot[:, 1:2], ALU.add)
            dve.tensor_copy(sel[:, :, :], sel_col[:, :].unsqueeze(2).broadcast_to([P, HEADS, P]))
            dve.tensor_reduce(wx[:, D:D + HEADS], wa[:, 1, :, :], AX.X, ALU.add)
            dve.tensor_reduce(wx[:, D + HEADS:WX], wa[:, 0, :, :], AX.X, ALU.add).then_inc(set_dve, 1)
            dve.wait_ge(set_dve, 5)
            for q in range(2):
                dve.tensor_scalar(w_ei[:, 32 * q:32 * q + HEADS], wx[:, D + HEADS:WX], -1.0, None, ALU.mult)
            dve.tensor_tensor(br_b, br_a, br_p[:, 0, :], ALU.subtract).then_inc(set_dve, 1)
            dve.wait_ge(set_dve, 6)
            dve.tensor_copy(br_p[:, 1, :], br_b)
            dve.tensor_copy(br[0:1, :], br_p[0:1, 0, :])
            dve.wait_ge(set_pe, 1)
            dve.tensor_copy(wT[:, :, :], tiles(bank(0)[:, 0:3 * P]))
            for q in range(3):
                dve.tensor_copy(w_se_pad[:, 32 * q:32 * q + SE], bank(0)[:, 3 * P:3 * P + SE])
            dve.tensor_copy(mask_sb[:, :], bank(1)[:, 0:GRAPHS * T])
            split = psum[:, :, :].rearrange("p b n -> p (b n)")[:, 5 * P:(5 + NSPLIT) * P]
            dve.tensor_copy(w_hi[:, :, :].rearrange("p a o -> p (a o)"), split).then_inc(set_dve, 1)
            dve.wait_ge(set_dve, 7)
            dve.tensor_tensor(w_lo[:, :, :].rearrange("p a o -> p (a o)"), split,
                              w_hi[:, :, :].rearrange("p a o -> p (a o)").bitcast(F32), ALU.subtract)
            dve.tensor_tensor(br_p[:, 2, :], br_b, br_p[:, 1, :], ALU.subtract)
            dve.tensor_copy(br[32:33, :], br_p[32:33, 1, :]).then_inc(set_dve, 1)
            dve.wait_ge(set_dve, 8)
            dve.tensor_copy(br[64:65, :], br_p[64:65, 2, :]).then_inc(set_dve, 1)

            def stats(i, q, src, half=None, b=None):
                if i == 0:
                    dve.wait_ge(x_loaded[b], 16 * (half + 1))
                    dve.wait_ge(rowsum_ok, q + 1)
                else:
                    dve.wait_ge((x1_ok, x2_ok, x3_ok)[i - 1], q + 1)
                dve.wait_ge(ln_mv_ok[i], q)
                for t in range(T):
                    ins = dve.bn_stats(ln_st[i][:, t, :], src[:, t, :])
                ins.then_inc(ln_st_ok[i], 1)

            def variance(i, q):
                dve.wait_ge(set_pool, 1)
                dve.wait_ge(ln_st_ok[i], q + 1)
                dve.wait_ge(ln_nm_ok[i], q)
                dve.wait_ge(ln_ve_ok[i], q)
                for t in range(T):
                    ins = dve.bn_aggr(ln_mv[i][:, t, :], ln_st[i][:, t, :])
                ins.then_inc(ln_mv_ok[i], 1)
                dve.wait_ge(ln_mv_ok[i], q + 1)
                dve.wait_ge(ln_rs_ok[i], q)
                dve.tensor_scalar(ln_ve[i][:, :], ln_mv[i][:, :, 1], LN_EPS, None, ALU.add).then_inc(ln_ve_ok[i], 1)

            def shift(i, q):
                dve.wait_ge(ln_rs_ok[i], q + 1)
                dve.wait_ge(h_ok[i], q)
                dve.scalar_tensor_tensor(out=ln_nm[i][:, :], in0=ln_mv[i][:, :, 0], scalar=-1.0, in1=ln_rs[i][:, :],
                                         op0=ALU.mult, op1=ALU.mult).then_inc(ln_nm_ok[i], 1)

            def degrees(q):
                dve.wait_ge(a_loaded, 16 * (q + 1))
                dve.wait_ge(degs_ok, 2 * q)
                dve.tensor_reduce(rowsum[:, :], a_nat[:, :, :], AX.X, ALU.add).then_inc(rowsum_ok, 1)

            def degree_sums(q):
                dve.wait_ge(rowsum_ok, q + 1)
                dve.wait_ge(dis_ok, q)
                dve.tensor_scalar(degs[:, 0, :], rowsum[:, :], 1.0, 1e-8, ALU.add, ALU.add).then_inc(degs_ok, 1)
                dve.scalar_tensor_tensor(out=degs[:, 1, :], in0=rowsum[:, :], scalar=0.0, in1=rowsum[:, :],
                                         op0=ALU.is_equal, op1=ALU.add).then_inc(degs_ok, 1)

            def mask_dis(q):
                dve.wait_ge(dis_ok, q + 1)
                dve.wait_ge(y0m_ok, q)
                dve.tensor_tensor(dmask[:, :], dis[:, 0, :], mask_sb[:, bass.ds(q * T, T)], ALU.mult
                                  ).then_inc(dmask_ok, 1)

            def take_aT(q, b, j):
                dve.wait_ge(a_turned, 4 * q + j + 1)
                if past(q - 1):
                    dve.wait_ge(adj_on_ok, q - 1)
                    dve.wait_ge(kadj_dve, 2 * (q - 1))
                    dve.wait_ge(kadj_pool, 2 * (q - 1))
                dve.tensor_copy(aT[b][:, j, :], bank(LIGHT + j % 2)).then_inc(aT_dve, 1)

            def bias0(q):
                dve.wait_ge(lin0, q + 1)
                dve.wait_ge(g0_ok, q)
                dve.tensor_tensor(t0[:, :, :], tiles(bank(LIGHT + 1)), b0B[:, :].unsqueeze(1).broadcast_to([P, T, D]),
                                  ALU.add).then_inc(t0_ok, 1)

            def self0(q):
                dve.wait_ge(agg0, q + 1)
                dve.wait_ge(g0_ok, q + 1)
                dve.wait_ge(y0m_ok, q)
                dve.tensor_tensor(y0[:, :, :], tiles(bank(LIGHT)), g0[:, :, :], ALU.add).then_inc(y0_ok, 1)

            def add0(q, b):
                dve.wait_ge(y0m_ok, q + 1)
                dve.wait_ge(h_ok[1], q)
                dve.wait_ge(r1_ok, q)
                dve.wait_ge(h_ok[0], q + 1)
                dve.scalar_tensor_tensor(out=x1[:, :, :], in0=y0[:, :, :], scalar=0.0, in1=x_in[b][:, :, :],
                                         op0=ALU.max, op1=ALU.add).then_inc(x1_ok, 1)

            def split1(q):
                dve.wait_ge(lin1, q + 1)
                dve.wait_ge(r1_ok, q)
                dve.wait_ge(agg1, q)
                dve.scalar_tensor_tensor(out=r0[:, :, :], in0=tiles(bank(LIGHT)), scalar=alpha_eff[:, 0:1],
                                         in1=b1B[:, :].unsqueeze(1).broadcast_to([P, T, D]), op0=ALU.mult, op1=ALU.add
                                         ).then_inc(r0_ok, 1)
                dve.tensor_tensor(g1[:, :, :], tiles(bank(LIGHT)), wide(dis[:, 1, :]), ALU.mult).then_inc(g1_ok, 1)

            def take_y1(q):
                dve.wait_ge(agg1, q + 1)
                dve.wait_ge(x2_ok, q)
                dve.tensor_tensor(y1[:, :, :], tiles(bank(LIGHT + 1)), wide(dis[:, 1, :]), ALU.mult).then_inc(y1_ok, 1)

            def add1(q, b):
                dve.wait_ge(y1_ok, q + 1)
                dve.wait_ge(r1_ok, q + 1)
                if past(q - 1):
                    dve.wait_ge(xn_ok, q - 1)
                    dve.wait_ge(h_ok[2], q - 1)
                dve.tensor_tensor(x2[b][:, :, :], y1[:, :, :], r0[:, :, :], ALU.add).then_inc(x2_ok, 1)

            def split_h2(q):
                dve.wait_ge(hT_ok[2], q + 1)
                dve.wait_ge(gru, 4 * q)
                dve.tensor_copy(h2_hi[:, :], hT[2][:, :]).then_inc(h2_hi_ok, 1)

            def rest_h2(q):
                dve.wait_ge(h2_hi_ok, q + 1)
                dve.tensor_tensor(h2_lo[:, :], hT[2][:, :], h2_hi[:, :].bitcast(F32), ALU.subtract).then_inc(h2_lo_ok, 1)

            def split_c1(q):
                dve.wait_ge(c1_ok, q + 1)
                dve.wait_ge(conv2, q)
                dve.tensor_copy(c1_hi[:, PAD:PAD + N], c1[:, :]).then_inc(c1_hi_ok, 1)

            def rest_c1(q):
                dve.wait_ge(c1_hi_ok, q + 1)
                dve.tensor_tensor(c1_lo[:, PAD:PAD + N], c1[:, :], c1_hi[:, PAD:PAD + N].bitcast(F32), ALU.subtract
                                  ).then_inc(c1_lo_ok, 1)

            def split_lr(q):
                dve.wait_ge(dist, 4 * q)
                dve.wait_ge(left_f_ok, q + 1)
                dve.tensor_copy(left[:, :], left_f[:, :]).then_inc(lr_hi_ok, 1)
                dve.wait_ge(right_f_ok, q + 1)
                dve.tensor_copy(right[:, :], right_f[:, :]).then_inc(lr_hi_ok, 1)

            def rest_lr(q):
                for n, (src, dst) in enumerate(((left_f, left), (right_f, right))):
                    c = slice(32 * (n + 1), 32 * (n + 2))
                    dve.wait_ge(lr_hi_ok, 2 * q + n + 1)
                    dve.tensor_tensor(dst[c, :], src[c, :], dst[c, :].bitcast(F32), ALU.subtract).then_inc(lr_ok, 1)

            def bias_msg(q):
                dve.wait_ge(msg_lin, q + 1)
                dve.wait_ge(msg_ok, q)
                dve.wait_ge(lr_ok, 2 * q + 1)
                dve.tensor_tensor(msg_b, tiles(bank(HEAVY + 2)), bmB[:, :].unsqueeze(1).broadcast_to([P, T, D]),
                                  ALU.add).then_inc(msg_b_ok, 1)

            def kernel_adj(q, b, j):
                dve.wait_ge(ker_ok, 4 * q + j + 1)
                dve.wait_ge(nmp, q)
                dve.tensor_tensor(kadj[:, j, :], ker[:, j % 2, :], aT[b][:, j, :], ALU.mult).then_inc(kadj_dve, 1)

            def adjacent(q, b):
                if past(q - 1):
                    dve.wait_ge(head_sum, 4 * (q - 1))
                    dve.wait_ge(S_ok, 4 * (q - 1))
                dve.wait_ge(aT_act, 2 * (q + 1))
                dve.tensor_scalar(adj_on[b][:, :, :], aT[b][:, :, :], 0.0, None, ALU.is_gt).then_inc(adj_on_ok, 1)

            def split_n(q):
                dve.wait_ge(n_hi_ok, q + 1)
                dve.tensor_tensor(n_lo[:, :], bank(HEAVY), n_hi[:, :].bitcast(F32), ALU.subtract
                                  ).then_inc(n_lo_ok, 1)

            def add_conv(q):
                dve.wait_ge(conv2, q + 1)
                dve.wait_ge(c_lo_ok, q)
                dve.scalar_tensor_tensor(out=u[:, :], in0=bank(HEAVY + 1), scalar=bn_sh[:, 1:2], in1=hT[2][:, :],
                                         op0=ALU.add, op1=ALU.add).then_inc(u_ok, 1)

            def split_conv(q):
                dve.wait_ge(c_hi_ok, q + 1)
                dve.scalar_tensor_tensor(out=c_lo[:, :], in0=u[:, :], scalar=0.0, in1=c_hi[:, :].bitcast(F32),
                                         op0=ALU.max, op1=ALU.subtract).then_inc(c_lo_ok, 1)

            def gates(q, t):
                dst = bank(GRU_BANK[t])
                dve.wait_ge(rz_ok, 4 * q + t + 1)
                dve.wait_ge(nn_ok, q)
                dve.scalar_tensor_tensor(out=q2[:, t, :], in0=rz[:, t, 0:D], scalar=1.0, in1=dst[:, 3 * D:4 * D],
                                         op0=ALU.add, op1=ALU.mult).then_inc(q1_ok, 1)

            def add_gi(q, t):
                dve.wait_ge(q1_ok, 4 * q + t + 1)
                dve.scalar_tensor_tensor(out=q2[:, t, :], in0=q2[:, t, :], scalar=0.5, in1=bank(GRU_BANK[t])[:, 0:D],
                                         op0=ALU.mult, op1=ALU.add).then_inc(q2_ok, 1)

            def mix(q):
                dve.wait_ge(nn_ok, q + 1)
                dve.wait_ge(zd_ok, q)
                dve.tensor_tensor(zd[:, :, :], h[2][:, :, :], nn[:, :, :], ALU.subtract).then_inc(hmn_ok, 1)

            def mix_z(q):
                dve.wait_ge(hmn_ok, q + 1)
                dve.wait_ge(x3_ok, q)
                dve.scalar_tensor_tensor(out=zd[:, :, :], in0=rz[:, :, D:2 * D], scalar=1.0, in1=zd[:, :, :],
                                         op0=ALU.add, op1=ALU.mult).then_inc(zd_ok, 1)

            def add2(q, b):
                dve.wait_ge(zd_ok, q + 1)
                dve.wait_ge(xn_ok, q + 1)
                if past(q - 1):
                    dve.wait_ge(xf_ok, q - 1)
                    dve.wait_ge(h_ok[3], q - 1)
                dve.scalar_tensor_tensor(out=x3[b][:, :, :], in0=zd[:, :, :], scalar=0.5, in1=xn[:, :, :],
                                         op0=ALU.mult, op1=ALU.add).then_inc(x3_ok, 1)

            def split_ei(q):
                dve.wait_ge(eh_hi_ok, q + 1)
                dve.tensor_tensor(eh[32:64, :], bank(LAST + 1)[32:64, :], eh[32:64, :].bitcast(F32), ALU.subtract
                                  ).then_inc(eh_ok, 1)

            def local_max(q):
                dve.wait_ge(hx_ok, 2 * (q + 1))
                dve.wait_ge(cB_ok, q)
                dve.tensor_reduce(mxl[:, :], hx[:, :, D:D + HEADS].rearrange("p t h -> p h t"), AX.X, ALU.max
                                  ).then_inc(mxl_ok, 1)

            def exponents(q):
                c = cB[:, :].unsqueeze(1).broadcast_to([P, T, HEADS])
                dve.wait_ge(cB_ok, q + 1)
                dve.wait_ge(ee_ok, q)
                dve.tensor_tensor(z[:, :, :], hx[:, :, D + HEADS:WX], c, ALU.add)
                dve.tensor_tensor(ex[:, 0, :, :], hx[:, :, D:D + HEADS], c, ALU.subtract).then_inc(z_ok, 1)

            def exponents2(q):
                dve.wait_ge(z_ok, q + 1)
                dve.wait_ge(ee_ok, q)
                dve.tensor_scalar(ex[:, 1, :, :], ex[:, 0, :, :], 0.2, None, ALU.mult)
                dve.tensor_scalar(ex[:, 2, :, :], z[:, :, :], 0.8, 0.0, ALU.mult, ALU.min)
                dve.tensor_scalar(ex[:, 3, :, :], z[:, :, :], -0.8, 0.0, ALU.mult, ALU.min).then_inc(ex_ok, 1)

            def weigh_e(q):
                dve.wait_ge(ee_ok, q + 1)
                dve.wait_ge(gr_ok, q)
                dve.wait_ge(gp0_ok, q)
                dve.tensor_tensor(gf[:, :, :, 0, 0:HD], hx[:, :, 0:D].rearrange("p t (h d) -> p t h d", d=HD),
                                  ee[:, 0, :, :].unsqueeze(3).broadcast_to([P, T, HEADS, HD]), ALU.mult)
                for s in range(2):
                    ins = dve.tensor_copy(gf[:, :, :, s, HD], ee[:, s, :, :])
                ins.then_inc(gf_dve, 1)

            def rest(q):
                dve.wait_ge(gp0_ok, q + 1)
                dve.wait_ge(gp2_ok, q)
                flat = "p t h s c -> p (t h s c)"
                dve.tensor_tensor(gf[:, :, :, :, :].rearrange(flat), gf[:, :, :, :, :].rearrange(flat),
                                  gp[0][:, :, :, :, :].rearrange(flat), ALU.subtract).then_inc(gr_ok, 1)

            def masks(q, b, i):
                dve.wait_ge(nei_ok, 4 * q + i + 1)
                dve.wait_ge(adj_on_ok, q + 1)
                if i >= 2:
                    dve.wait_ge(head_sum, 4 * q + i - 1)
                else:
                    dve.wait_ge(head_sum, 4 * q)
                for j in range(T):
                    ins = dve.scalar_tensor_tensor(out=S[i % 2][:, j, :], in0=nei[:, i, :],
                                                   scalar=hx[:, j, D + i:D + i + 1], in1=adj_on[b][:, j, :],
                                                   op0=ALU.is_lt, op1=ALU.mult)
                ins.then_inc(S_ok, 1)

            def combine(q):
                dve.wait_ge(sf_ok, 4 * (q + 1))
                dve.wait_ge(bf_ok, 2 * (q + 1))
                dve.wait_ge(v2_ok, q)
                dve.tensor_tensor(tot[:, :, :, :], bf[:, :, :, :].rearrange("p t h c -> p h t c"), sf[:, :, :, 1, :],
                                  ALU.subtract).then_inc(v1_ok, 1)

            def weigh_f(q):
                e3 = ee[:, 3, :, :].rearrange("p t h -> p h t").unsqueeze(3).broadcast_to([P, HEADS, T, C])
                dve.wait_ge(v1_ok, q + 1)
                dve.wait_ge(tot_ok, q)
                dve.tensor_tensor(tot[:, :, :, :], tot[:, :, :, :], e3, ALU.mult).then_inc(v2_ok, 1)

            def total(q):
                dve.wait_ge(v2_ok, q + 1)
                dve.wait_ge(ue_ok, q + 1)
                dve.wait_ge(o1_ok, q)
                dve.wait_ge(den_ok, q)
                dve.tensor_tensor(tot[:, :, :, :], tot[:, :, :, :], ue[:, :, :, :], ALU.add).then_inc(tot_ok, 1)

            def isolated(q):
                dve.wait_ge(tot_ok, q + 1)
                dve.wait_ge(fm_ok, q)
                dve.tensor_scalar(flag[:, :, :], tot[:, :, :, HD], 0.0, None, ALU.is_equal).then_inc(flag_ok, 1)

            def denominator(q):
                dve.wait_ge(flag_ok, q + 1)
                dve.wait_ge(rec_ok, q)
                dve.tensor_tensor(den[:, :, :], tot[:, :, :, HD], flag[:, :, :], ALU.add).then_inc(den_ok, 1)

            def invert(q):
                dve.wait_ge(den_ok, q + 1)
                dve.wait_ge(o1_ok, q)
                dve.reciprocal(rec[:, :, :], den[:, :, :]).then_inc(rec_ok, 1)

            def divide(q):
                dve.wait_ge(rec_ok, q + 1)
                dve.wait_ge(o_ok, q)
                dve.tensor_tensor(o1, tot[:, :, :, 0:HD],
                                  rec[:, :, :].unsqueeze(3).broadcast_to([P, HEADS, T, HD]), ALU.mult
                                  ).then_inc(o1_ok, 1)

            def finish(q):
                dve.wait_ge(o1_ok, q + 1)
                dve.wait_ge(xf_ok, q + 1)
                dve.wait_ge(stored, 16 * q)
                dve.tensor_tensor(o_sb[:, :, :].rearrange("p t (h d) -> p h t d", d=HD), o1,
                                  fm[:, :, :].rearrange("p t (h d) -> p h t d", d=HD), ALU.add).then_inc(o_ok, 1)

            def turn(g, half, b):
                if there(g):
                    shift(1, g)
                if there(g - 2):
                    masks(g - 2, b, 0)
                if there(g + 1):
                    degrees(g + 1)
                if there(g - 1):
                    kernel_adj(g - 1, 1 - b, 2)
                if there(g + 1):
                    stats(0, g + 1, x_in[1 - b], half + b, 1 - b)
                if there(g - 1):
                    add_conv(g - 1)
                if there(g):
                    split1(g)
                if there(g - 2):
                    masks(g - 2, b, 1)
                if there(g - 1):
                    split_n(g - 1)
                    split_conv(g - 1)
                if there(g + 1):
                    variance(0, g + 1)
                    degree_sums(g + 1)
                if there(g):
                    take_y1(g)
                    add1(g, b)
                if there(g + 1):
                    shift(0, g + 1)
                if there(g - 2):
                    masks(g - 2, b, 2)
                if there(g - 1):
                    gates(g - 1, 0)
                if there(g - 2):
                    masks(g - 2, b, 3)
                if there(g):
                    stats(2, g, x2[b])
                if there(g - 1):
                    add_gi(g - 1, 0)
                    gates(g - 1, 1)
                    add_gi(g - 1, 1)
                if there(g):
                    variance(2, g)
                    shift(2, g)
                if there(g - 1):
                    gates(g - 1, 2)
                    add_gi(g - 1, 2)
                    gates(g - 1, 3)
                    add_gi(g - 1, 3)
                    mix(g - 1)
                    mix_z(g - 1)
                    add2(g - 1, 1 - b)
                if there(g + 1):
                    take_aT(g + 1, 1 - b, 1)
                if there(g - 1):
                    stats(3, g - 1, x3[1 - b])
                    variance(3, g - 1)
                if there(g):
                    split_h2(g)
                    rest_h2(g)
                if there(g - 1):
                    shift(3, g - 1)
                if there(g - 2):
                    combine(g - 2)
                if there(g + 1):
                    take_aT(g + 1, 1 - b, 3)
                    mask_dis(g + 1)
                if there(g):
                    adjacent(g, b)
                    split_c1(g)
                    rest_c1(g)
                if there(g - 2):
                    weigh_f(g - 2)
                    total(g - 2)
                if there(g + 1):
                    bias0(g + 1)
                if there(g - 2):
                    isolated(g - 2)
                if there(g):
                    split_lr(g)
                if there(g - 2):
                    denominator(g - 2)
                if there(g):
                    rest_lr(g)
                if there(g - 2):
                    invert(g - 2)
                if there(g - 1):
                    local_max(g - 1)
                if there(g):
                    bias_msg(g)
                if there(g - 1):
                    exponents(g - 1)
                    exponents2(g - 1)
                if there(g - 2):
                    divide(g - 2)
                if there(g - 1):
                    weigh_e(g - 1)
                    split_ei(g - 1)
                if there(g - 2):
                    finish(g - 2)
                if there(g + 1):
                    self0(g + 1)
                if there(g):
                    kernel_adj(g, b, 0)
                if there(g + 1):
                    add0(g + 1, 1 - b)
                if there(g - 1):
                    rest(g - 1)
                if there(g + 1):
                    stats(1, g + 1, x1)
                    variance(1, g + 1)

            run(dve, turn)


_INS = ['x', 'adj', 'nodemask', 'L0_gnn_W', 'L0_gnn_b', 'L1_gnn_W', 'L1_gnn_b', 'L1_gnn_alpha', 'L2_gnn_w_se',
        'L2_gnn_b_se', 'L2_gnn_conv1_w', 'L2_gnn_bn1_g', 'L2_gnn_bn1_b', 'L2_gnn_bn1_m', 'L2_gnn_bn1_v',
        'L2_gnn_conv2_w', 'L2_gnn_bn2_g', 'L2_gnn_bn2_b', 'L2_gnn_bn2_m', 'L2_gnn_bn2_v', 'L2_gnn_w_msg',
        'L2_gnn_b_msg', 'L2_gnn_w_ih', 'L2_gnn_b_ih', 'L2_gnn_w_hh', 'L2_gnn_b_hh', 'L3_gnn_W', 'L3_gnn_a']


def kernel(**inputs):
    import numpy as _np
    import concourse.bacc as _bacc
    from concourse import mybir as _mybir
    from concourse.bass_utils import run_bass_kernel_spmd as _run

    nc = _bacc.Bacc("TRN2", target_bir_lowering=False, num_devices=1)
    arrays, args = {}, []
    for name in _INS:
        a = _np.ascontiguousarray(inputs[name])
        arrays[f"in_{name}_dram"] = a
        args.append(nc.dram_tensor(f"in_{name}_dram", a.shape, _mybir.dt.from_np(a.dtype), kind="ExternalInput").ap())
    shape = inputs['x'].shape
    args.append(nc.dram_tensor("out_0_dram", shape, _mybir.dt.float32, kind="ExternalOutput").ap())
    build_gnn(nc, *args)
    r = _run(nc, [arrays], core_ids=[0])
    return r.results[0]["out_0_dram"]
```

```python
from contextlib import ExitStack

import concourse.bass as bass
from concourse import mybir

P = 128
F32 = mybir.dt.float32
F32R = mybir.dt.float32r
BF16 = mybir.dt.bfloat16
ALU = mybir.AluOpType
ACT = mybir.ActivationFunctionType
AX = mybir.AxisListType
RMAX = bass.bass_isa.ReduceOp.max


def build_gnn(nc: bass.Bass, x, adj, nodemask, w0, b0, w1, b1, alpha, w_se, b_se, conv1_w, bn1_g, bn1_b,
              bn1_m, bn1_v, conv2_w, bn2_g, bn2_b, bn2_m, bn2_v, w_msg, b_msg, w_ih, b_ih, w_hh, b_hh,
              w3, a3, out):
    GRAPHS, N, D = x.shape
    T = N // P
    TAPS = conv2_w.shape[2]
    PAD = TAPS // 2
    HEADS = a3.shape[0]
    HD = D // HEADS
    SE = w_se.shape[0]
    C = HD + 1
    assert D == P and N == 4 * P and GRAPHS % 2 == 0 and SE == 3
    LN_EPS = 1e-5
    BN_EPS = 1e-5

    ctx = ExitStack()
    with ctx:
        def sb(name, shape, dt=F32):
            return ctx.enter_context(nc.sbuf_tensor(name, shape, dt))

        def sem(name):
            return ctx.enter_context(nc.semaphore(name))

        psum = ctx.enter_context(nc.psum_tensor("psum", [P, 8, N], F32))
        LIGHT, HEAVY, LAST = 0, 2, 5
        GRU_BANK = (HEAVY, HEAVY + 1, HEAVY + 2, HEAVY)
        HEAD_BANK = (LAST + 2, LAST + 1, LAST, LAST + 2)

        def bank(i):
            return psum[:, i, :]

        def tiles(ap, c=P):
            return ap.rearrange("p (t c) -> p t c", c=c)

        ident = sb("ident", [P, P])
        half_pow = sb("half_pow", [P, 8])
        se_nat = sb("se_nat", [SE, P])
        mask_nat = sb("mask_nat", [GRAPHS * T, P])
        mask_sb = sb("mask_sb", [P, GRAPHS * T])
        wT = sb("wT", [P, 3, P])
        E_TAPS, O_TAPS, HN = PAD + 1, PAD, N // 2
        PIECES = 2 * E_TAPS + O_TAPS
        HPAD = PAD // 2
        HLEN = HN + PAD + 2
        NSPLIT = 10 + TAPS + O_TAPS
        w_hi = sb("w_hi", [P, NSPLIT, P], F32R)
        w_lo = sb("w_lo", [P, NSPLIT, P], F32R)
        w_se_pad = sb("w_se_pad", [P, P])
        w_se_hi = sb("w_se_hi", [P, P], F32R)
        w_se_lo = sb("w_se_lo", [P, P], F32R)
        neg_sq = sb("neg_sq", [P, P])
        hot = sb("hot", [P, 3])
        bse = sb("bse", [P, 1])
        left_sc = sb("left_sc", [P, 2])
        right_sc = sb("right_sc", [P, 2])
        bn = sb("bn", [P, 2, 4])
        bn_ve = sb("bn_ve", [P, 2])
        bn_rs = sb("bn_rs", [P, 2])
        bn_sc = sb("bn_sc", [P, 2])
        bn_ms = sb("bn_ms", [P, 2])
        bn_sh = sb("bn_sh", [P, 2])
        b0B = sb("b0B", [P, P])
        b1B = sb("b1B", [P, P])
        bmB = sb("bmB", [P, P])
        alphaB = sb("alphaB", [P, 1])
        alpha_eff = sb("alpha_eff", [P, 1])
        aB = sb("aB", [P, HEADS, 2, HD])
        wx = sb("wx", [P, D + 2 * HEADS])
        w_ei = sb("w_ei", [P, P])
        sel_col = sb("sel_col", [P, HEADS])
        sel = sb("sel", [P, HEADS, P], F32R)
        br = sb("br", [P, N], BF16)
        ones3 = sb("ones3", [P, P], BF16)
        ones = sb("ones", [P, P])

        a_nat = sb("a_nat", [P, T, N])
        x_in = [sb(f"x_in{i}", [P, T, D]) for i in range(2)]
        aT = [sb(f"aT{i}", [P, T, N]) for i in range(2)]
        rowsum = sb("rowsum", [P, T])
        degs = sb("degs", [P, 2, T])
        dis = sb("dis", [P, 2, T])
        dmask = sb("dmask", [P, T])
        t0 = sb("t0", [P, T, D])
        g0 = sb("g0", [P, T, D])
        y0 = g0
        x1 = sb("x1", [P, T, D])
        r0 = sb("r0", [P, T, D])
        g1 = sb("g1", [P, T, D])
        y1 = t0
        x2 = [sb(f"x2_{i}", [P, T, D]) for i in range(2)]
        h_light, hT_light = sb("h_light", [P, T, D]), sb("hT_light", [P, N])
        h = [h_light, h_light, sb("h2", [P, T, D]), sb("h3", [P, T, D])]
        hT = [hT_light, hT_light, sb("hT2", [P, N]), sb("hT3", [P, N])]
        ln_st = [sb(f"ln_st{i}", [P, T, 6]) for i in range(4)]
        ln_mv = [sb(f"ln_mv{i}", [P, T, 2]) for i in range(4)]
        ln_ve = [sb(f"ln_ve{i}", [P, T]) for i in range(4)]
        ln_rs = [sb(f"ln_rs{i}", [P, T]) for i in range(4)]
        ln_nm = [sb(f"ln_nm{i}", [P, T]) for i in range(4)]

        h2_hi = sb("h2_hi", [P, N], F32R)
        h2_lo = sb("h2_lo", [P, N], F32R)
        c1 = sb("c1", [P, 2, HLEN])
        c1_hi = sb("c1_hi", [P, 2, HLEN], F32R)
        c1_lo = sb("c1_lo", [P, 2, HLEN], F32R)
        xs = sb("xs", [P, HN + PAD])
        xs_hi = sb("xs_hi", [P, HN + PAD], F32R)
        xs_lo = sb("xs_lo", [P, HN + PAD], F32R)
        left_f = sb("left_f", [P, N])
        right_f = sb("right_f", [P, N])
        s_sq = right_f
        left = sb("left", [P, N], F32R)
        right = sb("right", [P, N], F32R)
        msg_b = left_f[:, :].rearrange("p (t d) -> p t d", d=D)
        msg = msg_b
        ker_kadj = sb("ker_kadj", [P, T + 2, N])
        ker, kadj = ker_kadj[:, T:T + 2, :], ker_kadj[:, 0:T, :]
        adj_on = [sb(f"adj_on{i}", [P, T, N], BF16) for i in range(2)]
        n_hi = sb("n_hi", [P, N], F32R)
        n_lo = sb("n_lo", [P, N], F32R)
        u = c1[:, :, HPAD:HPAD + HN]
        c_hi = sb("c_hi", [P, N], F32R)
        c_lo = sb("c_lo", [P, N], F32R)
        rz = sb("rz", [P, T, 2 * D])
        q2 = sb("q2", [P, T, D])
        nn = q2
        zd = sb("zd", [P, T, D])
        x3 = [sb(f"x3_{i}", [P, T, D]) for i in range(2)]

        WX = D + 2 * HEADS
        hsum = sb("hsum", [P, 1])
        hsB = sb("hsB", [P, P])
        meanh = sb("meanh", [P, P])
        hx = sb("hx", [P, T, WX])
        eh = sb("eh", [P, N], F32R)
        nei = sb("nei", [P, HEADS, N])
        mxl = sb("mxl", [P, HEADS])
        cB = sb("cB", [P, HEADS])
        z = sb("z", [P, T, HEADS])
        ex = sb("ex", [P, 4, T, HEADS])
        ee = sb("ee", [P, 4, T, HEADS])
        gf = sb("gf", [P, T, HEADS, 2, C])
        gp = [sb(f"gp{i}", [P, T, HEADS, 2, C], BF16) for i in range(3)]
        S = [sb(f"S{i}", [P, T, N], BF16) for i in range(2)]
        bf = sb("bf", [P, T, HEADS, C])
        sf = sb("sf", [P, HEADS, T, 2, C])
        tot = bf[:, :, :, :].rearrange("p t h c -> p h t c")
        ue = sb("ue", [P, HEADS, T, C])
        flag = sb("flag", [P, HEADS, T])
        den = sb("den", [P, HEADS, T])
        rec = sb("rec", [P, HEADS, T])
        fm = sb("fm", [P, T, D])
        o1 = ue[:, :, :, 0:HD]
        o_sb = fm

        nat_lin = q2
        nat_ih = rz[:, :, :].rearrange("p t c -> p (t c)")[:, 0:6 * P].rearrange("p (w i) -> p w i", i=P)
        spare = gf[:, :, :, :, :].rearrange("p t h s c -> p (t h s c)")[:, 0:8 * P].rearrange("p (w i) -> p w i", i=P)
        nat_hh = spare[:, 0:4, :]
        c2sum = (zd, spare[:, 4:8, :])
        c2nat = ker_kadj[:, :, :].rearrange("p t n -> p (t n)")[:, 0:P * TAPS]
        br_a, br_b = nei[:, 0, :], nei[:, 1, :]
        wa = nei[:, 2, 0:2 * D].rearrange("p (s h d) -> p s h d", s=2, d=HD)
        br_p = S[0][:, 0:3, :]

        light_loaded = sem("light_loaded")
        split_loaded = sem("split_loaded")
        set_loaded = sem("set_loaded")
        set_pool = sem("set_pool")
        set_dve = sem("set_dve")
        set_pe = sem("set_pe")
        set_act = sem("set_act")
        a_loaded = sem("a_loaded")
        x_loaded = [sem(f"x_loaded{i}") for i in range(2)]
        stored = sem("stored")
        ln_st_ok = [sem(f"ln_st_ok{i}") for i in range(4)]
        ln_mv_ok = [sem(f"ln_mv_ok{i}") for i in range(4)]
        ln_ve_ok = [sem(f"ln_ve_ok{i}") for i in range(4)]
        ln_rs_ok = [sem(f"ln_rs_ok{i}") for i in range(4)]
        ln_nm_ok = [sem(f"ln_nm_ok{i}") for i in range(4)]
        h_ok = [sem(f"h_ok{i}") for i in range(4)]
        turned = [sem(f"turned{i}") for i in range(4)]
        hT_ok = [sem(f"hT_ok{i}") for i in range(4)]
        a_turned = sem("a_turned")
        aT_ok = sem("aT_ok")
        rowsum_ok = sem("rowsum_ok")
        degs_ok = sem("degs_ok")
        dis_ok = sem("dis_ok")
        dmask_ok = sem("dmask_ok")
        lin0 = sem("lin0")
        t0_ok = sem("t0_ok")
        g0_ok = sem("g0_ok")
        agg0 = sem("agg0")
        y0_ok = sem("y0_ok")
        y0m_ok = sem("y0m_ok")
        x1_ok = sem("x1_ok")
        lin1 = sem("lin1")
        r0_ok = sem("r0_ok")
        g1_ok = sem("g1_ok")
        r1_ok = sem("r1_ok")
        agg1 = sem("agg1")
        y1_ok = sem("y1_ok")
        x2_ok = sem("x2_ok")
        h2_hi_ok = sem("h2_hi_ok")
        h2_lo_ok = sem("h2_lo_ok")
        conv1 = sem("conv1")
        c1_ok = sem("c1_ok")
        c1_hi_ok = sem("c1_hi_ok")
        xs_ok = sem("xs_ok")
        xs_hi_ok = sem("xs_hi_ok")
        xs_lo_ok = sem("xs_lo_ok")
        u_part = sem("u_part")
        c1_lo_ok = sem("c1_lo_ok")
        s_lin = sem("s_lin")
        s_sq_ok = sem("s_sq_ok")
        s_all = sem("s_all")
        left_f_ok = sem("left_f_ok")
        right_f_ok = sem("right_f_ok")
        lr_hi_ok = sem("lr_hi_ok")
        lr_ok = sem("lr_ok")
        msg_lin = sem("msg_lin")
        msg_b_ok = sem("msg_b_ok")
        msg_ok = sem("msg_ok")
        dist = sem("dist")
        ker_ok = sem("ker_ok")
        kadj_dve = sem("kadj_dve")
        kadj_pool = sem("kadj_pool")
        adj_on_ok = sem("adj_on_ok")
        nmp = sem("nmp")
        n_hi_ok = sem("n_hi_ok")
        n_lo_ok = sem("n_lo_ok")
        conv2 = sem("conv2")
        u_ok = sem("u_ok")
        c_hi_ok = sem("c_hi_ok")
        c_lo_ok = sem("c_lo_ok")
        gru = sem("gru")
        rz_ok = sem("rz_ok")
        q1_ok = sem("q1_ok")
        q2_ok = sem("q2_ok")
        nn_ok = sem("nn_ok")
        hmn_ok = sem("hmn_ok")
        zd_ok = sem("zd_ok")
        xn_ok = sem("xn_ok")
        x3_ok = sem("x3_ok")
        hx_lin = sem("hx_lin")
        hx_ok = sem("hx_ok")
        hsB_ok = sem("hsB_ok")
        mean_lin = sem("mean_lin")
        meanh_ok = sem("meanh_ok")
        ei_lin = sem("ei_lin")
        eh_hi_ok = sem("eh_hi_ok")
        eh_ok = sem("eh_ok")
        ei_rows = sem("ei_rows")
        nei_ok = sem("nei_ok")
        mxl_ok = sem("mxl_ok")
        cB_ok = sem("cB_ok")
        z_ok = sem("z_ok")
        ex_ok = sem("ex_ok")
        ee_ok = sem("ee_ok")
        gf_dve = sem("gf_dve")
        gf_pool = sem("gf_pool")
        gp0_ok = sem("gp0_ok")
        gr_ok = sem("gr_ok")
        gp1_ok = sem("gp1_ok")
        gp2_ok = sem("gp2_ok")
        all_sum = sem("all_sum")
        bf_ok = sem("bf_ok")
        S_ok = sem("S_ok")
        head_sum = sem("head_sum")
        sf_ok = sem("sf_ok")
        v1_ok = sem("v1_ok")
        v2_ok = sem("v2_ok")
        ue_ok = sem("ue_ok")
        tot_ok = sem("tot_ok")
        flag_ok = sem("flag_ok")
        den_ok = sem("den_ok")
        rec_ok = sem("rec_ok")
        fm_ok = sem("fm_ok")
        xf_ok = sem("xf_ok")
        o1_ok = sem("o1_ok")
        o_ok = sem("o_ok")

        FIRST, LOOP, LOOP_END, END = -2, 4, GRAPHS - 2, GRAPHS + 2

        x_v = x.rearrange("g (t p) d -> g p t d", p=P)
        adj_v = adj.rearrange("g (t p) m -> g p t m", p=P)
        out_v = out.rearrange("g (t p) d -> g p t d", p=P)

        def wide(col):
            return col.unsqueeze(2).broadcast_to([P, T, D])

        def past(q):
            return not isinstance(q, int) or q >= 1

        def there(q):
            return not isinstance(q, int) or 0 <= q < GRAPHS

        def by_parity(ap):
            return ap.rearrange("p (m two) -> p two m", two=2)

        def first(q):
            return isinstance(q, int) and q == 0

        def run(eng, turn):
            for g in range(FIRST, LOOP):
                turn(g, g // 2, g % 2)
            with eng.Fori(0, (LOOP_END - LOOP) // 2, 1) as k:
                turn(2 * k + LOOP, k + LOOP // 2, 0)
                turn(2 * k + LOOP + 1, k + LOOP // 2, 1)
            for g in range(LOOP_END, END):
                turn(g, g // 2, g % 2)

        def slots(at, n):
            return psum[:, :, :].rearrange("p b n -> p (b n)")[:, at * P:(at + n) * P]

        W_PARTS = ((0, 10, 10), (10, 20, 20), (20, NSPLIT, 8))
        SET_DVE = 13

        block = ctx.enter_context(nc.Block())

        @block.sync
        def _(sp):
            def fetch(q, b):
                sp.dma_start(a_nat[:, :, :], adj_v[q]).then_inc(a_loaded, 16)
                sp.dma_start(x_in[b][:, :, :], x_v[q]).then_inc(x_loaded[b], 16)

            fetch(0, 0)

            def load(dst, src):
                sp.dma_start(dst, src).then_inc(set_loaded, 16)

            def load_light(dst, src):
                sp.dma_start(dst, src).then_inc(light_loaded, 16)

            load_light(nat_lin[:, 0, :], w0)
            load_light(nat_lin[:, 1, :], w1)
            load_light(mask_nat[:, :], nodemask.rearrange("g (t p) -> (g t) p", p=P))
            load_light(b0B[:, :], b0.partition_broadcast(P))
            load_light(b1B[:, :], b1.partition_broadcast(P))
            load_light(alphaB[:, :], alpha.partition_broadcast(P))
            def load_split(dst, src):
                sp.dma_start(dst, src).then_inc(split_loaded, 16)

            for i, v in enumerate((bn1_g, bn1_b, bn1_m, bn1_v)):
                load_split(bn[:, 0, i:i + 1], v.unsqueeze(1))
            for i, v in enumerate((bn2_g, bn2_b, bn2_m, bn2_v)):
                load_split(bn[:, 1, i:i + 1], v.unsqueeze(1))
            load_split(nat_lin[:, 3, :], conv1_w.rearrange("o i k -> o (i k)"))
            load_split(c2nat, conv2_w.rearrange("o i k -> o (i k)"))
            load_split(nat_lin[:, 2, :], w_msg)
            load_split(nat_ih, w_ih.rearrange("(r o) (c i) -> o r c i", o=P, c=2))
            load_split(nat_hh[:, 0:3, :], w_hh.rearrange("(r o) i -> o r i", o=P))
            load_split(se_nat[:, :], w_se)
            load(wx[:, 0:D], w3)
            load(bmB[:, :], b_msg.partition_broadcast(P))
            load(aB[:, :, :, :], a3.rearrange("h (s d) -> h s d", s=2).partition_broadcast(P))
            sp.wait_ge(set_pool, 1)
            for q in range(3):
                load(bse[32 * q:32 * q + SE, :], b_se.unsqueeze(1))
            rows = slice(0, 65, 32)
            load(br_a[rows, 0:D], b_ih[2 * D:3 * D].partition_broadcast(3))
            load(br_a[rows, D:3 * D], b_ih[0:2 * D].partition_broadcast(3))
            load(br_b[rows, D:4 * D], b_hh.partition_broadcast(3))

            def value(v):
                return v if isinstance(v, int) else sp.snap(v)

            def next_graph(q, b):
                turned4, read = value(4 * q), value(q)
                sp.wait_ge(set_pool, 1)
                sp.wait_ge(a_turned, turned4)
                sp.wait_ge(rowsum_ok, read)
                fetch(q, b)

            def store(q):
                done = value(q + 1)
                sp.wait_ge(set_pool, 1)
                sp.wait_ge(o_ok, done)
                sp.dma_start(out_v[q], o_sb[:, :, :]).then_inc(stored, 16)

            def turn(g, b):
                if there(g + 2) and past(g + 2):
                    next_graph(g + 2, b)
                if there(g - 2):
                    store(g - 2)

            for g in range(FIRST, LOOP):
                turn(g, g % 2)
            with sp.Fori(LOOP, LOOP_END - 1, 2) as g:
                turn(g, 0)
                turn(g + 1, 1)
            for g in range(LOOP_END, END):
                turn(g, g % 2)
            sp.wait_ge(stored, 16 * GRAPHS)

        LIGHT_LOADS = 6
        SPLIT_LOADS = 8 + 6
        LOADS = 3 + 3 + 3

        @block.gpsimd
        def _(pool):
            pool.memset(bse[:, :], 0.0)
            pool.memset(br_a, 0.0)
            pool.memset(br_b, 0.0).then_inc(set_pool, 1)
            pool.memset(ident[:, :], 0.0).then_inc(set_pool, 1)
            pool.wait_ge(set_pool, 2)
            pool.affine_select(out=ident[:, :], in_=ident[:, :], compare_op=ALU.not_equal, fill=1.0, base=0,
                               pattern=[[-1, P]], channel_multiplier=1).then_inc(set_pool, 1)
            pool.memset(half_pow[:, :], -0.5).then_inc(set_pool, 1)
            pool.memset(w_se_pad[:, :], 0.0)
            pool.memset(w_ei[:, :], 0.0)
            pool.memset(ones[:, :], 1.0)
            pool.memset(br[:, :], 0.0)
            pool.memset(ones3[:, :], 0.0)
            pool.memset(neg_sq[:, :], 0.0)
            for t in (c1[:, :, :], c1_hi[:, :, :].bitcast(F32), c1_lo[:, :, :].bitcast(F32)):
                pool.memset(t[:, :, 0:HPAD], 0.0)
                ins = pool.memset(t[:, :, HPAD + HN:HLEN], 0.0)
            ins.then_inc(set_pool, 1)
            pool.wait_ge(set_pool, 5)
            for q in range(3):
                pool.memset(ones3[32 * q:32 * q + 1, :], 1.0)
                ins = pool.memset(neg_sq[0:SE, 32 * q + 3:32 * q + 5], -1.0)
            ins.then_inc(set_pool, 1)

            pool.wait_ge(set_pool, 6)

            def norm_powers():
                pool.wait_ge(set_dve, 2)
                pool.tensor_tensor(bn_rs[:, :], bn_ve[:, :], half_pow[:, 0:2], ALU.pow).then_inc(set_pool, 1)

            def norm(i, q):
                pool.wait_ge(ln_ve_ok[i], q + 1)
                pool.wait_ge(ln_nm_ok[i], q)
                pool.wait_ge(h_ok[i], q)
                pool.tensor_tensor(ln_rs[i][:, :], ln_ve[i][:, :], half_pow[:, 0:T], ALU.pow).then_inc(ln_rs_ok[i], 1)

            def dis_pow(q):
                pool.wait_ge(degs_ok, 2 * (q + 1))
                pool.wait_ge(dmask_ok, q)
                pool.wait_ge(y1_ok, q)
                pool.tensor_tensor(dis[:, :, :].rearrange("p a t -> p (a t)"),
                                   degs[:, :, :].rearrange("p a t -> p (a t)"), half_pow[:, :], ALU.pow
                                   ).then_inc(dis_ok, 1)

            def scale_g0(q):
                pool.wait_ge(t0_ok, q + 1)
                pool.wait_ge(dis_ok, q + 1)
                pool.wait_ge(agg0, q)
                pool.wait_ge(x1_ok, q)
                pool.tensor_tensor(g0[:, :, :], t0[:, :, :], wide(dis[:, 0, :]), ALU.mult).then_inc(g0_ok, 1)

            def scale_y0(q):
                pool.wait_ge(y0_ok, q + 1)
                pool.wait_ge(dmask_ok, q + 1)
                pool.wait_ge(x1_ok, q)
                pool.tensor_tensor(y0[:, :, :], y0[:, :, :], wide(dmask[:, :]), ALU.mult).then_inc(y0m_ok, 1)

            def residual1(q):
                pool.wait_ge(r0_ok, q + 1)
                pool.wait_ge(x1_ok, q + 1)
                pool.wait_ge(x2_ok, q)
                pool.tensor_tensor(r0[:, :, :], r0[:, :, :], x1[:, :, :], ALU.add).then_inc(r1_ok, 1)

            def kernel_adj(q, b, j):
                pool.wait_ge(ker_ok, 4 * q + j + 1)
                pool.wait_ge(aT_ok, 4 * (q + 1))
                pool.wait_ge(nmp, q)
                pool.tensor_tensor(kadj[:, j, :], ker[:, j % 2, :], aT[b][:, j, :], ALU.mult).then_inc(kadj_pool, 1)

            def residual2(q, b):
                pool.wait_ge(nn_ok, q + 1)
                pool.wait_ge(x2_ok, q + 1)
                pool.wait_ge(x3_ok, q)
                pool.tensor_tensor(x2[b][:, :, :], nn[:, :, :], x2[b][:, :, :], ALU.add).then_inc(xn_ok, 1)

            def mean_col(q):
                pool.wait_ge(set_pool, 1)
                pool.wait_ge(hT_ok[3], q + 1)
                pool.wait_ge(mean_lin, q)
                pool.tensor_scalar(hsB[:, :], ones[:, :], hsum[:, 0:1], 1.0 / N, ALU.mult, ALU.mult).then_inc(hsB_ok, 1)

            def guard(q):
                pool.wait_ge(set_pool, 1)
                pool.wait_ge(mxl_ok, q + 1)
                pool.wait_ge(ex_ok, q)
                pool.partition_all_reduce(cB[:, :], mxl[:, :], P, RMAX).then_inc(cB_ok, 1)

            def weigh_f(q):
                pool.wait_ge(ee_ok, q + 1)
                pool.wait_ge(gr_ok, q)
                pool.wait_ge(gp0_ok, q)
                pool.tensor_tensor(gf[:, :, :, 1, 0:HD], hx[:, :, 0:D].rearrange("p t (h d) -> p t h d", d=HD),
                                   ee[:, 1, :, :].unsqueeze(3).broadcast_to([P, T, HEADS, HD]), ALU.mult
                                   ).then_inc(gf_pool, 1)

            def third_part(q):
                pool.wait_ge(gp1_ok, q + 1)
                pool.wait_ge(head_sum, 4 * q)
                flat = "p t h s c -> p (t h s c)"
                pool.tensor_tensor(gp[2][:, :, :, :, :].rearrange(flat), gf[:, :, :, :, :].rearrange(flat),
                                   gp[1][:, :, :, :, :].rearrange(flat), ALU.subtract).then_inc(gp2_ok, 1)

            def fallback(q, b):
                pool.wait_ge(flag_ok, q + 1)
                pool.wait_ge(meanh_ok, q + 1)
                pool.wait_ge(stored, 16 * q)
                pool.tensor_tensor(fm[:, :, :].rearrange("p t (h d) -> p h t d", d=HD),
                                   flag[:, :, :].unsqueeze(3).broadcast_to([P, HEADS, T, HD]),
                                   meanh[:, :].rearrange("p (h d) -> p h d", d=HD).unsqueeze(2).broadcast_to([P, HEADS, T, HD]),
                                   ALU.mult).then_inc(fm_ok, 1)
                pool.wait_ge(fm_ok, q + 1)
                pool.wait_ge(o_ok, q)
                pool.tensor_tensor(fm[:, :, :], fm[:, :, :], x3[b][:, :, :], ALU.add).then_inc(xf_ok, 1)

            def finish(q):
                pool.wait_ge(o1_ok, q + 1)
                pool.wait_ge(xf_ok, q + 1)
                pool.tensor_tensor(o_sb[:, :, :].rearrange("p t (h d) -> p h t d", d=HD), o1,
                                   fm[:, :, :].rearrange("p t (h d) -> p h t d", d=HD), ALU.add).then_inc(o_ok, 1)

            def weigh_e(q):
                pool.wait_ge(sf_ok, 4 * (q + 1))
                pool.wait_ge(ee_ok, q + 1)
                pool.wait_ge(o_ok, q)
                pool.tensor_tensor(ue[:, :, :, :], sf[:, :, :, 0, :],
                                   ee[:, 2, :, :].rearrange("p t h -> p h t").unsqueeze(3).broadcast_to([P, HEADS, T, C]),
                                   ALU.mult).then_inc(ue_ok, 1)

            def light_a(q):
                dis_pow(q)
                norm(0, q)

            def turn(g, half, b):
                if there(g + 1):
                    scale_g0(g + 1)
                if there(g - 1):
                    norm(3, g - 1)
                if there(g + 1):
                    scale_y0(g + 1)
                if there(g - 2):
                    weigh_e(g - 2)
                if there(g + 1):
                    norm(1, g + 1)
                if there(g - 1):
                    mean_col(g - 1)
                if there(g):
                    kernel_adj(g, b, 1)
                if there(g - 1):
                    guard(g - 1)
                if there(g):
                    kernel_adj(g, b, 2)
                    kernel_adj(g, b, 3)
                if there(g - 1):
                    weigh_f(g - 1)
                if there(g + 2):
                    norm(0, g + 2)
                if there(g - 2):
                    fallback(g - 2, b)
                if there(g + 1):
                    residual1(g + 1)
                if there(g - 1):
                    third_part(g - 1)
                if there(g + 2):
                    dis_pow(g + 2)
                if there(g + 1):
                    norm(2, g + 1)
                if there(g - 2):
                    finish(g - 2)
                if first(g + 2):
                    norm_powers()
                if there(g):
                    residual2(g, b)

            run(pool, turn)

        @block.scalar
        def _(act):
            def norm(i, q, src):
                act.wait_ge(ln_nm_ok[i], q + 1)
                act.wait_ge(ln_rs_ok[i], q + 1)
                act.wait_ge(turned[i], q)
                if i == 2:
                    act.wait_ge(hmn_ok, q)
                for t in range(T):
                    ins = act.activation(h[i][:, t, :], src[:, t, :], ACT.Relu, bias=ln_nm[i][:, t:t + 1],
                                         scale=ln_rs[i][:, t:t + 1])
                ins.then_inc(h_ok[i], 1)

            def take_aT(q, b, j):
                act.wait_ge(a_turned, 4 * q + j + 1)
                if past(q - 1):
                    act.wait_ge(adj_on_ok, q - 1)
                    act.wait_ge(kadj_dve, q - 1)
                    act.wait_ge(kadj_pool, 3 * (q - 1))
                act.activation(aT[b][:, j, :], bank(LIGHT + j % 2), ACT.Copy).then_inc(aT_ok, 1)

            def take_hT(i, q, at, used):
                act.wait_ge(turned[i], q + 1)
                act.wait_ge(used, q)
                if i == 2:
                    act.wait_ge(u_ok, q)
                    act.wait_ge(h2_lo_ok, q)
                if i == 3:
                    act.wait_ge(hsB_ok, q)
                    act.activation(hT[i][:, :], bank(at), ACT.Copy, accum_out=hsum[:, 0:1]).then_inc(hT_ok[i], 1)
                else:
                    act.activation(hT[i][:, :], bank(at), ACT.Copy).then_inc(hT_ok[i], 1)

            def take_h2_hi(q):
                act.wait_ge(turned[2], q + 1)
                act.wait_ge(gru, 4 * q)
                act.activation(h2_hi[:, :], bank(HEAVY + 1), ACT.Copy).then_inc(h2_hi_ok, 1)

            def take_c1_hi(q):
                act.wait_ge(conv1, q + 1)
                act.wait_ge(conv2, q)
                act.activation(c1_hi[:, :, HPAD:HPAD + HN], by_parity(bank(HEAVY + 2)), ACT.Relu, bias=bn_sh[:, 0:1]
                               ).then_inc(c1_hi_ok, 1)

            def take_c1(q):
                act.wait_ge(conv1, q + 1)
                act.wait_ge(c_lo_ok, q)
                act.activation(c1[:, :, HPAD:HPAD + HN], by_parity(bank(HEAVY + 2)), ACT.Relu, bias=bn_sh[:, 0:1]
                               ).then_inc(c1_ok, 1)

            def sums_hi(q):
                act.wait_ge(xs_ok, q + 1)
                act.wait_ge(conv2, q)
                act.activation(xs_hi[:, :], xs[:, :], ACT.Copy).then_inc(xs_hi_ok, 1)

            def square_s(q):
                act.wait_ge(s_lin, q + 1)
                act.wait_ge(lr_ok, 2 * q)
                act.activation(s_sq[:, :], bank(HEAVY), ACT.Square, bias=bse[:, 0:1]).then_inc(s_sq_ok, 1)

            def sides(q):
                act.wait_ge(s_all, q + 1)
                act.wait_ge(lr_ok, 2 * q)
                act.wait_ge(nmp, q)
                act.activation(left_f[:, :], bank(HEAVY), ACT.Identity, bias=left_sc[:, 1:2],
                               scale=left_sc[:, 0:1]).then_inc(left_f_ok, 1)
                act.activation(right_f[:, :], bank(HEAVY), ACT.Identity, bias=right_sc[:, 1:2],
                               scale=right_sc[:, 0:1]).then_inc(right_f_ok, 1)

            def sides_hi(q):
                act.wait_ge(s_all, q + 1)
                act.wait_ge(dist, 4 * q)
                act.activation(left[:, :], bank(HEAVY), ACT.Identity, bias=left_sc[:, 1:2], scale=left_sc[:, 0:1]
                               ).then_inc(lr_hi_ok, 1)
                act.activation(right[:, :], bank(HEAVY), ACT.Identity, bias=right_sc[:, 1:2], scale=right_sc[:, 0:1]
                               ).then_inc(lr_hi_ok, 1)

            def relu_msg(q):
                act.wait_ge(msg_b_ok, q + 1)
                act.wait_ge(nmp, q)
                act.activation(msg, msg_b, ACT.Relu).then_inc(msg_ok, 1)

            def exps(q, j):
                act.wait_ge(dist, 4 * q + j + 1)
                if j == 2:
                    act.wait_ge(kadj_dve, q + 1)
                elif j or past(q):
                    act.wait_ge(kadj_pool, 3 * q + (-1, 0, None, 1)[j])
                act.activation(ker[:, j % 2, :], bank(HEAVY), ACT.Exp).then_inc(ker_ok, 1)

            def take_n(q):
                act.wait_ge(nmp, q + 1)
                act.wait_ge(gru, 4 * q)
                act.activation(n_hi[:, :], bank(HEAVY), ACT.Copy).then_inc(n_hi_ok, 1)

            def relu_conv(q):
                act.wait_ge(u_ok, q + 1)
                act.wait_ge(gru, 4 * q)
                act.activation(by_parity(c_hi[:, :]), u, ACT.Relu).then_inc(c_hi_ok, 1)

            def gates(q, t):
                act.wait_ge(gru, 4 * q + t + 1)
                act.wait_ge(zd_ok, q)
                act.activation(rz[:, t, :], bank(GRU_BANK[t])[:, D:3 * D], ACT.Tanh, scale=0.5).then_inc(rz_ok, 1)

            def new_gate(q):
                act.wait_ge(q2_ok, 4 * (q + 1))
                act.wait_ge(xn_ok, q)
                act.activation(nn[:, :, :], q2[:, :, :], ACT.Tanh).then_inc(nn_ok, 1)

            def take_hx(q, i):
                act.wait_ge(hx_lin, 2 * q + i + 1)
                act.wait_ge(S_ok, 4 * q)
                act.wait_ge(gf_dve, q)
                act.wait_ge(gf_pool, q)
                act.activation(hx[:, 2 * i:2 * i + 2, :], tiles(bank(LAST + 1 + i)[:, 0:2 * WX], WX), ACT.Copy
                               ).then_inc(hx_ok, 1)

            def take_mean(q):
                act.wait_ge(mean_lin, q + 1)
                act.wait_ge(fm_ok, q)
                act.activation(meanh[:, :], bank(LAST)[:, 0:P], ACT.Copy).then_inc(meanh_ok, 1)

            def take_ei(q):
                act.wait_ge(ei_lin, q + 1)
                act.wait_ge(ei_rows, 4 * q)
                act.activation(eh[:, :], bank(LAST + 1), ACT.Copy).then_inc(eh_hi_ok, 1)

            def take_rows(q, i):
                act.wait_ge(ei_rows, 4 * q + i + 1)
                act.wait_ge(S_ok, 4 * q)
                act.activation(nei[:, i, :], bank(LAST + 2 - 2 * (i % 2)), ACT.Copy).then_inc(nei_ok, 1)

            def exp_e(q):
                act.wait_ge(ex_ok, q + 1)
                act.wait_ge(gf_dve, q)
                act.wait_ge(v2_ok, q)
                act.wait_ge(ue_ok, q)
                act.activation(ee[:, :, :, :].rearrange("p k t h -> p (k t h)"),
                               ex[:, :, :, :].rearrange("p k t h -> p (k t h)"), ACT.Exp).then_inc(ee_ok, 1)

            flat = "p t h s c -> p (t h s c)"

            def first_part(q):
                act.wait_ge(gf_dve, q + 1)
                act.wait_ge(gf_pool, q + 1)
                act.wait_ge(head_sum, 4 * q)
                act.activation(gp[0][:, :, :, :, :].rearrange(flat), gf[:, :, :, :, :].rearrange(flat), ACT.Copy
                               ).then_inc(gp0_ok, 1)

            def second_part(q):
                act.wait_ge(gr_ok, q + 1)
                act.activation(gp[1][:, :, :, :, :].rearrange(flat), gf[:, :, :, :, :].rearrange(flat), ACT.Copy
                               ).then_inc(gp1_ok, 1)

            def take_all(q, i):
                act.wait_ge(all_sum, 2 * q + i + 1)
                act.wait_ge(o1_ok, q)
                act.activation(bf[:, 2 * i:2 * i + 2, :, :].rearrange("p t h c -> p (t h c)"),
                               bank(LAST + 1 - i)[:, 0:2 * HEADS * C], ACT.Copy).then_inc(bf_ok, 1)

            def take_head(q, i):
                act.wait_ge(head_sum, 4 * q + i + 1)
                act.wait_ge(v1_ok, q)
                act.wait_ge(ue_ok, q)
                act.activation(sf[:, i, :, :, :].rearrange("p t s c -> p (t s c)"),
                               bank(HEAD_BANK[i])[:, 0:T * 2 * C], ACT.Copy).then_inc(sf_ok, 1)

            def weights_hi(n):
                i, end, at = W_PARTS[n]
                act.wait_ge(set_pe, n + 2)
                act.activation(w_hi[:, i:end, :].rearrange("p a o -> p (a o)"), slots(at, end - i), ACT.Copy
                               ).then_inc(set_act, 1)

            def set_up_done():
                act.wait_ge(set_dve, SET_DVE)

            def turn(g, half, b):
                if there(g + 1):
                    take_aT(g + 1, 1 - b, 1)
                if there(g - 2):
                    take_rows(g - 2, 2)
                if there(g - 1):
                    new_gate(g - 1)
                if there(g - 2):
                    take_rows(g - 2, 3)
                if there(g + 1):
                    take_aT(g + 1, 1 - b, 2)
                    take_aT(g + 1, 1 - b, 3)
                if there(g):
                    norm(2, g, x2[b])
                if there(g - 2):
                    take_all(g - 2, 0)
                if there(g + 1):
                    take_hT(0, g + 1, LIGHT, lin0)
                if there(g):
                    take_h2_hi(g)
                    take_hT(2, g, HEAVY + 1, msg_lin)
                if there(g - 2):
                    take_all(g - 2, 1)
                if there(g):
                    square_s(g)
                    take_c1_hi(g)
                if there(g - 2):
                    take_head(g - 2, 0)
                    take_head(g - 2, 1)
                if there(g):
                    take_c1(g)
                if there(g - 2):
                    take_head(g - 2, 2)
                if there(g):
                    sides_hi(g)
                    sides(g)
                if there(g - 1):
                    norm(3, g - 1, x3[1 - b])
                if there(g - 2):
                    take_head(g - 2, 3)
                if there(g):
                    sums_hi(g)
                if there(g - 1):
                    take_hT(3, g - 1, LAST, ei_lin)
                if there(g):
                    exps(g, 0)
                if there(g - 1):
                    take_hx(g - 1, 0)
                if there(g):
                    exps(g, 1)
                if there(g - 1):
                    take_hx(g - 1, 1)
                if first(g + 1):
                    weights_hi(0)
                if there(g):
                    exps(g, 2)
                if first(g + 1):
                    weights_hi(1)
                if there(g + 1):
                    norm(1, g + 1, x1)
                if there(g - 1):
                    take_ei(g - 1)
                if there(g):
                    exps(g, 3)
                if there(g - 1):
                    exp_e(g - 1)
                if there(g + 1):
                    take_hT(1, g + 1, LIGHT + 1, lin1)
                if there(g):
                    relu_msg(g)
                if there(g - 1):
                    first_part(g - 1)
                if there(g):
                    relu_conv(g)
                    take_n(g)
                if there(g - 1):
                    take_mean(g - 1)
                    take_rows(g - 1, 0)
                if there(g):
                    gates(g, 0)
                if there(g - 1):
                    take_rows(g - 1, 1)
                    second_part(g - 1)
                if first(g + 1):
                    weights_hi(2)
                    set_up_done()
                if there(g):
                    gates(g, 1)
                if there(g + 2):
                    take_aT(g + 2, b, 0)
                    norm(0, g + 2, x_in[b])
                if there(g):
                    gates(g, 2)
                    gates(g, 3)

            run(act, turn)

        @block.tensor
        def _(pe):
            def turn_weight(i, src, n=P):
                return pe.transpose(slots(i, 1)[:, 0:n], src, ident[0:n, 0:n])

            pe.wait_ge(light_loaded, 16 * LIGHT_LOADS)
            pe.wait_ge(set_pool, 3)
            turn_weight(28, nat_lin[:, 0, :])
            turn_weight(29, nat_lin[:, 1, :])
            turn_weight(30, mask_nat[:, :], GRAPHS * T).then_inc(set_pe, 1)
            pe.wait_ge(set_dve, 1)

            def turn_weights(n):
                if n == 0:
                    pe.wait_ge(set_dve, 4)
                    turn_weight(8, nat_lin[:, 2, :])
                    turn_weight(9, se_nat[:, :], SE)
                    turn_weight(10, nat_lin[:, 3, :])
                    for m, r in enumerate((2, 0, 1)):
                        turn_weight(11 + m, nat_ih[:, 2 * r, :])
                        turn_weight(14 + m, nat_ih[:, 2 * r + 1, :])
                    for r in range(3):
                        ins = turn_weight(17 + r, nat_hh[:, r, :])
                else:
                    if n == 2:
                        pe.wait_ge(set_dve, 10)
                    i0, end, at = W_PARTS[n]
                    for i in range(i0, end):
                        if i < 10 + TAPS:
                            src = c2nat.rearrange("p (i k) -> p i k", k=TAPS)[:, :, i - 10]
                        else:
                            src = c2sum[(i - 10 - TAPS) // T][:, (i - 10 - TAPS) % T, :]
                        ins = turn_weight(at + i - i0, src)
                ins.then_inc(set_pe, 1)

            def set_up_done():
                pe.wait_ge(set_dve, SET_DVE)

            def split_mm(dst, wh, wl, mh, ml, start, stop):
                pe.matmul(dst, wh, mh, start=start, stop=False, skip_group_check=True)
                pe.matmul(dst, wh, ml, start=False, stop=False, skip_group_check=True)
                return pe.matmul(dst, wl, mh, start=False, stop=stop, skip_group_check=True)

            def turn_a(q, j):
                if j == 0:
                    pe.wait_ge(a_loaded, 16 * (q + 1))
                    pe.wait_ge(g1_ok, q)
                if j == 1:
                    pe.wait_ge(y1_ok, q)
                if j >= 2:
                    pe.wait_ge(aT_ok, 4 * q + j - 1)
                for t in range(T):
                    ins = pe.transpose(bank(LIGHT + j % 2)[:, t * P:(t + 1) * P], a_nat[:, t, j * P:(j + 1) * P],
                                       ident[:, :])
                ins.then_inc(a_turned, 1)

            def turn_h(i, q, at):
                if i == 2 and past(q):
                    pe.wait_ge(q2_ok, 4 * q - 2)
                if i == 3 and past(q):
                    pe.wait_ge(sf_ok, 4 * q - 1)
                pe.wait_ge(h_ok[i], q + 1)
                for t in range(T):
                    ins = pe.transpose(bank(at)[:, t * P:(t + 1) * P], h[i][:, t, :], ident[:, :])
                ins.then_inc(turned[i], 1)

            def linear(at, i, w, done, q):
                if i == 2:
                    pe.wait_ge(lr_ok, 2 * (q + 1))
                pe.wait_ge(hT_ok[i], q + 1)
                for t in range(T):
                    ins = pe.matmul(bank(at)[:, t * P:(t + 1) * P], hT[i][:, t * P:(t + 1) * P], w, start=True,
                                    stop=True, skip_group_check=True)
                ins.then_inc(done, 1)

            def aggregate(at, b, g, done):
                for t in range(T):
                    for j in range(T):
                        ins = pe.matmul(bank(at)[:, t * P:(t + 1) * P], aT[b][:, j, t * P:(t + 1) * P], g[:, j, :],
                                        start=(j == 0), stop=(j == T - 1), skip_group_check=True)
                ins.then_inc(done, 1)

            def light1(q, b):
                pe.wait_ge(aT_ok, 4 * q + 3)
                turn_h(0, q, LIGHT)

            def light2(q, b):
                pe.wait_ge(aT_ok, 4 * (q + 1))
                linear(LIGHT + 1, 0, wT[:, 0, :], lin0, q)

            def light3(q, b):
                pe.wait_ge(g0_ok, q + 1)
                aggregate(LIGHT, b, g0, agg0)

            def light4(q, b):
                pe.wait_ge(t0_ok, q + 1)
                turn_h(1, q, LIGHT + 1)

            def light5(q, b):
                pe.wait_ge(y0_ok, q + 1)
                linear(LIGHT, 1, wT[:, 1, :], lin1, q)

            def light6(q, b):
                pe.wait_ge(g1_ok, q + 1)
                aggregate(LIGHT + 1, b, g1, agg1)

            B0, B1, B2 = HEAVY, HEAVY + 1, HEAVY + 2

            def do_conv1(q):
                if past(q):
                    pe.wait_ge(q2_ok, 4 * q - 1)
                pe.wait_ge(h2_lo_ok, q + 1)
                split_mm(bank(B2), w_hi[:, 0, :], w_lo[:, 0, :], h2_hi[:, :], h2_lo[:, :], True, True
                         ).then_inc(conv1, 1)

            def do_s(q):
                pe.wait_ge(q2_ok, 4 * q)
                pe.wait_ge(h2_lo_ok, q + 1)
                split_mm(bank(B0), w_se_hi[:, :], w_se_lo[:, :], h2_hi[:, :], h2_lo[:, :], True, False
                         ).then_inc(s_lin, 1)

            def do_sq(q):
                pe.wait_ge(s_sq_ok, q + 1)
                pe.matmul(bank(B0), neg_sq[:, :], s_sq[:, :], start=False, stop=True, skip_group_check=True
                          ).then_inc(s_all, 1)

            def do_dist(q, j):
                if j == 0:
                    pe.wait_ge(lr_ok, 2 * (q + 1))
                    pe.wait_ge(msg_b_ok, q + 1)
                else:
                    pe.wait_ge(ker_ok, 4 * q + j)
                pe.matmul(bank(B0), left[:, j * P:(j + 1) * P], right[:, :], start=True,
                              stop=True, skip_group_check=True).then_inc(dist, 1)

            def do_conv2(q, ks):
                for k in ks:
                    if k < O_TAPS:
                        i, w, dst = k, 10 + 2 * k + 1, bank(B1)[:, HN:N]
                        hi, lo = (x[:, 1, i:i + HN] for x in (c1_hi, c1_lo))
                        if i == 0:
                            pe.wait_ge(hT_ok[2], q + 1)
                            pe.wait_ge(h2_hi_ok, q + 1)
                            pe.wait_ge(c1_lo_ok, q + 1)
                    elif k < O_TAPS + E_TAPS:
                        i = k - O_TAPS
                        w, dst = 10 + 2 * i, bank(B2)[:, 0:HN + 2]
                        hi, lo = (x[:, 0, i:i + HN + 2] for x in (c1_hi, c1_lo))
                    else:
                        i = k - O_TAPS - E_TAPS
                        w, dst = 10 + TAPS + i if i < O_TAPS else 10 + TAPS - 1, bank(B1)[:, 0:HN]
                        hi, lo = (x[:, i:i + HN] for x in (xs_hi, xs_lo))
                        if i == 0:
                            pe.wait_ge(xs_lo_ok, q + 1)
                    last = i == (O_TAPS if k < O_TAPS else E_TAPS) - 1
                    ins = split_mm(dst, w_hi[:, w, :], w_lo[:, w, :], hi, lo, i == 0, last)
                    if k == PIECES - 1:
                        ins.then_inc(conv2, 1)

            def do_nmp(q):
                pe.wait_ge(msg_ok, q + 1)
                pe.wait_ge(kadj_dve, q + 1)
                pe.wait_ge(kadj_pool, 3 * (q + 1))
                pe.wait_ge(ker_ok, 4 * (q + 1))
                for j in range(T):
                    ins = pe.matmul(bank(B0), msg[:, j, :], kadj[:, j, :], start=(j == 0), stop=(j == T - 1),
                                    skip_group_check=True)
                ins.then_inc(nmp, 1)

            def gru_part(q, t, at, hi, lo, i, last=False):
                dst = bank(GRU_BANK[t])[:, at:at + 3 * D]
                c = slice(t * P, (t + 1) * P)
                wh = w_hi[:, i:i + 3, :].rearrange("p a o -> p (a o)")
                wl = w_lo[:, i:i + 3, :].rearrange("p a o -> p (a o)")
                pe.matmul(dst, hi[:, c], wh, start=False, stop=False, skip_group_check=True)
                pe.matmul(dst, hi[:, c], wl, start=False, stop=False, skip_group_check=True)
                return pe.matmul(dst, lo[:, c], wh, start=False, stop=last, skip_group_check=True)

            def do_gru_h(q, t):
                if t == 0:
                    pe.wait_ge(n_lo_ok, q + 1)
                if t in (1, 2):
                    pe.wait_ge(u_ok, q + 1)
                if t == 3:
                    pe.wait_ge(q2_ok, 4 * q + 1)
                pe.matmul(bank(GRU_BANK[t]), ones3[:, :], br[:, :], start=True, stop=False, skip_group_check=True)
                gru_part(q, t, D, h2_hi, h2_lo, 7)

            def do_gru_n(q, t):
                pe.wait_ge(n_lo_ok, q + 1)
                gru_part(q, t, 0, n_hi, n_lo, 4)

            def do_gru_c(q, t):
                pe.wait_ge(c_lo_ok, q + 1)
                gru_part(q, t, 0, c_hi, c_lo, 1, True).then_inc(gru, 1)

            C0, C1, C2 = LAST, LAST + 1, LAST + 2

            def do_hx(q, i):
                pe.wait_ge(hT_ok[3], q + 1)
                if i == 1:
                    pe.wait_ge(sf_ok, 4 * q)
                for t in range(2):
                    c = slice((2 * i + t) * P, (2 * i + t + 1) * P)
                    ins = pe.matmul(bank(C1 + i)[:, t * WX:(t + 1) * WX], hT[3][:, c], wx[:, :], start=True,
                                    stop=True, skip_group_check=True)
                ins.then_inc(hx_lin, 1)

            def do_mean(q):
                pe.wait_ge(hsB_ok, q + 1)
                pe.matmul(bank(C0)[:, 0:P], hsB[:, :], wx[:, 0:D], start=True, stop=True, skip_group_check=True
                          ).then_inc(mean_lin, 1)

            def do_ei(q):
                pe.wait_ge(hx_ok, 2 * q + 1)
                pe.matmul(bank(C1), w_ei[:, :], hT[3][:, :], start=True, stop=True, skip_group_check=True
                          ).then_inc(ei_lin, 1)

            def do_rows(q, i):
                if i == 0:
                    pe.wait_ge(eh_ok, q + 1)
                    pe.wait_ge(hx_ok, 2 * q + 2)
                if i == 1:
                    pe.wait_ge(meanh_ok, q + 1)
                if i >= 2:
                    pe.wait_ge(nei_ok, 4 * q + i - 1)
                pe.matmul(bank(C2 - 2 * (i % 2)), sel[:, i, :], eh[:, :], start=True, stop=True, skip_group_check=True
                              ).then_inc(ei_rows, 1)

            def do_all(q, b, i):
                pe.wait_ge(gp2_ok, q + 1)
                pe.wait_ge(adj_on_ok, q + 1)
                if i == 0:
                    pe.wait_ge(eh_ok, q + 1)
                else:
                    pe.wait_ge(nei_ok, 4 * (q + 1))
                for t in range(2):
                    tn = 2 * i + t
                    dst = tiles(bank(C1 - i)[:, t * HEADS * C:(t + 1) * HEADS * C], C)
                    for j in range(T):
                        for p in range(3):
                            ins = pe.matmul(dst, adj_on[b][:, j, tn * P:(tn + 1) * P], gp[p][:, j, :, 1, :],
                                            start=(j == 0 and p == 0), stop=(j == T - 1 and p == 2),
                                            skip_group_check=True)
                ins.then_inc(all_sum, 1)

            def do_head(q, i):
                if i == 0:
                    pe.wait_ge(gp2_ok, q + 1)
                    pe.wait_ge(nei_ok, 4 * q + 3)
                if i == 1:
                    pe.wait_ge(bf_ok, 2 * q + 1)
                if i == 2:
                    pe.wait_ge(bf_ok, 2 * q + 2)
                if i == 3:
                    pe.wait_ge(sf_ok, 4 * q + 1)
                pe.wait_ge(S_ok, 4 * q + i + 1)
                for tn in range(T):
                    dst = bank(HEAD_BANK[i])[:, tn * 2 * C:(tn + 1) * 2 * C]
                    for j in range(T):
                        for p in range(3):
                            ins = pe.matmul(dst, S[i % 2][:, j, tn * P:(tn + 1) * P],
                                            gp[p][:, j, i, :, :].rearrange("p s c -> p (s c)"),
                                            start=(j == 0 and p == 0), stop=(j == T - 1 and p == 2),
                                            skip_group_check=True)
                ins.then_inc(head_sum, 1)

            def turn(g, half, b):
                if there(g):
                    do_conv2(g, range(19, 22))
                if there(g + 1):
                    light4(g + 1, 1 - b)
                if there(g):
                    do_conv2(g, range(22, PIECES))
                if there(g + 1):
                    light5(g + 1, 1 - b)
                if there(g):
                    do_nmp(g)
                if there(g - 1):
                    do_mean(g - 1)
                    do_rows(g - 1, 0)
                if there(g + 1):
                    light6(g + 1, 1 - b)
                if there(g - 1):
                    do_rows(g - 1, 1)
                if there(g):
                    do_gru_h(g, 0)
                if there(g + 2):
                    turn_a(g + 2, 0)
                if there(g):
                    do_gru_n(g, 0)
                    do_gru_c(g, 0)
                    do_gru_h(g, 1)
                    do_gru_n(g, 1)
                    do_gru_c(g, 1)
                    do_gru_h(g, 2)
                    do_gru_n(g, 2)
                    do_gru_c(g, 2)
                    do_gru_h(g, 3)
                    do_gru_n(g, 3)
                    do_gru_c(g, 3)
                if there(g - 1):
                    do_rows(g - 1, 2)
                if there(g + 2):
                    turn_a(g + 2, 1)
                if there(g - 1):
                    do_rows(g - 1, 3)
                if there(g + 2):
                    turn_a(g + 2, 2)
                if there(g - 1):
                    do_all(g - 1, 1 - b, 0)
                if there(g + 2):
                    turn_a(g + 2, 3)
                if there(g - 1):
                    do_head(g - 1, 0)
                if first(g + 1):
                    set_up_done()
                if there(g + 2):
                    light1(g + 2, b)
                if there(g - 1):
                    do_all(g - 1, 1 - b, 1)
                if there(g + 1):
                    turn_h(2, g + 1, B1)
                if there(g - 1):
                    do_head(g - 1, 1)
                if there(g + 2):
                    light2(g + 2, b)
                if there(g + 1):
                    do_s(g + 1)
                    do_conv1(g + 1)
                if there(g - 1):
                    do_head(g - 1, 2)
                if first(g + 2):
                    turn_weights(0)
                if there(g + 1):
                    do_sq(g + 1)
                if there(g + 2):
                    light3(g + 2, b)
                if there(g - 1):
                    do_head(g - 1, 3)
                if there(g + 1):
                    do_conv2(g + 1, range(0, 6))
                    linear(B0, 2, wT[:, 2, :], msg_lin, g + 1)
                    do_conv2(g + 1, range(6, 7))
                if first(g + 2):
                    turn_weights(1)
                if there(g):
                    turn_h(3, g, C0)
                if there(g + 1):
                    do_conv2(g + 1, range(7, 9))
                    do_dist(g + 1, 0)
                    do_conv2(g + 1, range(9, 11))
                if first(g + 2):
                    turn_weights(2)
                if there(g + 1):
                    do_conv2(g + 1, range(11, 12))
                    do_dist(g + 1, 1)
                if there(g):
                    do_hx(g, 0)
                if there(g + 1):
                    do_conv2(g + 1, range(12, 13))
                if there(g):
                    do_hx(g, 1)
                if there(g + 1):
                    do_conv2(g + 1, range(13, 14))
                if there(g):
                    do_ei(g)
                if there(g + 1):
                    do_conv2(g + 1, range(14, 15))
                    do_dist(g + 1, 2)
                    do_conv2(g + 1, range(15, 19))
                    do_dist(g + 1, 3)

            run(pe, turn)

        @block.vector
        def _(dve):
            dve.wait_ge(light_loaded, 16 * LIGHT_LOADS)
            dve.tensor_scalar(alpha_eff[:, :], alphaB[:, :], 1e-10, None, ALU.max)
            dve.wait_ge(set_pe, 1)
            dve.tensor_copy(wT[:, 0:2, :], tiles(slots(28, 2)))
            dve.tensor_copy(mask_sb[:, :], slots(30, 1)[:, 0:GRAPHS * T]).then_inc(set_dve, 1)
            dve.wait_ge(set_dve, 1)

            def norm_variances():
                dve.wait_ge(split_loaded, 16 * SPLIT_LOADS)
                dve.wait_ge(set_pool, 6)
                dve.tensor_scalar(bn_ve[:, :], bn[:, :, 3], BN_EPS, None, ALU.add).then_inc(set_dve, 1)

            def scale_weights():
                dve.wait_ge(set_pool, 7)
                dve.tensor_tensor(bn_sc[:, :], bn_rs[:, :], bn[:, :, 0], ALU.mult).then_inc(set_dve, 1)
                dve.wait_ge(set_dve, 3)
                dve.tensor_tensor(bn_ms[:, :], bn_sc[:, :], bn[:, :, 2], ALU.mult)
                dve.tensor_scalar(nat_lin[:, 3, :], nat_lin[:, 3, :], bn_sc[:, 0:1], None, ALU.mult)
                dve.tensor_scalar(c2nat, c2nat, bn_sc[:, 1:2], None, ALU.mult).then_inc(set_dve, 1)

            def small_weights():
                dve.wait_ge(set_dve, 4)
                dve.wait_ge(set_loaded, 16 * LOADS)
                dve.tensor_tensor(bn_sh[:, :], bn[:, :, 1], bn_ms[:, :], ALU.subtract)
                hots = ident[:, 0:96].rearrange("p (q c) -> p q c", c=32)
                dve.tensor_reduce(hot[:, 0:1], hots[:, :, 0:3], AX.XY, ALU.add)
                dve.tensor_reduce(hot[:, 1:2], hots[:, :, 3:4], AX.XY, ALU.add)
                dve.tensor_reduce(hot[:, 2:3], hots[:, :, 4:5], AX.XY, ALU.add)
                dve.tensor_tensor(sel_col[:, :], ident[:, 0:HEADS], ident[:, 32:32 + HEADS], ALU.add)
                w3h = wx[:, 0:D].rearrange("p (h d) -> p h d", d=HD)
                for s in range(2):
                    dve.tensor_tensor(wa[:, s, :, :], w3h, aB[:, :, s, :], ALU.mult)
                taps = c2nat.rearrange("p (i k) -> p k i", k=TAPS)
                for n in range(2):
                    dve.tensor_tensor(c2sum[n][:, :, :], taps[:, 8 * n:8 * n + 8:2, :], taps[:, 8 * n + 1:8 * n + 9:2, :],
                                      ALU.add)
                dve.tensor_tensor(br_a, br_a, br_b, ALU.add).then_inc(set_dve, 1)
                dve.wait_ge(set_dve, 5)
                dve.tensor_copy(br_p[:, 0, :], br_a)
                dve.scalar_tensor_tensor(out=left_sc[:, 0:1], in0=hot[:, 0:1], scalar=2.0, in1=hot[:, 1:2],
                                         op0=ALU.mult, op1=ALU.add)
                dve.scalar_tensor_tensor(out=left_sc[:, 1:2], in0=bse[:, :], scalar=2.0, in1=hot[:, 2:3],
                                         op0=ALU.mult, op1=ALU.add)
                dve.tensor_tensor(right_sc[:, 0:1], hot[:, 0:1], hot[:, 2:3], ALU.add)
                dve.tensor_tensor(right_sc[:, 1:2], bse[:, :], hot[:, 1:2], ALU.add)
                dve.tensor_copy(sel[:, :, :], sel_col[:, :].unsqueeze(2).broadcast_to([P, HEADS, P]))
                dve.tensor_reduce(wx[:, D:D + HEADS], wa[:, 1, :, :], AX.X, ALU.add)
                dve.tensor_reduce(wx[:, D + HEADS:WX], wa[:, 0, :, :], AX.X, ALU.add).then_inc(set_dve, 1)
                dve.wait_ge(set_dve, 6)
                for q in range(2):
                    dve.tensor_scalar(w_ei[:, 32 * q:32 * q + HEADS], wx[:, D + HEADS:WX], -1.0, None, ALU.mult)
                dve.tensor_tensor(br_b, br_a, br_p[:, 0, :], ALU.subtract).then_inc(set_dve, 1)
                dve.wait_ge(set_dve, 7)
                dve.tensor_copy(br_p[:, 1, :], br_b)
                dve.tensor_copy(br[0:1, :], br_p[0:1, 0, :]).then_inc(set_dve, 1)

            def weights_lo(n):
                i, end, at = W_PARTS[n]
                dve.wait_ge(set_act, n + 1)
                if n == 0:
                    dve.tensor_copy(wT[:, 2, :], slots(8, 1))
                    for q in range(3):
                        dve.tensor_copy(w_se_pad[:, 32 * q:32 * q + SE], slots(9, 1)[:, 0:SE])
                dve.tensor_tensor(w_lo[:, i:end, :].rearrange("p a o -> p (a o)"), slots(at, end - i),
                                  w_hi[:, i:end, :].rearrange("p a o -> p (a o)").bitcast(F32), ALU.subtract
                                  ).then_inc(set_dve, 1)

            def bias_rows():
                dve.wait_ge(set_dve, 11)
                dve.tensor_copy(w_se_hi[:, :], w_se_pad[:, :])
                dve.tensor_tensor(br_p[:, 2, :], br_b, br_p[:, 1, :], ALU.subtract)
                dve.tensor_copy(br[32:33, :], br_p[32:33, 1, :]).then_inc(set_dve, 1)
                dve.wait_ge(set_dve, 12)
                dve.tensor_tensor(w_se_lo[:, :], w_se_pad[:, :], w_se_hi[:, :].bitcast(F32), ALU.subtract)
                dve.tensor_copy(br[64:65, :], br_p[64:65, 2, :]).then_inc(set_dve, 1)

            def stats(i, q, src, half=None, b=None):
                if i == 0:
                    dve.wait_ge(x_loaded[b], 16 * (half + 1))
                    dve.wait_ge(rowsum_ok, q + 1)
                else:
                    dve.wait_ge((x1_ok, x2_ok, x3_ok)[i - 1], q + 1)
                dve.wait_ge(ln_mv_ok[i], q)
                for t in range(T):
                    ins = dve.bn_stats(ln_st[i][:, t, :], src[:, t, :])
                ins.then_inc(ln_st_ok[i], 1)

            def variance(i, q):
                dve.wait_ge(set_pool, 1)
                dve.wait_ge(ln_st_ok[i], q + 1)
                dve.wait_ge(ln_nm_ok[i], q)
                dve.wait_ge(ln_ve_ok[i], q)
                for t in range(T):
                    ins = dve.bn_aggr(ln_mv[i][:, t, :], ln_st[i][:, t, :])
                ins.then_inc(ln_mv_ok[i], 1)
                dve.wait_ge(ln_mv_ok[i], q + 1)
                dve.wait_ge(ln_rs_ok[i], q)
                dve.tensor_scalar(ln_ve[i][:, :], ln_mv[i][:, :, 1], LN_EPS, None, ALU.add).then_inc(ln_ve_ok[i], 1)

            def shift(i, q):
                dve.wait_ge(ln_rs_ok[i], q + 1)
                dve.wait_ge(h_ok[i], q)
                dve.scalar_tensor_tensor(out=ln_nm[i][:, :], in0=ln_mv[i][:, :, 0], scalar=-1.0, in1=ln_rs[i][:, :],
                                         op0=ALU.mult, op1=ALU.mult).then_inc(ln_nm_ok[i], 1)

            def degrees(q):
                dve.wait_ge(a_loaded, 16 * (q + 1))
                dve.wait_ge(degs_ok, 2 * q)
                dve.tensor_reduce(rowsum[:, :], a_nat[:, :, :], AX.X, ALU.add).then_inc(rowsum_ok, 1)

            def degree_sums(q):
                dve.wait_ge(rowsum_ok, q + 1)
                dve.wait_ge(dis_ok, q)
                dve.tensor_scalar(degs[:, 0, :], rowsum[:, :], 1.0, 1e-8, ALU.add, ALU.add).then_inc(degs_ok, 1)
                dve.scalar_tensor_tensor(out=degs[:, 1, :], in0=rowsum[:, :], scalar=0.0, in1=rowsum[:, :],
                                         op0=ALU.is_equal, op1=ALU.add).then_inc(degs_ok, 1)

            def mask_dis(q):
                dve.wait_ge(dis_ok, q + 1)
                dve.wait_ge(y0m_ok, q)
                dve.tensor_tensor(dmask[:, :], dis[:, 0, :], mask_sb[:, bass.ds(q * T, T)], ALU.mult
                                  ).then_inc(dmask_ok, 1)

            def bias0(q):
                dve.wait_ge(lin0, q + 1)
                dve.wait_ge(g0_ok, q)
                dve.tensor_tensor(t0[:, :, :], tiles(bank(LIGHT + 1)), b0B[:, :].unsqueeze(1).broadcast_to([P, T, D]),
                                  ALU.add).then_inc(t0_ok, 1)

            def self0(q):
                dve.wait_ge(agg0, q + 1)
                dve.wait_ge(g0_ok, q + 1)
                dve.wait_ge(y0m_ok, q)
                dve.tensor_tensor(y0[:, :, :], tiles(bank(LIGHT)), g0[:, :, :], ALU.add).then_inc(y0_ok, 1)

            def add0(q, b):
                dve.wait_ge(y0m_ok, q + 1)
                dve.wait_ge(h_ok[1], q)
                dve.wait_ge(r1_ok, q)
                dve.wait_ge(h_ok[0], q + 1)
                dve.scalar_tensor_tensor(out=x1[:, :, :], in0=y0[:, :, :], scalar=0.0, in1=x_in[b][:, :, :],
                                         op0=ALU.max, op1=ALU.add).then_inc(x1_ok, 1)

            def split1(q):
                dve.wait_ge(lin1, q + 1)
                dve.wait_ge(r1_ok, q)
                dve.wait_ge(agg1, q)
                dve.scalar_tensor_tensor(out=r0[:, :, :], in0=tiles(bank(LIGHT)), scalar=alpha_eff[:, 0:1],
                                         in1=b1B[:, :].unsqueeze(1).broadcast_to([P, T, D]), op0=ALU.mult, op1=ALU.add
                                         ).then_inc(r0_ok, 1)
                dve.tensor_tensor(g1[:, :, :], tiles(bank(LIGHT)), wide(dis[:, 1, :]), ALU.mult).then_inc(g1_ok, 1)

            def take_y1(q):
                dve.wait_ge(agg1, q + 1)
                dve.wait_ge(x2_ok, q)
                dve.tensor_tensor(y1[:, :, :], tiles(bank(LIGHT + 1)), wide(dis[:, 1, :]), ALU.mult).then_inc(y1_ok, 1)

            def add1(q, b):
                dve.wait_ge(y1_ok, q + 1)
                dve.wait_ge(r1_ok, q + 1)
                if past(q - 1):
                    dve.wait_ge(x3_ok, q - 1)
                    dve.wait_ge(h_ok[2], q - 1)
                dve.tensor_tensor(x2[b][:, :, :], y1[:, :, :], r0[:, :, :], ALU.add).then_inc(x2_ok, 1)

            def rest_h2(q):
                dve.wait_ge(hT_ok[2], q + 1)
                dve.wait_ge(gru, 4 * q)
                dve.wait_ge(h2_hi_ok, q + 1)
                dve.tensor_tensor(h2_lo[:, :], hT[2][:, :], h2_hi[:, :].bitcast(F32), ALU.subtract).then_inc(h2_lo_ok, 1)

            def rest_c1(q):
                dve.wait_ge(c1_ok, q + 1)
                dve.wait_ge(conv2, q)
                dve.wait_ge(c1_hi_ok, q + 1)
                dve.tensor_tensor(c1_lo[:, :, HPAD:HPAD + HN], c1[:, :, HPAD:HPAD + HN],
                                  c1_hi[:, :, HPAD:HPAD + HN].bitcast(F32), ALU.subtract).then_inc(c1_lo_ok, 1)

            def sums(q):
                dve.wait_ge(c1_ok, q + 1)
                dve.wait_ge(xs_lo_ok, q)
                dve.tensor_tensor(xs[:, :], c1[:, 1, 0:HN + PAD], c1[:, 0, 1:HN + PAD + 1], ALU.add).then_inc(xs_ok, 1)

            def rest_sums(q):
                dve.wait_ge(xs_hi_ok, q + 1)
                dve.wait_ge(conv2, q)
                dve.tensor_tensor(xs_lo[:, :], xs[:, :], xs_hi[:, :].bitcast(F32), ALU.subtract).then_inc(xs_lo_ok, 1)

            def rest_lr(q):
                for n, (src, dst, ok) in enumerate(((left_f, left, left_f_ok), (right_f, right, right_f_ok))):
                    c = slice(32 * (n + 1), 32 * (n + 2))
                    dve.wait_ge(ok, q + 1)
                    dve.wait_ge(lr_hi_ok, 2 * q + n + 1)
                    dve.tensor_tensor(dst[c, :], src[c, :], dst[c, :].bitcast(F32), ALU.subtract).then_inc(lr_ok, 1)

            def bias_msg(q):
                dve.wait_ge(msg_lin, q + 1)
                dve.wait_ge(nmp, q)
                dve.wait_ge(lr_ok, 2 * q + 1)
                dve.tensor_tensor(msg_b, tiles(bank(HEAVY)), bmB[:, :].unsqueeze(1).broadcast_to([P, T, D]),
                                  ALU.add).then_inc(msg_b_ok, 1)

            def kernel_adj(q, b, j):
                dve.wait_ge(ker_ok, 4 * q + j + 1)
                dve.wait_ge(nmp, q)
                dve.tensor_tensor(kadj[:, j, :], ker[:, j % 2, :], aT[b][:, j, :], ALU.mult).then_inc(kadj_dve, 1)

            def adjacent(q, b):
                if past(q - 1):
                    dve.wait_ge(head_sum, 4 * (q - 1))
                    dve.wait_ge(S_ok, 4 * (q - 1))
                dve.wait_ge(aT_ok, 4 * (q + 1))
                dve.tensor_scalar(adj_on[b][:, :, :], aT[b][:, :, :], 0.0, None, ALU.is_gt).then_inc(adj_on_ok, 1)

            def split_n(q):
                dve.wait_ge(n_hi_ok, q + 1)
                dve.tensor_tensor(n_lo[:, :], bank(HEAVY), n_hi[:, :].bitcast(F32), ALU.subtract
                                  ).then_inc(n_lo_ok, 1)

            def conv_h(q):
                h_eo = by_parity(hT[2][:, :])
                dve.wait_ge(conv2, q + 1)
                dve.wait_ge(c_lo_ok, q)
                dve.scalar_tensor_tensor(out=u[:, 0, :], in0=bank(HEAVY + 1)[:, HN:N], scalar=bn_sh[:, 1:2],
                                         in1=h_eo[:, 0, :], op0=ALU.add, op1=ALU.add)
                dve.scalar_tensor_tensor(out=u[:, 1, :], in0=bank(HEAVY + 1)[:, 0:HN], scalar=bn_sh[:, 1:2],
                                         in1=h_eo[:, 1, :], op0=ALU.add, op1=ALU.add).then_inc(u_part, 1)

            def conv_a(q):
                dve.wait_ge(u_part, 2 * q + 1)
                dve.tensor_tensor(u[:, 1, :], u[:, 1, :], bank(HEAVY + 2)[:, 1:HN + 1], ALU.subtract)
                dve.tensor_tensor(u[:, 0, :], u[:, 0, :], bank(HEAVY + 2)[:, 0:HN], ALU.add).then_inc(u_part, 1)

            def conv_b(q):
                dve.wait_ge(u_part, 2 * q + 2)
                dve.tensor_tensor(u[:, 1, :], u[:, 1, :], bank(HEAVY + 1)[:, HN:N], ALU.subtract).then_inc(u_ok, 1)

            def split_conv(q):
                dve.wait_ge(c_hi_ok, q + 1)
                dve.scalar_tensor_tensor(out=by_parity(c_lo[:, :]), in0=u, scalar=0.0,
                                         in1=by_parity(c_hi[:, :].bitcast(F32)),
                                         op0=ALU.max, op1=ALU.subtract).then_inc(c_lo_ok, 1)

            def gates(q, t):
                dst = bank(GRU_BANK[t])
                dve.wait_ge(rz_ok, 4 * q + t + 1)
                dve.wait_ge(hmn_ok, q)
                dve.wait_ge(xn_ok, q)
                dve.scalar_tensor_tensor(out=q2[:, t, :], in0=rz[:, t, 0:D], scalar=1.0, in1=dst[:, 3 * D:4 * D],
                                         op0=ALU.add, op1=ALU.mult).then_inc(q1_ok, 1)

            def add_gi(q, t):
                dve.wait_ge(q1_ok, 4 * q + t + 1)
                dve.scalar_tensor_tensor(out=q2[:, t, :], in0=q2[:, t, :], scalar=0.5, in1=bank(GRU_BANK[t])[:, 0:D],
                                         op0=ALU.mult, op1=ALU.add).then_inc(q2_ok, 1)

            def mix(q):
                dve.wait_ge(nn_ok, q + 1)
                dve.wait_ge(zd_ok, q)
                dve.tensor_tensor(zd[:, :, :], h[2][:, :, :], nn[:, :, :], ALU.subtract).then_inc(hmn_ok, 1)

            def mix_z(q):
                dve.wait_ge(hmn_ok, q + 1)
                dve.wait_ge(x3_ok, q)
                dve.scalar_tensor_tensor(out=zd[:, :, :], in0=rz[:, :, D:2 * D], scalar=1.0, in1=zd[:, :, :],
                                         op0=ALU.add, op1=ALU.mult).then_inc(zd_ok, 1)

            def add2(q, b):
                dve.wait_ge(zd_ok, q + 1)
                dve.wait_ge(xn_ok, q + 1)
                if past(q - 1):
                    dve.wait_ge(xf_ok, q - 1)
                    dve.wait_ge(h_ok[3], q - 1)
                dve.scalar_tensor_tensor(out=x3[b][:, :, :], in0=zd[:, :, :], scalar=0.5, in1=x2[b][:, :, :],
                                         op0=ALU.mult, op1=ALU.add).then_inc(x3_ok, 1)

            def split_ei(q):
                dve.wait_ge(eh_hi_ok, q + 1)
                dve.tensor_tensor(eh[32:64, :], bank(LAST + 1)[32:64, :], eh[32:64, :].bitcast(F32), ALU.subtract
                                  ).then_inc(eh_ok, 1)

            def local_max(q):
                dve.wait_ge(hx_ok, 2 * (q + 1))
                dve.wait_ge(cB_ok, q)
                dve.tensor_reduce(mxl[:, :], hx[:, :, D:D + HEADS].rearrange("p t h -> p h t"), AX.X, ALU.max
                                  ).then_inc(mxl_ok, 1)

            def exponents(q):
                c = cB[:, :].unsqueeze(1).broadcast_to([P, T, HEADS])
                dve.wait_ge(cB_ok, q + 1)
                dve.wait_ge(ee_ok, q)
                dve.tensor_tensor(z[:, :, :], hx[:, :, D + HEADS:WX], c, ALU.add)
                dve.tensor_tensor(ex[:, 0, :, :], hx[:, :, D:D + HEADS], c, ALU.subtract).then_inc(z_ok, 1)

            def exponents2(q):
                dve.wait_ge(z_ok, q + 1)
                dve.wait_ge(ee_ok, q)
                dve.tensor_scalar(ex[:, 1, :, :], ex[:, 0, :, :], 0.2, None, ALU.mult)
                dve.tensor_scalar(ex[:, 2, :, :], z[:, :, :], 0.8, 0.0, ALU.mult, ALU.min)
                dve.tensor_scalar(ex[:, 3, :, :], z[:, :, :], -0.8, 0.0, ALU.mult, ALU.min).then_inc(ex_ok, 1)

            def weigh_e(q):
                dve.wait_ge(ee_ok, q + 1)
                dve.wait_ge(gr_ok, q)
                dve.wait_ge(gp0_ok, q)
                dve.tensor_tensor(gf[:, :, :, 0, 0:HD], hx[:, :, 0:D].rearrange("p t (h d) -> p t h d", d=HD),
                                  ee[:, 0, :, :].unsqueeze(3).broadcast_to([P, T, HEADS, HD]), ALU.mult)
                for s in range(2):
                    ins = dve.tensor_copy(gf[:, :, :, s, HD], ee[:, s, :, :])
                ins.then_inc(gf_dve, 1)

            def rest(q):
                dve.wait_ge(gp0_ok, q + 1)
                dve.wait_ge(gp2_ok, q)
                flat = "p t h s c -> p (t h s c)"
                dve.tensor_tensor(gf[:, :, :, :, :].rearrange(flat), gf[:, :, :, :, :].rearrange(flat),
                                  gp[0][:, :, :, :, :].rearrange(flat), ALU.subtract).then_inc(gr_ok, 1)

            def masks(q, b, i):
                dve.wait_ge(nei_ok, 4 * q + i + 1)
                dve.wait_ge(adj_on_ok, q + 1)
                if i >= 2:
                    dve.wait_ge(head_sum, 4 * q + i - 1)
                else:
                    dve.wait_ge(head_sum, 4 * q)
                for j in range(T):
                    ins = dve.scalar_tensor_tensor(out=S[i % 2][:, j, :], in0=nei[:, i, :],
                                                   scalar=hx[:, j, D + i:D + i + 1], in1=adj_on[b][:, j, :],
                                                   op0=ALU.is_lt, op1=ALU.mult)
                ins.then_inc(S_ok, 1)

            def combine(q):
                dve.wait_ge(sf_ok, 4 * (q + 1))
                dve.wait_ge(bf_ok, 2 * (q + 1))
                dve.wait_ge(v2_ok, q)
                dve.tensor_tensor(tot[:, :, :, :], tot[:, :, :, :], sf[:, :, :, 1, :],
                                  ALU.subtract).then_inc(v1_ok, 1)

            def weigh_f(q):
                e3 = ee[:, 3, :, :].rearrange("p t h -> p h t").unsqueeze(3).broadcast_to([P, HEADS, T, C])
                dve.wait_ge(v1_ok, q + 1)
                dve.wait_ge(tot_ok, q)
                dve.tensor_tensor(tot[:, :, :, :], tot[:, :, :, :], e3, ALU.mult).then_inc(v2_ok, 1)

            def total(q):
                dve.wait_ge(v2_ok, q + 1)
                dve.wait_ge(ue_ok, q + 1)
                dve.wait_ge(o1_ok, q)
                dve.wait_ge(den_ok, q)
                dve.tensor_tensor(tot[:, :, :, :], tot[:, :, :, :], ue[:, :, :, :], ALU.add).then_inc(tot_ok, 1)

            def isolated(q):
                dve.wait_ge(tot_ok, q + 1)
                dve.wait_ge(fm_ok, q)
                dve.tensor_scalar(flag[:, :, :], tot[:, :, :, HD], 0.0, None, ALU.is_equal).then_inc(flag_ok, 1)

            def denominator(q):
                dve.wait_ge(flag_ok, q + 1)
                dve.wait_ge(rec_ok, q)
                dve.tensor_tensor(den[:, :, :], tot[:, :, :, HD], flag[:, :, :], ALU.add).then_inc(den_ok, 1)

            def invert(q):
                dve.wait_ge(den_ok, q + 1)
                dve.wait_ge(o1_ok, q)
                dve.reciprocal(rec[:, :, :], den[:, :, :]).then_inc(rec_ok, 1)

            def divide(q):
                dve.wait_ge(rec_ok, q + 1)
                dve.wait_ge(o_ok, q)
                dve.tensor_tensor(o1, tot[:, :, :, 0:HD],
                                  rec[:, :, :].unsqueeze(3).broadcast_to([P, HEADS, T, HD]), ALU.mult
                                  ).then_inc(o1_ok, 1)

            def turn(g, half, b):
                if there(g - 1):
                    mix(g - 1)
                    mix_z(g - 1)
                if first(g + 1):
                    scale_weights()
                if there(g - 2):
                    masks(g - 2, b, 2)
                if there(g - 1):
                    add2(g - 1, 1 - b)
                if there(g):
                    rest_h2(g)
                if there(g + 1):
                    bias0(g + 1)
                if there(g - 1):
                    stats(3, g - 1, x3[1 - b])
                    variance(3, g - 1)
                if there(g - 2):
                    masks(g - 2, b, 3)
                if there(g):
                    sums(g)
                    rest_c1(g)
                if there(g - 1):
                    shift(3, g - 1)
                if there(g):
                    rest_lr(g)
                if first(g + 1):
                    small_weights()
                if there(g + 1):
                    self0(g + 1)
                if there(g - 2):
                    combine(g - 2)
                if first(g + 1):
                    weights_lo(0)
                if there(g + 1):
                    add0(g + 1, 1 - b)
                if there(g):
                    bias_msg(g)
                if there(g - 2):
                    weigh_f(g - 2)
                if there(g + 1):
                    stats(1, g + 1, x1)
                if there(g - 2):
                    total(g - 2)
                if there(g):
                    rest_sums(g)
                if there(g - 2):
                    isolated(g - 2)
                if first(g + 1):
                    weights_lo(1)
                if there(g + 1):
                    variance(1, g + 1)
                if there(g):
                    kernel_adj(g, b, 0)
                if there(g - 1):
                    local_max(g - 1)
                if there(g + 1):
                    shift(1, g + 1)
                if there(g + 2):
                    degrees(g + 2)
                if there(g - 1):
                    exponents(g - 1)
                if there(g + 2):
                    stats(0, g + 2, x_in[b], half + 1, b)
                if there(g - 1):
                    exponents2(g - 1)
                if there(g):
                    adjacent(g, b)
                if there(g + 2):
                    variance(0, g + 2)
                if there(g - 1):
                    split_ei(g - 1)
                    weigh_e(g - 1)
                if there(g - 2):
                    denominator(g - 2)
                if there(g + 2):
                    degree_sums(g + 2)
                if there(g):
                    conv_h(g)
                if there(g + 1):
                    split1(g + 1)
                if there(g):
                    conv_a(g)
                if first(g + 1):
                    weights_lo(2)
                    bias_rows()
                if there(g):
                    conv_b(g)
                if there(g - 1):
                    rest(g - 1)
                if there(g + 2):
                    shift(0, g + 2)
                if there(g):
                    split_conv(g)
                if there(g - 2):
                    invert(g - 2)
                if there(g):
                    split_n(g)
                if there(g - 1):
                    masks(g - 1, 1 - b, 0)
                if there(g + 1):
                    take_y1(g + 1)
                    add1(g + 1, 1 - b)
                    stats(2, g + 1, x2[1 - b])
                if there(g):
                    gates(g, 0)
                if there(g + 1):
                    variance(2, g + 1)
                if there(g):
                    add_gi(g, 0)
                if there(g - 1):
                    masks(g - 1, 1 - b, 1)
                if first(g + 2):
                    norm_variances()
                if there(g):
                    gates(g, 1)
                    gates(g, 2)
                    add_gi(g, 1)
                    add_gi(g, 2)
                    gates(g, 3)
                    add_gi(g, 3)
                if there(g + 1):
                    shift(2, g + 1)
                if there(g - 2):
                    divide(g - 2)
                if there(g + 2):
                    mask_dis(g + 2)

            run(dve, turn)


_INS = ['x', 'adj', 'nodemask', 'L0_gnn_W', 'L0_gnn_b', 'L1_gnn_W', 'L1_gnn_b', 'L1_gnn_alpha', 'L2_gnn_w_se',
        'L2_gnn_b_se', 'L2_gnn_conv1_w', 'L2_gnn_bn1_g', 'L2_gnn_bn1_b', 'L2_gnn_bn1_m', 'L2_gnn_bn1_v',
        'L2_gnn_conv2_w', 'L2_gnn_bn2_g', 'L2_gnn_bn2_b', 'L2_gnn_bn2_m', 'L2_gnn_bn2_v', 'L2_gnn_w_msg',
        'L2_gnn_b_msg', 'L2_gnn_w_ih', 'L2_gnn_b_ih', 'L2_gnn_w_hh', 'L2_gnn_b_hh', 'L3_gnn_W', 'L3_gnn_a']


def kernel(**inputs):
    import numpy as _np
    import concourse.bacc as _bacc
    from concourse import mybir as _mybir
    from concourse.bass_utils import run_bass_kernel_spmd as _run

    nc = _bacc.Bacc("TRN2", target_bir_lowering=False, num_devices=1)
    arrays, args = {}, []
    for name in _INS:
        a = _np.ascontiguousarray(inputs[name])
        arrays[f"in_{name}_dram"] = a
        args.append(nc.dram_tensor(f"in_{name}_dram", a.shape, _mybir.dt.from_np(a.dtype), kind="ExternalInput").ap())
    shape = inputs['x'].shape
    args.append(nc.dram_tensor("out_0_dram", shape, _mybir.dt.float32, kind="ExternalOutput").ap())
    build_gnn(nc, *args)
    r = _run(nc, [arrays], core_ids=[0])
    return r.results[0]["out_0_dram"]
```
